# Optimizing a Trainium2 kernel written in Bass

```python
import numpy as np
import jax
import jax.numpy as jnp

def _softmax(x, axis=-1):
    return jax.nn.softmax(x, axis=axis)

def _gelu(x):
    return jax.nn.gelu(x, approximate=True)

def _silu(x):
    return jax.nn.silu(x)

def _sigmoid(x):
    return jax.nn.sigmoid(x)

def _layernorm(x, axis=-1, eps=1e-05):
    m = jnp.mean(x, axis=axis, keepdims=True)
    v = jnp.var(x, axis=axis, keepdims=True)
    return (x - m) / jnp.sqrt(v + eps)

def _scatter_add(tgt, idx, src, axis=0):
    return tgt.at[idx].add(src)

def _segment_sum(src, seg, n):
    return jax.ops.segment_sum(src, seg, n)
kernel_name = 'mk_gnn_resnorm_d2_gnn_r8_9c3471'

def setup_inputs(seed: int=0):
    np.random.seed(seed)
    _w = jnp.asarray

    def _rec_inputs():
        import jax
        import jax.numpy as jnp
        _gk = jax.random.key(seed)
        x = -0.0002117 + 1 * jax.random.normal(jax.random.fold_in(_gk, 1), (6250, 256), jnp.float32)
        src = jax.random.randint(jax.random.fold_in(_gk, 2), (100000,), 0, 6250, jnp.int32)
        dst = jnp.minimum((6250 * jax.random.uniform(jax.random.fold_in(_gk, 3), (100000,)) ** 2.0).astype(jnp.int32), 49999)
        _o = jnp.argsort(dst, stable=True)
        src = src[_o]
        dst = dst[_o]
        edge_attr_64 = 0.000279952 + 1.00013 * jax.random.normal(jax.random.fold_in(_gk, 11), (100000, 64), jnp.float32)
        return (x, src, dst, edge_attr_64)
    x, src, dst, edge_attr_64 = _rec_inputs()

    def _L0_gnn_setup():
        import jax, jax.numpy as jnp
        import numpy as np
        N = 12500
        E = 40000
        CIN = 256
        EDIM = 64
        EEMB = 256
        H = 1024
        LN_EPS = 1e-05

        def _ln(x, g, b):
            m = jnp.mean(x, axis=-1, keepdims=True)
            v = jnp.var(x, axis=-1, keepdims=True)
            return (x - m) * jax.lax.rsqrt(v + LN_EPS) * g + b
        key = jax.random.key(seed)
        ks = jax.random.split(key, 16)

        def w(k, i, o):
            return (jax.random.normal(k, (i, o), jnp.float32) / np.sqrt(i)).astype(jnp.float32)
        return {'x': jax.random.normal(ks[0], (N, CIN), jnp.float32), 'edge_index': jax.random.randint(ks[1], (2, E), 0, N, dtype=jnp.int64), 'edge_attr': jax.random.normal(ks[2], (E, EDIM), jnp.float32), 'eps': jnp.float32(0.0), 'ee_w1': w(ks[3], EDIM, EEMB), 'ee_b1': jnp.zeros((EEMB,), jnp.float32), 'ee_w2': w(ks[4], EEMB, CIN), 'ee_b2': jnp.zeros((CIN,), jnp.float32), 'w1': w(ks[5], CIN, H), 'b1': jnp.zeros((H,), jnp.float32), 'g1': jnp.ones((H,), jnp.float32), 'be1': jnp.zeros((H,), jnp.float32), 'w2': w(ks[6], H, H), 'b2': jnp.zeros((H,), jnp.float32), 'g2': jnp.ones((H,), jnp.float32), 'be2': jnp.zeros((H,), jnp.float32), 'w3': w(ks[7], H, CIN), 'b3': jnp.zeros((CIN,), jnp.float32), 'bn_g': jnp.ones((CIN,), jnp.float32), 'bn_b': jnp.zeros((CIN,), jnp.float32)}
    _L0_gnn_all = _L0_gnn_setup()
    _L0_gnn_in = {k: v for k, v in _L0_gnn_all.items() if k in ('eps', 'ee_w1', 'ee_b1', 'ee_w2', 'ee_b2', 'w1', 'b1', 'g1', 'be1', 'w2', 'b2', 'g2', 'be2', 'w3', 'b3', 'bn_g', 'bn_b')}
    del _L0_gnn_all

    def _L1_gnn_setup():
        import jax, jax.numpy as jnp
        import numpy as np
        N, E, IN_CH, H, C = (6250, 100000, 256, 4, 64)
        key = jax.random.key(seed)
        k1, k2, k3, k4 = jax.random.split(key, 4)
        x = jax.random.normal(k1, (N, IN_CH), dtype=jnp.float32)
        edge_index = jax.random.randint(k2, (2, E), 0, N, dtype=jnp.int64)
        W = jax.random.normal(k3, (H * C, IN_CH), dtype=jnp.float32) * 0.05
        att = jax.random.normal(k4, (H, 2 * C), dtype=jnp.float32) * 0.05
        return {'x': x, 'edge_index': edge_index, 'W': W, 'att': att}
    _L1_gnn_all = _L1_gnn_setup()
    _L1_gnn_in = {k: v for k, v in _L1_gnn_all.items() if k in ('W', 'att')}
    del _L1_gnn_all
    return {'x': x, 'src': src, 'dst': dst, 'edge_attr_64': edge_attr_64, 'L0_gnn_eps': _L0_gnn_in['eps'], 'L0_gnn_ee_w1': _L0_gnn_in['ee_w1'], 'L0_gnn_ee_b1': _L0_gnn_in['ee_b1'], 'L0_gnn_ee_w2': _L0_gnn_in['ee_w2'], 'L0_gnn_ee_b2': _L0_gnn_in['ee_b2'], 'L0_gnn_w1': _L0_gnn_in['w1'], 'L0_gnn_b1': _L0_gnn_in['b1'], 'L0_gnn_g1': _L0_gnn_in['g1'], 'L0_gnn_be1': _L0_gnn_in['be1'], 'L0_gnn_w2': _L0_gnn_in['w2'], 'L0_gnn_b2': _L0_gnn_in['b2'], 'L0_gnn_g2': _L0_gnn_in['g2'], 'L0_gnn_be2': _L0_gnn_in['be2'], 'L0_gnn_w3': _L0_gnn_in['w3'], 'L0_gnn_b3': _L0_gnn_in['b3'], 'L0_gnn_bn_g': _L0_gnn_in['bn_g'], 'L0_gnn_bn_b': _L0_gnn_in['bn_b'], 'L1_gnn_W': _L1_gnn_in['W'], 'L1_gnn_att': _L1_gnn_in['att']}

def reference(x, src, dst, edge_attr_64, L0_gnn_eps, L0_gnn_ee_w1, L0_gnn_ee_b1, L0_gnn_ee_w2, L0_gnn_ee_b2, L0_gnn_w1, L0_gnn_b1, L0_gnn_g1, L0_gnn_be1, L0_gnn_w2, L0_gnn_b2, L0_gnn_g2, L0_gnn_be2, L0_gnn_w3, L0_gnn_b3, L0_gnn_bn_g, L0_gnn_bn_b, L1_gnn_W, L1_gnn_att):
    import jax
    import jax.numpy as jnp

    def _L0_gnn_ref(x, edge_index, edge_attr, eps, ee_w1, ee_b1, ee_w2, ee_b2, w1, b1, g1, be1, w2, b2, g2, be2, w3, b3, bn_g, bn_b):
        import jax, jax.numpy as jnp
        import numpy as np
        N = 12500
        E = 40000
        CIN = 256
        EDIM = 64
        EEMB = 256
        H = 1024
        LN_EPS = 1e-05

        def _ln(x, g, b):
            m = jnp.mean(x, axis=-1, keepdims=True)
            v = jnp.var(x, axis=-1, keepdims=True)
            return (x - m) * jax.lax.rsqrt(v + LN_EPS) * g + b
        n = x.shape[0]
        sl = jnp.arange(n, dtype=edge_index.dtype)
        ei = jnp.concatenate([edge_index, jnp.stack([sl, sl], axis=0)], axis=1)
        ea = jnp.concatenate([edge_attr, jnp.zeros((n, edge_attr.shape[1]), edge_attr.dtype)], axis=0)
        src, dst = (ei[0], ei[1])
        e = jax.nn.relu(ea @ ee_w1 + ee_b1) @ ee_w2 + ee_b2
        msg = x[src] + e
        agg = jax.ops.segment_sum(msg, dst, num_segments=n)
        h = (1.0 + eps) * x + agg
        h = jax.nn.relu(_ln(h @ w1 + b1, g1, be1))
        h = jax.nn.relu(_ln(h @ w2 + b2, g2, be2))
        y = h @ w3 + b3
        out = x + y
        out = _ln(out, bn_g, bn_b)
        return jax.nn.relu(out)

    def _L1_gnn_ref(x, edge_index, W, att):
        import jax, jax.numpy as jnp
        import numpy as np
        N, E, IN_CH, H, C = (6250, 100000, 256, 4, 64)
        n = x.shape[0]
        src, dst = (edge_index[0], edge_index[1])
        Wh = (x @ W.T).reshape(n, H, C)
        e_src = jnp.einsum('ehc,hc->eh', Wh[src], att[:, :C])
        e_dst = jnp.einsum('ehc,hc->eh', Wh[dst], att[:, C:])
        e = jax.nn.leaky_relu(e_src + e_dst, negative_slope=0.2)
        e_max = jax.ops.segment_max(e, dst, num_segments=n)
        e_exp = jnp.exp(e - e_max[dst])
        denom = jax.ops.segment_sum(e_exp, dst, num_segments=n)
        alpha = e_exp / (denom[dst] + 1e-16)
        agg = jax.ops.segment_sum(alpha[:, :, None] * Wh[src], dst, num_segments=n)
        return jax.nn.elu(agg.reshape(n, H * C))
    edge_index = jnp.stack([src, dst])
    x = _layernorm(x + _L0_gnn_ref(x, edge_index, edge_attr_64, L0_gnn_eps, L0_gnn_ee_w1, L0_gnn_ee_b1, L0_gnn_ee_w2, L0_gnn_ee_b2, L0_gnn_w1, L0_gnn_b1, L0_gnn_g1, L0_gnn_be1, L0_gnn_w2, L0_gnn_b2, L0_gnn_g2, L0_gnn_be2, L0_gnn_w3, L0_gnn_b3, L0_gnn_bn_g, L0_gnn_bn_b), axis=-1)
    x = _layernorm(x + _L1_gnn_ref(x, edge_index, L1_gnn_W, L1_gnn_att), axis=-1)
    return x

_drawn_inputs = setup_inputs


def setup_inputs(seed=0):
    import zlib

    import numpy as np

    out = dict(_drawn_inputs(seed))
    spreads = {'L0_gnn_ee_b1': (0.0, 0.267),
     'L0_gnn_ee_b2': (0.0, 0.1),
     'L0_gnn_b1': (0.0, 0.8),
     'L0_gnn_g1': (1.0, 0.2),
     'L0_gnn_be1': (0.0, 0.296),
     'L0_gnn_b2': (0.0, 0.1),
     'L0_gnn_g2': (1.0, 0.2),
     'L0_gnn_be2': (0.0, 0.274),
     'L0_gnn_b3': (0.0, 0.1),
     'L0_gnn_bn_g': (1.0, 0.2),
     'L0_gnn_bn_b': (0.0, 0.1)}
    factors = {}
    for name, (base, spread) in spreads.items():
        noise = np.random.default_rng([zlib.crc32(name.encode()), seed]).standard_normal(out[name].shape)
        drawn = base * np.exp(spread * noise) if base else spread * noise
        out[name] = jnp.asarray(drawn.astype(out[name].dtype))
    for name, factor in factors.items():
        out[name] = (out[name] * factor).astype(out[name].dtype)
    return out
```

```python
from contextlib import ExitStack

import concourse.bass as bass
from concourse import mybir

ALU = mybir.AluOpType
ACT = mybir.ActivationFunctionType
AX = mybir.AxisListType
F32 = mybir.dt.float32
I32 = mybir.dt.int32
BF16 = mybir.dt.bfloat16

P = 128
N_NODES, N_EDGES = 6250, 100000
D, EDIM, EMB, H = 256, 64, 256, 1024
HEADS, C = 4, 64
NODE_TILES = -(-N_NODES // P)
EDGE_TILES = -(-N_EDGES // P)
UNIT = 2
AHEAD = 4
PAD_TILES = 12
ALL_TILES = EDGE_TILES + PAD_TILES
TILE_ROWS = -(-EDGE_TILES // P)
GROW = C + 1
BIG = 1.0e30
FAR = 1000.0
LN_EPS = 1e-5
SLOPE = 0.2
DEN_EPS = 1e-16
MANY = 1 << 20


class Chain:

    def __init__(self, eng, sem):
        self.eng, self.sem, self.base, self.count = eng, sem, None, 0

    def note(self, ins):
        self.count += 1
        ins.then_inc(self.sem, 1)
        return self.count

    def reach(self, count):
        self.eng.wait_ge(self.sem, count if self.base is None else self.base + count)

    def step(self, ins):
        self.reach(self.note(ins))

    def enter(self):
        self.reg = self.eng.alloc_register(f"{self.sem.name}_count")
        self.eng.reg_mov(self.reg, self.count)
        self.before = self.count

    def begin(self):
        self.base, self.count = self.eng.snap(self.reg, min_val=0, max_val=MANY * 64), 0

    def end(self):
        self.eng.reg_add(self.reg, self.reg, self.count)

    def leave(self, trips):
        self.count, self.base = self.before + trips * self.count, None


class Walk:

    def __init__(self, eng, plan, name):
        self.eng, self.plan = eng, plan
        self.tile = eng.alloc_register(f"{name}_tile")
        self.node = eng.alloc_register(f"{name}_node")
        self.left = eng.alloc_register(f"{name}_left")
        eng.reg_mov(self.node, 0)
        eng.reg_load(self.tile, plan[0:1, 0, 0:1])
        eng.reg_load(self.left, plan[0:1, 1, 0:1])

    def place(self):
        return (self.eng.snap(self.tile, min_val=0, max_val=ALL_TILES - UNIT),
                self.eng.snap(self.node, min_val=0, max_val=NODE_TILES))

    def advance(self):
        eng = self.eng
        eng.reg_add(self.tile, self.tile, UNIT)
        eng.reg_add(self.left, self.left, -1)
        with eng.If_eq(self.left, 0):
            eng.reg_add(self.node, self.node, 1)
            node = eng.snap(self.node, min_val=0, max_val=NODE_TILES)
            eng.reg_load(self.tile, self.plan[0:1, 0, bass.ds(node, 1)])
            eng.reg_load(self.left, self.plan[0:1, 1, bass.ds(node, 1)])


class Rounds:

    def __init__(self, eng, plan, name):
        self.eng, self.name = eng, name
        self.reg = eng.alloc_register(f"{name}_round")
        eng.reg_mov(self.reg, 1)
        self.trips = eng.value_load(plan[0:1, 2, 0:1], min_val=1, max_val=MANY)
        self.now = [1, 2, 3]

    def begin(self):
        n = self.eng.snap(self.reg, min_val=1, max_val=MANY)
        self.now = [n, self.eng.snap(n + 1), self.eng.snap(n + 2)]

    def end(self):
        self.eng.reg_add(self.reg, self.reg, 1)

    def seen(self, sems, at):
        self.eng.wait_ge(sems[at % AHEAD], self.now[1 + at // AHEAD])

    def landed(self, sems, at, k=None):
        sem = sems[at % AHEAD] if k is None else sems[UNIT * (at % AHEAD) + k]
        self.eng.wait_ge(sem, self.now[at // AHEAD] * 16)


def bass_gnn_resnorm(nc, x, srcT, dstT, dst_rows, eaT, eps, ee_w1, ee_b1, ee_w2, ee_b2, w1, b1, g1T,
                     be1T, w2, b2, g2T, be2T, w3, b3, bn_g, bn_b, gat_wT, att_src, att_dst, out):
    with ExitStack() as ctx:
        def sb(name, shape, dt=F32):
            return ctx.enter_context(nc.sbuf_tensor(name, shape, dt))

        in_phase = []

        def phase_sem(name):
            in_phase.append(nc.alloc_semaphore(name))
            return in_phase[-1]

        def end_phase():
            nc.clear_and_free_semaphores(in_phase)
            nc.all_engine_barrier()
            in_phase.clear()

        table = nc.dram_tensor("wh_table", (NODE_TILES * P, HEADS * GROW), F32, kind="Internal").ap()
        x1_dram = nc.dram_tensor("x1_rows", (NODE_TILES * P, D), F32, kind="Internal").ap()

        plan = sb("plan", [1, 3, NODE_TILES + 1], I32)
        src_cols = sb("src_cols", [P, ALL_TILES], I32)
        dst_cols = sb("dst_cols", [P, ALL_TILES])
        node_base = sb("node_base", [P, NODE_TILES + 1, UNIT])
        iota_row = sb("iota_row", [P, P])
        ident = sb("ident", [P, P])
        ident_bf = sb("ident_bf", [P, P], BF16)
        ee_w1b = sb("ee_w1b", [EDIM + 1, EMB])
        ee_w2s = sb("ee_w2s", [P, 2, D])
        w1s = sb("w1s", [P, D // P, H])
        w2s = sb("w2s", [P, H // P, H])
        w3s = sb("w3s", [P, H // P, D])
        gat_w = sb("gat_w", [P, D // P, D])
        g1s, be1s = sb("g1s", [P, H // P]), sb("be1s", [P, H // P])
        g2s, be2s = sb("g2s", [P, H // P]), sb("be2s", [P, H // P])
        b1_all, b2_all = sb("b1_all", [P, H]), sb("b2_all", [P, H])
        self_row = sb("self_row", [P, EMB + 1])
        ee_b2_all = sb("ee_b2_all", [P, D])
        b3_all = sb("b3_all", [P, D])
        bn_g_all, bn_b_all = sb("bn_g_all", [P, D]), sb("bn_b_all", [P, D])
        att_s, att_d = sb("att_s", [P, D]), sb("att_d", [P, D])
        eps2 = sb("eps2", [P, 1])
        powers = sb("powers", [P, 3])
        score_dst = sb("score_dst", [P, NODE_TILES + 1, HEADS])
        z_max = sb("z_max", [P, NODE_TILES + 1, HEADS])
        SUM0 = D + EMB + 1
        sums = sb("sums", [P, (NODE_TILES + 1) * SUM0])
        sum0 = sums[:, :].rearrange("p (b f) -> p b f", f=SUM0)
        SUM1 = HEADS * GROW
        sum1 = sums[:, 0:(NODE_TILES + 1) * SUM1].rearrange("p (b f) -> p b f", f=SUM1)
        SPARE = (NODE_TILES + 1) * SUM1
        arena = sb("arena", [P, 7000])

        def take(tensor, at, shape):
            n = 1
            for s in shape:
                n *= s
            v = tensor[:, at[0]:at[0] + n]
            at[0] += n
            if len(shape) == 2:
                return v.rearrange("p (a b) -> p a b", b=shape[1])
            if len(shape) == 3:
                return v.rearrange("p (a b c) -> p a b c", b=shape[1], c=shape[2])
            return v

        with ExitStack() as own:
            at = [0]
            dst_f = take(arena, at, [TILE_ROWS, P])
            dst_neg = take(arena, at, [TILE_ROWS, P])
            hi, lo = take(arena, at, [TILE_ROWS]), take(arena, at, [TILE_ROWS])
            tile_no, tile_back = take(arena, at, [TILE_ROWS]), take(arena, at, [TILE_ROWS])
            base_lo, base_hi = take(arena, at, [NODE_TILES]), take(arena, at, [NODE_TILES])
            above, meets = take(arena, at, [NODE_TILES]), take(arena, at, [NODE_TILES])
            ranges, ranges_all = take(arena, at, [2, NODE_TILES]), take(arena, at, [2, NODE_TILES])
            firsts, counts = take(arena, at, [NODE_TILES]), take(arena, at, [NODE_TILES])
            total = take(arena, at, [1])
            counts_i = own.enter_context(nc.sbuf_tensor("counts_i", [1, NODE_TILES + 1], I32))
            rows_i = sums[:, ALL_TILES:ALL_TILES + TILE_ROWS * P].bitcast(I32).rearrange("p (c e) -> p c e", e=P)
            cols_i = sums[:, 0:ALL_TILES].bitcast(I32)
            plan_in, loaded = phase_sem("plan_in"), phase_sem("loaded")
            made = phase_sem("made")
            ranged = phase_sem("ranged")
            reduced = phase_sem("reduced")
            own_steps, pool_steps = phase_sem("plan_steps"), phase_sem("const_steps")
            block = own.enter_context(nc.Block())

            def every_partition(row, n):
                return row.rearrange("(o n) -> o n", o=1).to_broadcast([P, n])

            @block.sync
            def _(sp):
                sp.dma_start(rows_i[:, :, :], dst_rows).then_inc(plan_in, 16)
                sp.dma_start(cols_i, dstT).then_inc(plan_in, 16)
                sp.dma_start(src_cols[:, :], srcT).then_inc(loaded, 16)
                sp.dma_start(ee_w1b[0:EDIM, :], ee_w1).then_inc(loaded, 16)
                sp.dma_start(ee_w1b[EDIM:EDIM + 1, :], ee_b1.rearrange("(o n) -> o n", o=1)).then_inc(loaded, 16)
                n = 3
                for to, of in [(ee_w2s, ee_w2), (w1s, w1), (w2s, w2), (w3s, w3), (gat_w, gat_wT)]:
                    sp.dma_start(to[:, :, :], of.rearrange("(k p) n -> p k n", p=P)).then_inc(loaded, 16)
                    n += 1
                for to, of in [(g1s, g1T), (be1s, be1T), (g2s, g2T), (be2s, be2T)]:
                    sp.dma_start(to[:, :], of).then_inc(loaded, 16)
                    n += 1
                for to, of in [(b1_all, b1), (b2_all, b2), (ee_b2_all, ee_b2), (b3_all, b3),
                               (bn_g_all, bn_g), (bn_b_all, bn_b), (att_s, att_src), (att_d, att_dst)]:
                    sp.dma_start(to[:, :], every_partition(of, to.shape[1])).then_inc(loaded, 16)
                    n += 1
                sp.dma_start(self_row[:, 0:EMB], every_partition(ee_b1, EMB)).then_inc(loaded, 16)
                sp.dma_start(eps2[:, :], every_partition(eps, 1)).then_inc(loaded, 16)
                sp.wait_ge(loaded, 16 * (n + 2))

            @block.gpsimd
            def _(pool):
                g = nc.gpsimd
                g.iota(tile_no, [[P, TILE_ROWS]], base=0, channel_multiplier=1,
                       allow_small_or_imprecise_dtypes=True).then_inc(made, 1)
                g.iota(base_lo, [[P, NODE_TILES]], base=0, channel_multiplier=0,
                       allow_small_or_imprecise_dtypes=True).then_inc(made, 1)
                g.iota(base_hi, [[P, NODE_TILES]], base=P - 1, channel_multiplier=0,
                       allow_small_or_imprecise_dtypes=True).then_inc(made, 1)
                g.iota(iota_row[:, :], [[1, P]], base=0, channel_multiplier=0,
                       allow_small_or_imprecise_dtypes=True)
                g.iota(node_base[:, :, :], [[P, NODE_TILES + 1], [0, UNIT]], base=0, channel_multiplier=0,
                       allow_small_or_imprecise_dtypes=True)
                for n, c in enumerate((LN_EPS, -0.5, -1.0)):
                    g.memset(powers[:, n:n + 1], c)
                g.memset(ident[:, :], 0.0).then_inc(pool_steps, 1)
                pool.wait_ge(pool_steps, 1)
                g.affine_select(out=ident[:, :], in_=ident[:, :], compare_op=ALU.not_equal, fill=1.0, base=0,
                                pattern=[[-1, P]], channel_multiplier=1)
                pool.wait_ge(ranged, 1)
                g.partition_all_reduce(ranges_all, ranges, P, bass.bass_isa.ReduceOp.max).then_inc(reduced, 1)

            @block.vector
            def _(dve):
                v, chain = nc.vector, Chain(dve, own_steps)
                dve.wait_ge(plan_in, 32)
                v.tensor_copy(dst_cols[:, :], cols_i)
                v.memset(score_dst[:, :, :], 0.0)
                v.memset(z_max[:, :, :], -BIG)
                chain.step(v.tensor_copy(dst_f, rows_i[:, :, :]))
                v.tensor_reduce(hi, dst_f, AX.X, ALU.max)
                chain.step(v.tensor_scalar(dst_neg, dst_f, 0.0, 1.0e6, ALU.is_lt, ALU.mult))
                chain.step(v.tensor_tensor(dst_neg, dst_neg, dst_f, ALU.add))
                chain.step(v.tensor_reduce(lo, dst_neg, AX.X, ALU.min))
                dve.wait_ge(made, 3)
                v.memset(ranges, 0.0)
                v.tensor_scalar(tile_back, tile_no, -1.0, FAR, ALU.mult, ALU.add)
                chain.step(v.tensor_scalar(tile_no, tile_no, 1.0, None, ALU.add))
                for c in range(TILE_ROWS):
                    chain.step(v.tensor_scalar(above, base_hi, lo[:, c:c + 1], None, ALU.is_ge))
                    chain.step(v.scalar_tensor_tensor(meets, base_lo, hi[:, c:c + 1], above, ALU.is_le, ALU.mult))
                    v.scalar_tensor_tensor(ranges[:, 0, :], meets, tile_back[:, c:c + 1], ranges[:, 0, :],
                                           ALU.mult, ALU.max)
                    chain.step(v.scalar_tensor_tensor(ranges[:, 1, :], meets, tile_no[:, c:c + 1],
                                                      ranges[:, 1, :], ALU.mult, ALU.max))
                v.tensor_copy(total[0:1, :], total_zero(v, chain, total)).then_inc(ranged, 1)
                dve.wait_ge(reduced, 1)
                r = ranges_all[0:1, :, :]
                chain.step(v.tensor_scalar(firsts[0:1, :], r[:, 0, :], -1.0, FAR, ALU.mult, ALU.add))
                v.tensor_scalar(plan[0:1, 0, 0:NODE_TILES], firsts[0:1, :], float(EDGE_TILES), None, ALU.min)
                chain.step(v.scalar_tensor_tensor(counts[0:1, :], r[:, 0, :], -FAR, r[:, 1, :], ALU.add, ALU.add))
                v.memset(counts_i[0:1, NODE_TILES:NODE_TILES + 1], 0)
                chain.step(v.tensor_scalar(counts_i[0:1, 0:NODE_TILES], counts[0:1, :], 1.0, float(UNIT - 1),
                                           ALU.max, ALU.add))
                chain.step(v.tensor_scalar(plan[0:1, 1, 0:NODE_TILES], counts_i[0:1, 0:NODE_TILES], 1, None,
                                           ALU.logical_shift_right))
                v.memset(plan[0:1, 0, NODE_TILES:], EDGE_TILES)
                v.memset(plan[0:1, 1, NODE_TILES:], MANY)
                chain.step(v.tensor_reduce(total[0:1, :], plan[0:1, 1, 0:NODE_TILES], AX.X, ALU.add))
                chain.step(v.tensor_scalar(counts_i[0:1, 0:1], total[0:1, :], float(AHEAD - 1), None, ALU.add))
                chain.step(v.tensor_scalar(plan[0:1, 2, 0:1], counts_i[0:1, 0:1], 2, None, ALU.logical_shift_right))
                v.memset(sum0, 0.0)

        with ExitStack() as own:
            block = own.enter_context(nc.Block())

            @block.vector
            def _(dve):
                v = nc.vector
                v.tensor_scalar(self_row[:, 0:EMB], self_row[:, 0:EMB], 0.0, None, ALU.max)
                v.memset(self_row[:, EMB:], 1.0)
                v.tensor_scalar(eps2[:, :], eps2[:, :], 2.0, None, ALU.add)
                v.tensor_copy(ident_bf[:, :], ident[:, :])

        with ExitStack() as own:
            at = [0]
            xg = take(arena, at, [AHEAD * UNIT, D])
            hid = take(arena, at, [2, UNIT, (EMB + 2)])
            ea = take(arena, at, [AHEAD, UNIT * P])
            hits = take(arena, at, [AHEAD, UNIT, P])
            rel = take(arena, at, [AHEAD, UNIT])
            idx = [own.enter_context(nc.sbuf_tensor(f"idx{u}", [P, UNIT], I32)) for u in range(AHEAD)]
            ps_hid = [own.enter_context(nc.psum_tensor(f"ps_hid{i}", [P, UNIT, EMB], F32)) for i in range(2)]
            ps_sum = [own.enter_context(nc.psum_tensor(f"ps_sum{i}", [P, 2, 512], F32)) for i in range(2)]

            def many(name, n=AHEAD):
                return [phase_sem(f"{name}{i}") for i in range(n)]

            ea_in, xg_in = many("ea_in"), many("xg_in", AHEAD * UNIT)
            rel_set, hits_set = many("rel_set"), many("hits_set")
            hid_mm, hid_set, sum_mm, sum_out = many("hid_mm"), many("hid_set"), many("sum_mm"), many("sum_out")
            ones_set = phase_sem("ones_set")
            idx_set = many("idx_set")
            block = own.enter_context(nc.Block())

            @block.sync
            def _(sp):
                rounds, walk = Rounds(sp, plan, "ea"), Walk(sp, plan, "ea")

                def load(p):
                    tile, _ = walk.place()
                    rounds.seen(hid_mm, p - AHEAD)
                    sp.dma_start(ea[0:EDIM, p % AHEAD, :], eaT[:, bass.ds(tile * P, UNIT * P)]).then_inc(
                        ea_in[p % AHEAD], 16)
                    walk.advance()

                load(0)
                with sp.Fori(0, rounds.trips):
                    rounds.begin()
                    for u in range(AHEAD):
                        load(u + 1)
                    rounds.end()

            @block.gpsimd
            def _(pool):
                g = nc.gpsimd
                for s in rel_set + idx_set:
                    pool.sem_inc(s, 1)
                rounds, walk = Rounds(pool, plan, "xg"), Walk(pool, plan, "xg")

                def prepare(p):
                    u = p % AHEAD
                    rounds.seen(sum_mm, p - AHEAD)
                    tile, node = walk.place()
                    g.tensor_copy(idx[u][:, :], src_cols[:, bass.ds(tile, UNIT)]).then_inc(idx_set[u], 1)
                    g.tensor_tensor(rel[:, u, :], dst_cols[:, bass.ds(tile, UNIT)],
                                    node_base[:, bass.ds(node, 1), :].rearrange("p a b -> p (a b)"),
                                    ALU.subtract).then_inc(rel_set[u], 1)
                    rounds.seen(idx_set, p)
                    walk.advance()
                    for k in range(UNIT):
                        g.indirect_dma_start(xg[:, UNIT * u + k, :], None, x,
                                             bass.IndirectOffsetOnAxis(ap=idx[u][:, k:k + 1], axis=0)
                                             ).then_inc(xg_in[UNIT * u + k], 16)

                prepare(0)
                with pool.Fori(0, rounds.trips):
                    rounds.begin()
                    for u in range(AHEAD):
                        prepare(u + 1)
                    rounds.end()
                for k in range(UNIT):
                    pool.wait_ge(xg_in[k], pool.snap(rounds.trips * 16) + 16)

            @block.scalar
            def _(act):
                for s in hid_set:
                    act.sem_inc(s, 1)
                rounds = Rounds(act, plan, "hid")

                def relu(p):
                    rounds.seen(hid_mm, p)
                    rounds.seen(sum_mm, p - 2)
                    nc.scalar.activation(hid[:, p % 2, :, 0:EMB], ps_hid[p % 2][:, :, :],
                                         ACT.Relu).then_inc(hid_set[p % AHEAD], 1)

                relu(0)
                with act.Fori(0, rounds.trips):
                    rounds.begin()
                    for u in range(AHEAD):
                        relu(u + 1)
                    rounds.end()

            @block.tensor
            def _(pe):
                for s in hid_mm + sum_mm:
                    pe.sem_inc(s, 1)
                rounds = Rounds(pe, plan, "mm")

                def hidden(p):
                    rounds.landed(ea_in, p)
                    rounds.seen(hid_set, p - 2)
                    for k in range(UNIT):
                        mm = nc.tensor.matmul(ps_hid[p % 2][:, k, :], ea[0:EDIM + 1, p % AHEAD, k * P:(k + 1) * P],
                                              ee_w1b[:, :], start=True, stop=True)
                    mm.then_inc(hid_mm[p % AHEAD], 1)

                pe.wait_ge(ones_set, 1)
                hidden(0)
                with pe.Fori(0, rounds.trips):
                    rounds.begin()
                    for u in range(AHEAD):
                        hidden(u + 1)
                        rounds.seen(hits_set, u)
                        rounds.seen(hid_set, u)
                        rounds.seen(sum_out, u - 2)
                        for k in range(UNIT):
                            rounds.landed(xg_in, u, k)
                            nc.tensor.matmul(ps_sum[u % 2][:, 0, 0:D], hits[:, u, k, :], xg[:, UNIT * u + k, :],
                                             start=(k == 0), stop=(k == UNIT - 1))
                            mm = nc.tensor.matmul(ps_sum[u % 2][:, 1, 0:EMB + 2], hits[:, u, k, :],
                                                  hid[:, u % 2, k, :], start=(k == 0), stop=(k == UNIT - 1))
                        mm.then_inc(sum_mm[u], 1)
                    rounds.end()

            @block.vector
            def _(dve):
                v = nc.vector
                for s in hits_set + sum_out:
                    dve.sem_inc(s, 1)
                v.memset(hid[:, :, :, EMB:EMB + 1], 1.0)
                v.memset(hid[:, :, :, EMB + 1:EMB + 2], 0.0)
                v.memset(ea[EDIM:EDIM + 1, :, :], 1.0).then_inc(ones_set, 1)
                rounds, walk = Rounds(dve, plan, "sum"), Walk(dve, plan, "sum")

                def compare(p):
                    rounds.seen(rel_set, p)
                    rounds.seen(sum_mm, p - AHEAD)
                    for k in range(UNIT):
                        ins = v.tensor_scalar(hits[:, p % AHEAD, k, :], iota_row[:, :], rel[:, p % AHEAD, k:k + 1],
                                              None, ALU.is_equal)
                    ins.then_inc(hits_set[p % AHEAD], 1)

                compare(0)
                with dve.Fori(0, rounds.trips):
                    rounds.begin()
                    for u in range(AHEAD):
                        compare(u + 1)
                        _, node = walk.place()
                        rounds.seen(sum_mm, u)
                        rounds.seen(sum_out, u - 1)
                        to = sum0[:, bass.ds(node, 1), :].rearrange("p a f -> p (a f)")
                        v.tensor_tensor(to[:, 0:D + EMB].rearrange("p (a f) -> p a f", a=2),
                                        to[:, 0:D + EMB].rearrange("p (a f) -> p a f", a=2),
                                        ps_sum[u % 2][:, :, 0:EMB], ALU.add)
                        v.tensor_tensor(to[:, D + EMB:], to[:, D + EMB:], ps_sum[u % 2][:, 1, EMB:EMB + 1],
                                        ALU.add).then_inc(sum_out[u], 1)
                        walk.advance()
                    rounds.end()

        end_phase()
        node_mlp(nc, locals())
        end_phase()
        attention(nc, locals())


def total_zero(v, chain, total):
    chain.step(v.memset(total[0:1, :], 0.0))
    return total[0:1, :]


def norm_factors(g, chain, mv, powers):
    chain.step(g.tensor_tensor(mv[:, 2:3], mv[:, 1:2], powers[:, 0:1], ALU.add))
    g.tensor_tensor(mv[:, 3:4], mv[:, 0:1], powers[:, 2:3], ALU.mult)
    chain.step(g.tensor_tensor(mv[:, 2:3], mv[:, 2:3], powers[:, 1:2], ALU.pow))
    return g.tensor_tensor(mv[:, 3:4], mv[:, 3:4], mv[:, 2:3], ALU.mult)


def node_mlp(nc, env):
    e, phase_sem = env, env["phase_sem"]
    arena, take, sum0 = e["arena"], e["take"], e["sum0"]
    KH, KD = H // P, D // P
    STEPS = 4
    with ExitStack() as own:
        def sem(name):
            return phase_sem(name)

        def ps(name, shape):
            return own.enter_context(nc.psum_tensor(name, shape, F32))

        at = [0]
        edge_sum = take(arena, at, [EMB + 1])
        edge_sumT = take(arena, at, [KD, P])
        xa, xc = take(arena, at, [D]), take(arena, at, [D])
        h0, hT = take(arena, at, [D]), take(arena, at, [KD, P])
        a1, a2 = take(arena, at, [H]), take(arena, at, [H])
        a1T, a2T = take(arena, at, [KH, P]), take(arena, at, [KH, P])
        y, x1, x1T = take(arena, at, [D]), take(arena, at, [D]), take(arena, at, [KD, P])
        wh = take(arena, at, [HEADS, GROW])
        prod = take(arena, at, [D])
        st1, st2 = take(arena, at, [2, 6]), take(arena, at, [2, 6])
        mv1, mv2, mvx = take(arena, at, [4]), take(arena, at, [4]), take(arena, at, [4])
        ps_e = ps("ps_e", [P, 2, D])
        ps_y = ps("ps_y", [P, D])
        ps_x = ps("ps_x", [P, 2, D])
        ps_w = ps("ps_w", [P, 2, 512])
        ps_n = ps("ps_n", [P, KH, P])

        (xa_in, xc_in, edge_set, edge_t, edge_c, e_mm, h_set, h_t, h_c, a1_mm, a1_out, a1_set, a1_n,
         a1_t, a1_c, a2_mm, a2_out, a2_set, a2_n, a2_t, a2_c, y_mm, x1_set, x1_t, x1_c, wh_mm, wh_set,
         x1_stored, wh_stored, xc_used, h0_used, steps, a1_var, a2_var, y_var, y_set, x1_var, x1_fac,
         pool_steps) = [sem(f"s_{n}") for n in (
            "xa_in xc_in edge_set edge_t edge_c e_mm h_set h_t h_c a1_mm a1_out a1_set a1_n a1_t a1_c "
            "a2_mm a2_out a2_set a2_n a2_t a2_c y_mm x1_set x1_t x1_c wh_mm wh_set x1_stored "
            "wh_stored xc_used h0_used dve_steps a1_var a2_var y_var y_set x1_var x1_fac pool_steps").split()]

        def pipeline(eng, body, chain=None, last=NODE_TILES):
            for i in range(STEPS - 1):
                body(i)
            if chain:
                chain.enter()
            with eng.Fori(STEPS - 1, last) as i:
                i = eng.snap(i, min_val=STEPS - 1, max_val=last - 1)
                if chain:
                    chain.begin()
                body(i)
                if chain:
                    chain.end()
            if chain:
                chain.leave(last - STEPS + 1)
            for i in range(last, NODE_TILES + STEPS - 1):
                body(i)

        def runs(i, lag):
            return not isinstance(i, int) or 0 <= i - lag < NODE_TILES

        def past(i, n=0):
            return not isinstance(i, int) or i - n > 0

        def rows(dram, i):
            return dram[bass.ds(i * P, P), :]

        block = own.enter_context(nc.Block())

        @block.sync
        def _(sp):
            def body(i):
                if runs(i, 0):
                    if past(i):
                        sp.wait_ge(h0_used, i)
                    sp.dma_start(xa, rows(e["x"], i)).then_inc(xa_in, 16)
                if runs(i, 2):
                    if past(i, 2):
                        sp.wait_ge(xc_used, i - 2)
                    sp.dma_start(xc, rows(e["x"], i - 2)).then_inc(xc_in, 16)
                    sp.wait_ge(x1_set, i - 1)
                    sp.dma_start(rows(e["x1_dram"], i - 2), x1).then_inc(x1_stored, 16)
                if runs(i, 3):
                    sp.wait_ge(wh_set, i - 2)
                    sp.dma_start(rows(e["table"], i - 3), wh.rearrange("p h c -> p (h c)")).then_inc(wh_stored, 16)

            pipeline(sp, body)
            sp.wait_ge(x1_stored, 16 * NODE_TILES)
            sp.wait_ge(wh_stored, 16 * NODE_TILES)

        @block.gpsimd
        def _(pool):
            g, chain = nc.gpsimd, Chain(pool, pool_steps)

            def edges(i):
                if past(i):
                    pool.wait_ge(edge_t, i)
                    pool.wait_ge(h0_used, i)
                g.tensor_tensor(edge_sum, sum0[:, bass.ds(i, 1), D:].rearrange("p a f -> p (a f)"),
                                e["self_row"][:, :], ALU.add).then_inc(edge_set, 1)

            def factors(i, aggregated, mv, done):
                pool.wait_ge(aggregated, i)
                norm_factors(g, chain, mv, e["powers"]).then_inc(done, 1)

            def body(i):
                if runs(i, 1):
                    factors(i, a2_var, mv2, a2_set)
                if runs(i, 0):
                    factors(i + 1, a1_var, mv1, a1_set)
                if runs(i, 2):
                    factors(i - 1, y_var, mvx, y_set)
                    factors(i - 1, x1_var, mvx, x1_fac)
                if runs(i, -1):
                    edges(i + 1)

            edges(0)
            pipeline(pool, body, chain, last=NODE_TILES - 1)

        @block.tensor
        def _(pe):
            t = nc.tensor
            ident = e["ident"]

            def body(i):
                if runs(i, 1):
                    pe.wait_ge(a1_n, i)
                    if past(i, 2):
                        pe.wait_ge(a2_c, i - 2)
                    for k in range(KH):
                        mm = t.transpose(ps_n[:, k, :], a1[:, k * P:(k + 1) * P], ident[:, :])
                    mm.then_inc(a1_t, 1)
                if runs(i, 0):
                    pe.wait_ge(edge_set, i + 1)
                    if past(i):
                        pe.wait_ge(h_c, i)
                    for k in range(KD):
                        mm = t.transpose(ps_e[:, 0, k * P:(k + 1) * P], edge_sum[:, k * P:(k + 1) * P], ident[:, :])
                    mm.then_inc(edge_t, 1)
                    pe.wait_ge(edge_c, i + 1)
                    for k in range(KD):
                        mm = t.matmul(ps_e[:, 1, :], edge_sumT[:, k, :], e["ee_w2s"][:, k, :],
                                      start=(k == 0), stop=(k == KD - 1))
                    mm.then_inc(e_mm, 1)
                if runs(i, 1):
                    pe.wait_ge(a1_c, i)
                    if past(i, 1):
                        pe.wait_ge(a1_out, i)
                    for n in range(2):
                        for k in range(KH):
                            mm = t.matmul(ps_w[:, n, :], a1T[:, k, :], e["w2s"][:, k, n * 512:(n + 1) * 512],
                                          start=(k == 0), stop=(k == KH - 1))
                    mm.then_inc(a2_mm, 1)
                if runs(i, 2):
                    pe.wait_ge(a2_n, i - 1)
                    pe.wait_ge(a1_c, min(i, NODE_TILES) if isinstance(i, int) else i)
                    for k in range(KH):
                        mm = t.transpose(ps_n[:, k, :], a2[:, k * P:(k + 1) * P], ident[:, :])
                    mm.then_inc(a2_t, 1)
                if runs(i, 0):
                    pe.wait_ge(h_set, i + 1)
                    for k in range(KD):
                        mm = t.transpose(ps_e[:, 0, k * P:(k + 1) * P], h0[:, k * P:(k + 1) * P], ident[:, :])
                    mm.then_inc(h_t, 1)
                if runs(i, 3):
                    pe.wait_ge(x1_set, i - 2)
                    if past(i, 3):
                        pe.wait_ge(wh_set, i - 3)
                    for k in range(KD):
                        mm = t.transpose(ps_x[:, 0, k * P:(k + 1) * P], x1[:, k * P:(k + 1) * P], ident[:, :])
                    mm.then_inc(x1_t, 1)
                if runs(i, 0):
                    pe.wait_ge(h_c, i + 1)
                    if past(i):
                        pe.wait_ge(a2_out, i)
                    for n in range(2):
                        for k in range(KD):
                            mm = t.matmul(ps_w[:, n, :], hT[:, k, :], e["w1s"][:, k, n * 512:(n + 1) * 512],
                                          start=(k == 0), stop=(k == KD - 1))
                    mm.then_inc(a1_mm, 1)
                if runs(i, 2):
                    pe.wait_ge(a2_c, i - 1)
                    if past(i, 2):
                        pe.wait_ge(x1_set, i - 2)
                    for k in range(KH):
                        mm = t.matmul(ps_y[:, :], a2T[:, k, :], e["w3s"][:, k, :],
                                      start=(k == 0), stop=(k == KH - 1))
                    mm.then_inc(y_mm, 1)
                if runs(i, 3):
                    pe.wait_ge(x1_c, i - 2)
                    for k in range(KD):
                        mm = t.matmul(ps_x[:, 1, :], x1T[:, k, :], e["gat_w"][:, k, :],
                                      start=(k == 0), stop=(k == KD - 1))
                    mm.then_inc(wh_mm, 1)

            pipeline(pe, body)

        @block.scalar
        def _(act):
            a = nc.scalar

            def body(i):
                if runs(i, 1):
                    act.wait_ge(a1_t, i)
                    if past(i, 1):
                        act.wait_ge(a2_mm, i - 1)
                    for k in range(KH):
                        ins = a.activation(a1T[:, k, :], ps_n[:, k, :], ACT.Relu, bias=e["be1s"][:, k:k + 1],
                                           scale=e["g1s"][:, k:k + 1])
                    ins.then_inc(a1_c, 1)
                if runs(i, 0):
                    act.wait_ge(edge_t, i + 1)
                    if past(i):
                        act.wait_ge(e_mm, i)
                    a.activation(edge_sumT.rearrange("p k n -> p (k n)"), ps_e[:, 0, :], ACT.Copy).then_inc(edge_c, 1)
                if runs(i, 2):
                    act.wait_ge(a2_t, i - 1)
                    if past(i, 2):
                        act.wait_ge(y_mm, i - 2)
                    for k in range(KH):
                        ins = a.activation(a2T[:, k, :], ps_n[:, k, :], ACT.Relu, bias=e["be2s"][:, k:k + 1],
                                           scale=e["g2s"][:, k:k + 1])
                    ins.then_inc(a2_c, 1)
                if runs(i, 0):
                    act.wait_ge(h_t, i + 1)
                    if past(i):
                        act.wait_ge(a1_mm, i)
                    a.activation(hT.rearrange("p k n -> p (k n)"), ps_e[:, 0, :], ACT.Copy).then_inc(h_c, 1)
                if runs(i, 3):
                    act.wait_ge(x1_t, i - 2)
                    if past(i, 3):
                        act.wait_ge(wh_mm, i - 3)
                    a.activation(x1T.rearrange("p k n -> p (k n)"), ps_x[:, 0, :], ACT.Copy).then_inc(x1_c, 1)
                if runs(i, 1):
                    act.wait_ge(a2_set, i)
                    a.activation(a2, a2, ACT.Identity, bias=mv2[:, 3:4], scale=mv2[:, 2:3]).then_inc(a2_n, 1)
                if runs(i, 0):
                    act.wait_ge(a1_set, i + 1)
                    a.activation(a1, a1, ACT.Identity, bias=mv1[:, 3:4], scale=mv1[:, 2:3]).then_inc(a1_n, 1)

            pipeline(act, body)

        @block.vector
        def _(dve):
            v, chain = nc.vector, Chain(dve, steps)

            def wide(i, mm, bias, a, st, mv, turned, read, aggregated):
                dve.wait_ge(mm, i)
                if past(i, 1):
                    dve.wait_ge(turned, i - 1)
                ins = v.tensor_tensor(a.rearrange("p (n f) -> p n f", n=2), ps_w[:, :, :],
                                      bias.rearrange("p (n f) -> p n f", n=2), ALU.add)
                ins.then_inc(read, 1)
                dve.wait_ge(read, i)
                for n in range(2):
                    ins = v.bn_stats(st[:, n, :], a[:, n * 512:(n + 1) * 512])
                chain.step(ins)
                v.memset(idle, 0.0)
                v.bn_aggr(mv[:, 0:2], st.rearrange("p a b -> p (a b)")).then_inc(aggregated, 1)

            def narrow(i, out, in_, aggregated, factors):
                chain.step(v.bn_stats(st1x, in_))
                v.memset(idle, 0.0)
                v.bn_aggr(mvx[:, 0:2], st1x).then_inc(aggregated, 1)
                dve.wait_ge(factors, i)
                return v.tensor_scalar(out, in_, mvx[:, 2:3], mvx[:, 3:4], ALU.mult, ALU.add)

            st1x, idle = take(arena, at, [6]), take(arena, at, [1])

            def body(i):
                if runs(i, 0):
                    dve.wait_ge(edge_set, i + 1)
                    dve.wait_ge(xa_in, (i + 1) * 16)
                    if past(i):
                        dve.wait_ge(h_t, i)
                    chain.step(v.scalar_tensor_tensor(h0, xa, e["eps2"][:, 0:1],
                                                      sum0[:, bass.ds(i, 1), 0:D].rearrange("p a f -> p (a f)"),
                                                      ALU.mult, ALU.add))
                    ins = v.scalar_tensor_tensor(h0, e["ee_b2_all"][:, :], edge_sum[:, EMB:EMB + 1], h0,
                                                 ALU.mult, ALU.add)
                    ins.then_inc(h0_used, 1)
                    dve.wait_ge(h0_used, i + 1)
                    dve.wait_ge(e_mm, i + 1)
                    v.tensor_tensor(h0, ps_e[:, 1, :], h0, ALU.add).then_inc(h_set, 1)
                if runs(i, 1):
                    wide(i, a2_mm, e["b2_all"][:, :], a2, st2, mv2, a2_t, a2_out, a2_var)
                if runs(i, 0):
                    wide(i + 1, a1_mm, e["b1_all"][:, :], a1, st1, mv1, a1_t, a1_out, a1_var)
                if runs(i, 2):
                    dve.wait_ge(y_mm, i - 1)
                    chain.step(v.tensor_tensor(y, ps_y[:, :], e["b3_all"][:, :], ALU.add))
                    dve.wait_ge(xc_in, (i - 1) * 16)
                    chain.step(v.tensor_tensor(y, y, xc, ALU.add))
                    chain.step(narrow(i - 1, y, y, y_var, y_set))
                    chain.step(v.tensor_tensor(y, y, e["bn_g_all"][:, :], ALU.mult))
                    chain.step(v.tensor_tensor(y, y, e["bn_b_all"][:, :], ALU.add))
                    ins = v.scalar_tensor_tensor(y, y, 0.0, xc, ALU.max, ALU.add)
                    ins.then_inc(xc_used, 1)
                    dve.wait_ge(xc_used, i - 1)
                    if past(i, 2):
                        dve.wait_ge(x1_t, i - 2)
                        dve.wait_ge(x1_stored, (i - 2) * 16)
                    narrow(i - 1, x1, y, x1_var, x1_fac).then_inc(x1_set, 1)
                if runs(i, 3):
                    dve.wait_ge(wh_mm, i - 2)
                    if past(i, 3):
                        dve.wait_ge(wh_stored, (i - 3) * 16)
                    v.tensor_copy(wh[:, :, 0:C], ps_x[:, 1, :].rearrange("p (h c) -> p h c", h=HEADS))
                    chain.step(v.tensor_tensor(prod, ps_x[:, 1, :], e["att_d"][:, :], ALU.mult))
                    chain.step(v.tensor_reduce(e["score_dst"][:, bass.ds(i - 3, 1), :],
                                               prod.rearrange("p (o h c) -> p o h c", o=1, h=HEADS), AX.X, ALU.add))
                    chain.step(v.tensor_tensor(prod, ps_x[:, 1, :], e["att_s"][:, :], ALU.mult))
                    v.tensor_reduce(wh[:, :, C:GROW], prod.rearrange("p (h c) -> p h c", h=HEADS), AX.X,
                                    ALU.add).then_inc(wh_set, 1)

            pipeline(dve, body, chain)


def attention(nc, env):
    e, phase_sem = env, env["phase_sem"]
    take, sums, sum1, plan = e["take"], e["sums"], e["sum1"], e["plan"]
    src_cols, dst_cols, ident = e["src_cols"], e["dst_cols"], e["ident"]
    with ExitStack() as own:
        def many(name, n=AHEAD):
            return [phase_sem(f"{name}{i}") for i in range(n)]

        def ps(name, shape):
            return own.enter_context(nc.psum_tensor(name, shape, F32))

        at = [e["SPARE"]]
        whg = take(sums, at, [AHEAD * UNIT, HEADS, GROW])
        cand = take(sums, at, [2 * UNIT, HEADS, P])
        miss = own.enter_context(nc.sbuf_tensor("miss", [P, 2, UNIT, P], BF16))
        hits = take(sums, at, [AHEAD, UNIT, P])
        hitsT = take(sums, at, [2, UNIT, P])
        weighted = take(sums, at, [2 * UNIT, HEADS, GROW])
        rel = take(sums, at, [AHEAD, UNIT])
        top = take(sums, at, [HEADS])
        zt = take(sums, at, [HEADS])
        node_z = take(sums, at, [2, 2 * HEADS])
        fall = take(sums, at, [2, HEADS])
        shrink = take(sums, at, [2, HEADS])
        ze = take(sums, at, [UNIT, HEADS])
        zp = take(sums, at, [2, UNIT, HEADS])
        assert at[0] <= sums.shape[1]
        idx = [own.enter_context(nc.sbuf_tensor(f"gidx{u}", [P, UNIT], I32)) for u in range(AHEAD)]
        ps_cand = [ps(f"ps_cand{i}", [P, UNIT, HEADS, P]) for i in range(2)]
        ps_miss = own.enter_context(nc.psum_tensor("ps_miss", [P, UNIT, P], BF16))
        ps_node = ps("ps_node", [P, UNIT, 2 * HEADS])
        ps_sum = [ps(f"ps_att{i}", [P, HEADS, GROW]) for i in range(2)]
        whg_in = many("whg_in", AHEAD * UNIT)
        (rel_set, idx_set, miss_set, cand_set, hits_set, turned, hitsT_set, top_set, node_set, fall_set,
         shrink_set, node_mm, zp_set, p_set, w_set, att_mm, att_out) = [many(n) for n in (
            "g_rel g_idx g_miss g_cand g_hits g_turned g_hitsT g_top g_node g_fall g_shrink g_nodemm "
            "g_zp g_p g_w g_attmm g_attout").split()]
        ident_bf = e["ident_bf"]
        zeroed = phase_sem("g_zeroed")
        steps = phase_sem("g_steps")
        block = own.enter_context(nc.Block())

        @block.gpsimd
        def _(pool):
            g = nc.gpsimd
            for s in rel_set + idx_set:
                pool.sem_inc(s, 1)
            rounds, walk = Rounds(pool, plan, "whg"), Walk(pool, plan, "whg")

            def prepare(p):
                u = p % AHEAD
                rounds.seen(w_set, p - AHEAD)
                rounds.seen(miss_set, p - AHEAD)
                tile, node = walk.place()
                g.tensor_copy(idx[u][:, :], src_cols[:, bass.ds(tile, UNIT)]).then_inc(idx_set[u], 1)
                g.tensor_tensor(rel[:, u, :], dst_cols[:, bass.ds(tile, UNIT)],
                                e["node_base"][:, bass.ds(node, 1), :].rearrange("p a b -> p (a b)"),
                                ALU.subtract).then_inc(rel_set[u], 1)
                rounds.seen(idx_set, p)
                walk.advance()
                for k in range(UNIT):
                    g.indirect_dma_start(whg[:, UNIT * u + k, :, :].rearrange("p h c -> p (h c)"), None,
                                         e["table"], bass.IndirectOffsetOnAxis(ap=idx[u][:, k:k + 1], axis=0)
                                         ).then_inc(whg_in[UNIT * u + k], 16)

            prepare(0)
            prepare(1)
            with pool.Fori(0, rounds.trips):
                rounds.begin()
                for u in range(AHEAD):
                    prepare(u + 2)
                rounds.end()

        @block.scalar
        def _(act):
            a = nc.scalar
            for s in cand_set + hits_set + hitsT_set + shrink_set + p_set:
                act.sem_inc(s, 1)
            rounds = Rounds(act, plan, "cand")

            def candidates(p, k):
                q, u = p % 2, p % AHEAD
                rounds.landed(whg_in, p, k)
                for h in range(HEADS):
                    ins = a.activation(cand[:, UNIT * q + k, h, :], miss[:, q, k, :], ACT.Identity,
                                       bias=whg[:, UNIT * u + k, h, C:GROW], scale=-BIG)
                return ins

            def first(p, between=None):
                q, s = p % 2, p % AHEAD
                rounds.seen(miss_set, p)
                rounds.seen(turned, p - 2)
                candidates(p, 0)
                if between:
                    between()
                candidates(p, 1).then_inc(cand_set[s], 1)

            def hit(p):
                s = p % AHEAD
                rounds.seen(att_mm, p - AHEAD)
                a.activation(hits[:, s, :, :], miss[:, p % 2, :, :], ACT.Copy, bias=1.0, scale=-1.0).then_inc(hits_set[s], 1)

            def turned_hits(p):
                q, s = p % 2, p % AHEAD
                rounds.seen(turned, p)
                rounds.seen(node_mm, p - 2)
                a.activation(hitsT[:, q, :, :], ps_miss[:, :, :], ACT.Copy, bias=1.0,
                             scale=-1.0).then_inc(hitsT_set[s], 1)

            def shrinks(p):
                rounds.seen(fall_set, p)
                rounds.seen(att_out, p - 2)
                a.activation(shrink[:, p % 2, :], fall[:, p % 2, :], ACT.Exp).then_inc(shrink_set[p % AHEAD], 1)

            def weights(u):
                rounds.seen(zp_set, u)
                rounds.seen(att_mm, u - 2)
                a.activation(weighted[:, UNIT * (u % 2):UNIT * (u % 2) + UNIT, :, C:GROW].rearrange(
                    "p k h c -> p k (h c)"), zp[:, u % 2, :, :], ACT.Exp).then_inc(p_set[u], 1)

            first(0)
            hit(0)
            turned_hits(0)
            first(1)
            hit(1)
            shrinks(0)
            with act.Fori(0, rounds.trips):
                rounds.begin()
                for u in range(AHEAD):
                    weights(u)
                    first(u + 2, lambda: turned_hits(u + 1))
                    hit(u + 2)
                    shrinks(u + 1)
                rounds.end()

        @block.tensor
        def _(pe):
            t = nc.tensor
            for s in turned + node_mm + att_mm:
                pe.sem_inc(s, 1)
            rounds = Rounds(pe, plan, "att")

            def turn(p):
                q = p % 2
                rounds.seen(cand_set, p)
                rounds.seen(top_set, p - 2)
                rounds.seen(hitsT_set, p - 1)
                for k in range(UNIT):
                    for h in range(HEADS):
                        t.transpose(ps_cand[q][:, k, h, :], cand[:, UNIT * q + k, h, :], ident[:, :])
                for k in range(UNIT):
                    mm = t.transpose(ps_miss[:, k, :], miss[:, q, k, :], ident_bf[:, :])
                mm.then_inc(turned[p % AHEAD], 1)

            turn(0)
            with pe.Fori(0, rounds.trips):
                rounds.begin()
                for u in range(AHEAD):
                    q = u % 2
                    rounds.seen(node_set, u)
                    rounds.seen(hitsT_set, u)
                    rounds.seen(zp_set, u - 1)
                    for k in range(UNIT):
                        mm = t.matmul(ps_node[:, k, :], hitsT[:, q, k, :], node_z[:, q, :], start=True, stop=True)
                    mm.then_inc(node_mm[u], 1)
                    turn(u + 1)
                    rounds.seen(w_set, u)
                    rounds.seen(hits_set, u)
                    rounds.seen(att_out, u - 2)
                    for k in range(UNIT):
                        mm = t.matmul(ps_sum[q][:, :, :], hits[:, u, k, :], weighted[:, UNIT * q + k, :, :],
                                      start=(k == 0), stop=(k == UNIT - 1))
                    mm.then_inc(att_mm[u], 1)
                rounds.end()

        @block.vector
        def _(dve):
            v, chain = nc.vector, Chain(dve, steps)
            for s in miss_set + top_set + node_set + fall_set + zp_set + w_set + att_out:
                dve.sem_inc(s, 1)
            v.memset(sum1, 0.0).then_inc(zeroed, 1)
            dve.wait_ge(zeroed, 1)
            rounds = Rounds(dve, plan, "top")
            ahead = Walk(dve, plan, "ahead")
            before = dve.alloc_register("node_before")
            dve.reg_mov(before, 0)

            def state(tensor, node):
                return tensor[:, bass.ds(node, 1), :].rearrange("p a h -> p (a h)")

            def misses(p):
                q = p % 2
                rounds.seen(rel_set, p)
                rounds.seen(turned, p - 2)
                rounds.seen(hits_set, p - 2)
                for k in range(UNIT):
                    ins = v.tensor_scalar(miss[:, q, k, :], iota_row[:, :], rel[:, p % AHEAD, k:k + 1], None,
                                          ALU.not_equal)
                ins.then_inc(miss_set[p % AHEAD], 1)

            def tops(p):
                q, s = p % 2, p % AHEAD
                rounds.seen(turned, p)
                ins = v.tensor_reduce(top, ps_cand[q][:, :, :, :].rearrange("p k h e -> p h k e"), AX.XY, ALU.max)
                ins.then_inc(top_set[s], 1)
                _, node = ahead.place()
                node_before = dve.snap(before, min_val=0, max_val=NODE_TILES)
                dve.reg_mov(before, ahead.node)
                ahead.advance()
                score, z = state(e["score_dst"], node), state(e["z_max"], node)
                rounds.seen(node_mm, p - 2)
                v.tensor_tensor(node_z[:, q, HEADS:], score, score, ALU.max)
                rounds.seen(top_set, p)
                m = chain.note(v.tensor_tensor(top, top, score, ALU.add))
                chain.reach(m)
                m = chain.note(v.scalar_tensor_tensor(zt, top, SLOPE, top, ALU.mult, ALU.max))
                chain.reach(m)
                v.tensor_tensor(node_z[:, q, 0:HEADS], z, zt, ALU.max).then_inc(node_set[s], 1)
                rounds.seen(node_set, p)
                rounds.seen(shrink_set, p - 2)
                v.tensor_tensor(fall[:, q, :], z, node_z[:, q, 0:HEADS], ALU.subtract).then_inc(fall_set[s], 1)
                rounds.seen(fall_set, p)
                chain.step(v.tensor_tensor(z, z, node_z[:, q, 0:HEADS], ALU.max))
                return node_before

            iota_row = e["iota_row"]
            misses(0)
            misses(1)
            tops(0)
            chain.enter()
            with dve.Fori(0, rounds.trips):
                rounds.begin()
                chain.begin()
                for u in range(AHEAD):
                    q = u % 2
                    rounds.seen(node_mm, u)
                    slots = slice(UNIT * u, UNIT * u + UNIT)
                    for k in range(UNIT):
                        rounds.landed(whg_in, u, k)
                    chain.step(v.tensor_tensor(ze, whg[:, slots, :, C:GROW].rearrange("p k h c -> p k (h c)"),
                                               ps_node[:, :, HEADS:], ALU.add))
                    chain.step(v.scalar_tensor_tensor(ze, ze, SLOPE, ze, ALU.mult, ALU.max))
                    chain.step(v.tensor_tensor(ze, ze, ps_node[:, :, 0:HEADS], ALU.subtract))
                    rounds.seen(p_set, u - 2)
                    v.tensor_scalar(zp[:, q, :, :], ze, 0.0, None, ALU.min).then_inc(zp_set[u], 1)
                    misses(u + 2)
                    rounds.seen(p_set, u)
                    wslots = slice(UNIT * q, UNIT * q + UNIT)
                    v.tensor_tensor(weighted[:, wslots, :, 0:C].rearrange("p k h c -> p (k h) c"),
                                    whg[:, slots, :, 0:C].rearrange("p k h c -> p (k h) c"),
                                    weighted[:, wslots, :, C:GROW].rearrange("p k h c -> p (k h) c").to_broadcast(
                                        [P, UNIT * HEADS, C]), ALU.mult).then_inc(w_set[u], 1)
                    node = tops(u + 1)
                    rounds.seen(att_mm, u)
                    rounds.seen(shrink_set, u)
                    rounds.seen(att_out, u - 1)
                    to = sum1[:, bass.ds(node, 1), :].rearrange("p a (h c) -> p (a h) c", h=HEADS)
                    for h in range(HEADS):
                        ins = v.scalar_tensor_tensor(to[:, h, :], to[:, h, :], shrink[:, q, h:h + 1],
                                                     ps_sum[q][:, h, :], ALU.mult, ALU.add)
                    ins.then_inc(att_out[u], 1)
                chain.end()
                rounds.end()

    with ExitStack() as own:
        def sem(name):
            return phase_sem(name)

        at = [0]
        arena = e["arena"]
        x1 = take(arena, at, [2, D])
        den = take(arena, at, [HEADS])
        low, high = take(arena, at, [2, D]), take(arena, at, [2, D])
        res, st, mv = take(arena, at, [2, D]), take(arena, at, [6]), take(arena, at, [2, 4])
        idle = take(arena, at, [1])
        x1_in = [sem("x1_in0"), sem("x1_in1")]
        stored = [sem("stored0"), sem("stored1")]
        low_set, exp_set, var_set, res_set, normed, steps, pool_steps = [
            sem(f"f_{n}") for n in "low exp var res normed steps pool_steps".split()]
        out, x1_dram = e["out"], e["x1_dram"]
        PAIRS = -(-NODE_TILES // 2)
        block = own.enter_context(nc.Block())

        @block.sync
        def _(sp):
            def load(i, q):
                sp.dma_start(x1[:, q, :], x1_dram[bass.ds(i * P, P), :]).then_inc(x1_in[q], 16)

            def store(i, q):
                sp.wait_ge(normed, i + 1)
                sp.dma_start(out[bass.ds(i * P, P), :], res[:, q, :]).then_inc(stored[q], 16)

            load(0, 0)
            load(1, 1)
            with sp.Fori(0, NODE_TILES // 2 - 1) as j:
                j = sp.snap(j, min_val=0, max_val=NODE_TILES // 2 - 2)
                for q in range(2):
                    store(2 * j + q, q)
                    load(2 * j + 2 + q, q)
            store(NODE_TILES - 3, 0)
            load(NODE_TILES - 1, 0)
            store(NODE_TILES - 2, 1)
            store(NODE_TILES - 1, 0)
            sp.wait_ge(stored[0], 16 * PAIRS)
            sp.wait_ge(stored[1], 16 * (NODE_TILES - PAIRS))

        def halves(eng, body, chain=None):
            for q in range(2):
                body(q, q, 0)
            if chain:
                chain.enter()
            with eng.Fori(1, NODE_TILES // 2) as j:
                j = eng.snap(j, min_val=1, max_val=NODE_TILES // 2 - 1)
                if chain:
                    chain.begin()
                for q in range(2):
                    body(2 * j + q, q, j)
                if chain:
                    chain.end()
            if chain:
                chain.leave(NODE_TILES // 2 - 1)
            body(NODE_TILES - 1, 0, NODE_TILES // 2)

        @block.gpsimd
        def _(pool):
            g, chain = nc.gpsimd, Chain(pool, pool_steps)

            def body(i, q, j):
                pool.wait_ge(var_set, i + 1)
                norm_factors(g, chain, mv[:, q, :], e["powers"]).then_inc(res_set, 1)

            halves(pool, body, chain)

        @block.scalar
        def _(act):
            def body(i, q, j):
                act.wait_ge(low_set, i + 1)
                nc.scalar.activation(low[:, q, :], low[:, q, :], ACT.Exp).then_inc(exp_set, 1)
                act.wait_ge(res_set, i + 1)
                nc.scalar.activation(res[:, q, :], res[:, q, :], ACT.Identity, bias=mv[:, q, 3:4],
                                     scale=mv[:, q, 2:3]).then_inc(normed, 1)

            halves(act, body)

        @block.vector
        def _(dve):
            v, chain = nc.vector, Chain(dve, steps)

            def body(i, q, j):
                s = sum1[:, bass.ds(i, 1), :].rearrange("p a (h c) -> p (a h) c", h=HEADS)
                chain.step(v.tensor_scalar(den, s[:, :, C:GROW].rearrange("p h c -> p (h c)"), DEN_EPS, None,
                                           ALU.add))
                chain.step(v.reciprocal(den, den))
                hq = high[:, q, :].rearrange("p (h c) -> p h c", h=HEADS)
                chain.step(v.tensor_tensor(hq, s[:, :, 0:C], den.rearrange("p (h c) -> p h c", c=1).to_broadcast(
                    [P, HEADS, C]), ALU.mult))
                v.tensor_scalar(low[:, q, :], high[:, q, :], 0.0, None, ALU.min).then_inc(low_set, 1)
                dve.wait_ge(x1_in[q], (j + 1) * 16)
                if not isinstance(i, int) or i >= 2:
                    dve.wait_ge(stored[q], j * 16)
                chain.step(v.scalar_tensor_tensor(res[:, q, :], high[:, q, :], 0.0, x1[:, q, :], ALU.max, ALU.add))
                dve.wait_ge(exp_set, i + 1)
                chain.step(v.scalar_tensor_tensor(res[:, q, :], low[:, q, :], -1.0, res[:, q, :], ALU.add, ALU.add))
                chain.step(v.bn_stats(st, res[:, q, :]))
                v.memset(idle, 0.0)
                v.bn_aggr(mv[:, q, 0:2], st).then_inc(var_set, 1)

            halves(dve, body, chain)


def kernel(**inputs):
    import numpy as np
    import concourse.bacc as bacc
    from concourse.bass_utils import run_bass_kernel_spmd

    a = {k: np.asarray(v) for k, v in inputs.items()}
    L0 = {k[len("L0_gnn_"):]: v for k, v in a.items() if k.startswith("L0_gnn_")}

    def padded(v, n, fill):
        out = np.full((n, *v.shape[1:]), fill, v.dtype)
        out[:len(v)] = v
        return out

    dst = padded(a["dst"], ALL_TILES * P, -1)
    arrays = {
        "x": padded(a["x"], NODE_TILES * P, 0),
        "srcT": padded(a["src"], ALL_TILES * P, 0).reshape(ALL_TILES, P).T,
        "dstT": dst.reshape(ALL_TILES, P).T,
        "dst_rows": padded(a["dst"], TILE_ROWS * P * P, -1).reshape(TILE_ROWS, P, P).transpose(1, 0, 2),
        "eaT": padded(a["edge_attr_64"], ALL_TILES * P, 0).T,
        "eps": L0["eps"].reshape(1),
        "ee_w1": L0["ee_w1"], "ee_b1": L0["ee_b1"], "ee_w2": L0["ee_w2"], "ee_b2": L0["ee_b2"],
        "w1": L0["w1"], "b1": L0["b1"],
        "g1T": L0["g1"].reshape(-1, P).T, "be1T": L0["be1"].reshape(-1, P).T,
        "w2": L0["w2"], "b2": L0["b2"],
        "g2T": L0["g2"].reshape(-1, P).T, "be2T": L0["be2"].reshape(-1, P).T,
        "w3": L0["w3"], "b3": L0["b3"], "bn_g": L0["bn_g"], "bn_b": L0["bn_b"],
        "gat_wT": a["L1_gnn_W"].T,
        "att_src": a["L1_gnn_att"][:, :C].reshape(-1), "att_dst": a["L1_gnn_att"][:, C:].reshape(-1),
    }
    nc = bacc.Bacc("TRN2", target_bir_lowering=False, num_devices=1)
    args, fed = [], {}
    for name, v in arrays.items():
        v = np.ascontiguousarray(v)
        fed[f"in_{name}"] = v
        args.append(nc.dram_tensor(f"in_{name}", v.shape, mybir.dt.from_np(v.dtype), kind="ExternalInput").ap())
    out = nc.dram_tensor("out_rows", (NODE_TILES * P, D), F32, kind="ExternalOutput").ap()
    bass_gnn_resnorm(nc, *args, out)
    r = run_bass_kernel_spmd(nc, [fed], core_ids=[0])
    return r.results[0]["out_rows"][:N_NODES]
```

```python
from contextlib import ExitStack

import concourse.bass as bass
from concourse import mybir

ALU = mybir.AluOpType
ACT = mybir.ActivationFunctionType
AX = mybir.AxisListType
F32 = mybir.dt.float32
I32 = mybir.dt.int32
BF16 = mybir.dt.bfloat16

P = 128
N_NODES, N_EDGES = 6250, 100000
D, EDIM, EMB, H = 256, 64, 256, 1024
HEADS, C = 4, 64
NODE_TILES = -(-N_NODES // P)
EDGE_TILES = -(-N_EDGES // P)
UNIT = 2
AHEAD = 4
GROUP = 6
PAD_TILES = 2 * AHEAD * GROUP
ALL_TILES = EDGE_TILES + PAD_TILES
TILE_ROWS = -(-EDGE_TILES // P)
GROW = C + 1
PARTS = 3
TABLE = HEADS * GROW + HEADS * PARTS // 2
BIG = 2.0 ** 100
BANKS = 3
DIV_GROUP = float(65536 // GROUP + 1)
FAR = 1000.0
LN_EPS = 1e-5
SLOPE = 0.2
DEN_EPS = 1e-16
MANY = 1 << 20
COUNT_ROW = {UNIT: 1, GROUP: 3}


class Chain:

    def __init__(self, eng, sem):
        self.eng, self.sem, self.base, self.count = eng, sem, None, 0

    def note(self, ins):
        self.count += 1
        ins.then_inc(self.sem, 1)
        return self.count

    def reach(self, count):
        self.eng.wait_ge(self.sem, count if self.base is None else self.base + count)

    def step(self, ins):
        self.reach(self.note(ins))

    def enter(self):
        self.reg = self.eng.alloc_register(f"{self.sem.name}_count")
        self.eng.reg_mov(self.reg, self.count)
        self.before = self.count

    def begin(self):
        self.base, self.count = self.eng.snap(self.reg, min_val=0, max_val=MANY * 64), 0

    def end(self):
        self.eng.reg_add(self.reg, self.reg, self.count)

    def leave(self, trips):
        self.count, self.base = self.before + trips * self.count, None


class Walk:

    def __init__(self, eng, plan, name, size=UNIT):
        self.eng, self.plan, self.size = eng, plan, size
        self.row = COUNT_ROW[size]
        self.tile = eng.alloc_register(f"{name}_tile")
        self.node = eng.alloc_register(f"{name}_node")
        self.left = eng.alloc_register(f"{name}_left")
        eng.reg_mov(self.node, 0)
        eng.reg_load(self.tile, plan[0:1, 0, 0:1])
        eng.reg_load(self.left, plan[0:1, self.row, 0:1])

    def place(self):
        return (self.eng.snap(self.tile, min_val=0, max_val=ALL_TILES - self.size),
                self.eng.snap(self.node, min_val=0, max_val=NODE_TILES))

    def advance(self):
        eng = self.eng
        eng.reg_add(self.tile, self.tile, self.size)
        eng.reg_add(self.left, self.left, -1)
        with eng.If_eq(self.left, 0):
            eng.reg_add(self.node, self.node, 1)
            node = eng.snap(self.node, min_val=0, max_val=NODE_TILES)
            eng.reg_load(self.tile, self.plan[0:1, 0, bass.ds(node, 1)])
            eng.reg_load(self.left, self.plan[0:1, self.row, bass.ds(node, 1)])


class Rounds:

    def __init__(self, eng, plan, name, size=UNIT):
        self.eng, self.name, self.size = eng, name, size
        self.reg = eng.alloc_register(f"{name}_round")
        eng.reg_mov(self.reg, 1)
        self.trips = eng.value_load(plan[0:1, COUNT_ROW[size] + 1, 0:1], min_val=1, max_val=MANY)
        self.now = [1, 2, 3]

    def begin(self):
        n = self.eng.snap(self.reg, min_val=1, max_val=MANY)
        self.now = [n, self.eng.snap(n + 1), self.eng.snap(n + 2)]

    def end(self):
        self.eng.reg_add(self.reg, self.reg, 1)

    def seen(self, sems, at, k=None):
        sem = sems[at % AHEAD] if k is None else sems[self.size * (at % AHEAD) + k]
        self.eng.wait_ge(sem, self.now[1 + at // AHEAD])

    def landed(self, sems, at, k=None):
        sem = sems[at % AHEAD] if k is None else sems[self.size * (at % AHEAD) + k]
        self.eng.wait_ge(sem, self.now[at // AHEAD] * 16)


def bass_gnn_resnorm(nc, x, srcT, dstT, dst_rows, eaT, eps, ee_w1, ee_b1, ee_w2, ee_b2, w1, b1, g1T,
                     be1T, w2, b2, g2T, be2T, w3, b3, bn_g, bn_b, gat_wT, att_src, att_dst, out):
    with ExitStack() as ctx:
        def sb(name, shape, dt=F32):
            return ctx.enter_context(nc.sbuf_tensor(name, shape, dt))

        in_phase = []

        def phase_sem(name):
            in_phase.append(nc.alloc_semaphore(name))
            return in_phase[-1]

        def end_phase():
            nc.clear_and_free_semaphores(in_phase)
            nc.all_engine_barrier()
            in_phase.clear()

        table = nc.dram_tensor("wh_table", (NODE_TILES * P, TABLE), F32, kind="Internal").ap()
        x1_dram = nc.dram_tensor("x1_rows", (NODE_TILES * P, D), F32, kind="Internal").ap()

        plan = sb("plan", [1, 5, NODE_TILES + 1], I32)
        src_cols = sb("src_cols", [P, ALL_TILES], I32)
        dst_cols = sb("dst_cols", [P, ALL_TILES])
        node_base = sb("node_base", [P, NODE_TILES + 1, GROUP])
        iota_row = sb("iota_row", [P, P])
        ident = sb("ident", [P, P])
        ident_bf = sb("ident_bf", [P, P], BF16)
        ee_w1b = sb("ee_w1b", [EDIM + 1, EMB])
        ee_w2s = sb("ee_w2s", [P, 2, D])
        w1s = sb("w1s", [P, D // P, H])
        w2s = sb("w2s", [P, H // P, H])
        w3s = sb("w3s", [P, H // P, D])
        gat_w = sb("gat_w", [P, D // P, D])
        g1s, be1s = sb("g1s", [P, H // P]), sb("be1s", [P, H // P])
        g2s, be2s = sb("g2s", [P, H // P]), sb("be2s", [P, H // P])
        b1_all, b2_all = sb("b1_all", [P, H]), sb("b2_all", [P, H])
        self_row = sb("self_row", [P, EMB + 1])
        ee_b2_all = sb("ee_b2_all", [P, D])
        b3_all = sb("b3_all", [P, D])
        bn_g_all, bn_b_all = sb("bn_g_all", [P, D]), sb("bn_b_all", [P, D])
        att_s, att_d = sb("att_s", [P, D]), sb("att_d", [P, D])
        eps2 = sb("eps2", [P, 1])
        powers = sb("powers", [P, 4])
        score_dst = sb("score_dst", [P, NODE_TILES + 1, HEADS])
        z_max = sb("z_max", [P, NODE_TILES + 1, HEADS])
        SUM0 = D + EMB + 1
        sums = sb("sums", [P, (NODE_TILES + 1) * SUM0])
        sum0 = sums[:, :].rearrange("p (b f) -> p b f", f=SUM0)
        SUM1 = HEADS * GROW
        sum1 = sums[:, 0:(NODE_TILES + 1) * SUM1].rearrange("p (b f) -> p b f", f=SUM1)
        SPARE = (NODE_TILES + 1) * SUM1
        arena = sb("arena", [P, 7000])

        def take(tensor, at, shape):
            n = 1
            for s in shape:
                n *= s
            v = tensor[:, at[0]:at[0] + n]
            at[0] += n
            if len(shape) == 2:
                return v.rearrange("p (a b) -> p a b", b=shape[1])
            if len(shape) == 3:
                return v.rearrange("p (a b c) -> p a b c", b=shape[1], c=shape[2])
            return v

        with ExitStack() as own:
            at = [0]
            dst_f = take(arena, at, [TILE_ROWS, P])
            dst_neg = take(arena, at, [TILE_ROWS, P])
            hi, lo = take(arena, at, [TILE_ROWS]), take(arena, at, [TILE_ROWS])
            tile_no, tile_back = take(arena, at, [TILE_ROWS]), take(arena, at, [TILE_ROWS])
            base_lo, base_hi = take(arena, at, [NODE_TILES]), take(arena, at, [NODE_TILES])
            above, meets = take(arena, at, [NODE_TILES]), take(arena, at, [NODE_TILES])
            ranges, ranges_all = take(arena, at, [2, NODE_TILES]), take(arena, at, [2, NODE_TILES])
            firsts, counts = take(arena, at, [NODE_TILES]), take(arena, at, [NODE_TILES])
            total, wanted = take(arena, at, [1]), take(arena, at, [NODE_TILES])
            counts_i = own.enter_context(nc.sbuf_tensor("counts_i", [1, NODE_TILES + 1], I32))
            rows_i = sums[:, ALL_TILES:ALL_TILES + TILE_ROWS * P].bitcast(I32).rearrange("p (c e) -> p c e", e=P)
            cols_i = sums[:, 0:ALL_TILES].bitcast(I32)
            plan_in, loaded = phase_sem("plan_in"), phase_sem("loaded")
            made = phase_sem("made")
            ranged = phase_sem("ranged")
            reduced = phase_sem("reduced")
            own_steps, pool_steps = phase_sem("plan_steps"), phase_sem("const_steps")
            block = own.enter_context(nc.Block())

            def every_partition(row, n):
                return row.rearrange("(o n) -> o n", o=1).to_broadcast([P, n])

            @block.sync
            def _(sp):
                sp.dma_start(rows_i[:, :, :], dst_rows).then_inc(plan_in, 16)
                sp.dma_start(cols_i, dstT).then_inc(plan_in, 16)
                sp.dma_start(src_cols[:, :], srcT).then_inc(loaded, 16)
                sp.dma_start(ee_w1b[0:EDIM, :], ee_w1).then_inc(loaded, 16)
                sp.dma_start(ee_w1b[EDIM:EDIM + 1, :], ee_b1.rearrange("(o n) -> o n", o=1)).then_inc(loaded, 16)
                n = 3
                for to, of in [(ee_w2s, ee_w2), (w1s, w1), (w2s, w2), (w3s, w3), (gat_w, gat_wT)]:
                    sp.dma_start(to[:, :, :], of.rearrange("(k p) n -> p k n", p=P)).then_inc(loaded, 16)
                    n += 1
                for to, of in [(g1s, g1T), (be1s, be1T), (g2s, g2T), (be2s, be2T)]:
                    sp.dma_start(to[:, :], of).then_inc(loaded, 16)
                    n += 1
                for to, of in [(b1_all, b1), (b2_all, b2), (ee_b2_all, ee_b2), (b3_all, b3),
                               (bn_g_all, bn_g), (bn_b_all, bn_b), (att_s, att_src), (att_d, att_dst)]:
                    sp.dma_start(to[:, :], every_partition(of, to.shape[1])).then_inc(loaded, 16)
                    n += 1
                sp.dma_start(self_row[:, 0:EMB], every_partition(ee_b1, EMB)).then_inc(loaded, 16)
                sp.dma_start(eps2[:, :], every_partition(eps, 1)).then_inc(loaded, 16)
                sp.wait_ge(loaded, 16 * (n + 2))

            @block.gpsimd
            def _(pool):
                g = nc.gpsimd
                g.iota(tile_no, [[P, TILE_ROWS]], base=0, channel_multiplier=1,
                       allow_small_or_imprecise_dtypes=True).then_inc(made, 1)
                g.iota(base_lo, [[P, NODE_TILES]], base=0, channel_multiplier=0,
                       allow_small_or_imprecise_dtypes=True).then_inc(made, 1)
                g.iota(base_hi, [[P, NODE_TILES]], base=P - 1, channel_multiplier=0,
                       allow_small_or_imprecise_dtypes=True).then_inc(made, 1)
                g.iota(iota_row[:, :], [[1, P]], base=0, channel_multiplier=0,
                       allow_small_or_imprecise_dtypes=True)
                g.iota(node_base[:, :, :], [[P, NODE_TILES + 1], [0, GROUP]], base=0, channel_multiplier=0,
                       allow_small_or_imprecise_dtypes=True)
                for n, c in enumerate((LN_EPS, -0.5, -1.0, 0.0)):
                    g.memset(powers[:, n:n + 1], c)
                g.memset(ident[:, :], 0.0).then_inc(pool_steps, 1)
                pool.wait_ge(pool_steps, 1)
                g.affine_select(out=ident[:, :], in_=ident[:, :], compare_op=ALU.not_equal, fill=1.0, base=0,
                                pattern=[[-1, P]], channel_multiplier=1)
                pool.wait_ge(ranged, 1)
                g.partition_all_reduce(ranges_all, ranges, P, bass.bass_isa.ReduceOp.max).then_inc(reduced, 1)

            @block.vector
            def _(dve):
                v, chain = nc.vector, Chain(dve, own_steps)
                dve.wait_ge(plan_in, 32)
                v.tensor_copy(dst_cols[:, :], cols_i)
                v.memset(score_dst[:, :, :], 0.0)
                v.memset(z_max[:, :, :], -BIG)
                chain.step(v.tensor_copy(dst_f, rows_i[:, :, :]))
                v.tensor_reduce(hi, dst_f, AX.X, ALU.max)
                chain.step(v.tensor_scalar(dst_neg, dst_f, 0.0, 1.0e6, ALU.is_lt, ALU.mult))
                chain.step(v.tensor_tensor(dst_neg, dst_neg, dst_f, ALU.add))
                chain.step(v.tensor_reduce(lo, dst_neg, AX.X, ALU.min))
                dve.wait_ge(made, 3)
                v.memset(ranges, 0.0)
                v.tensor_scalar(tile_back, tile_no, -1.0, FAR, ALU.mult, ALU.add)
                chain.step(v.tensor_scalar(tile_no, tile_no, 1.0, None, ALU.add))
                for c in range(TILE_ROWS):
                    chain.step(v.tensor_scalar(above, base_hi, lo[:, c:c + 1], None, ALU.is_ge))
                    chain.step(v.scalar_tensor_tensor(meets, base_lo, hi[:, c:c + 1], above, ALU.is_le, ALU.mult))
                    v.scalar_tensor_tensor(ranges[:, 0, :], meets, tile_back[:, c:c + 1], ranges[:, 0, :],
                                           ALU.mult, ALU.max)
                    chain.step(v.scalar_tensor_tensor(ranges[:, 1, :], meets, tile_no[:, c:c + 1],
                                                      ranges[:, 1, :], ALU.mult, ALU.max))
                v.tensor_copy(total[0:1, :], total_zero(v, chain, total)).then_inc(ranged, 1)
                dve.wait_ge(reduced, 1)
                r = ranges_all[0:1, :, :]
                chain.step(v.tensor_scalar(firsts[0:1, :], r[:, 0, :], -1.0, FAR, ALU.mult, ALU.add))
                v.tensor_scalar(plan[0:1, 0, 0:NODE_TILES], firsts[0:1, :], float(EDGE_TILES), None, ALU.min)
                chain.step(v.scalar_tensor_tensor(counts[0:1, :], r[:, 0, :], -FAR, r[:, 1, :], ALU.add, ALU.add))
                v.memset(plan[0:1, 0, NODE_TILES:], EDGE_TILES)
                for size, times, shift in ((UNIT, 1.0, 1), (GROUP, DIV_GROUP, 16)):
                    row = COUNT_ROW[size]
                    chain.step(v.tensor_scalar(wanted[0:1, :], counts[0:1, :], 1.0, float(size - 1), ALU.max,
                                               ALU.add))
                    chain.step(v.tensor_scalar(counts_i[0:1, 0:NODE_TILES], wanted[0:1, :], times, None, ALU.mult))
                    chain.step(v.tensor_scalar(plan[0:1, row, 0:NODE_TILES], counts_i[0:1, 0:NODE_TILES], shift,
                                               None, ALU.logical_shift_right))
                    v.memset(plan[0:1, row, NODE_TILES:], MANY)
                    chain.step(v.tensor_reduce(total[0:1, :], plan[0:1, row, 0:NODE_TILES], AX.X, ALU.add))
                    chain.step(v.tensor_scalar(counts_i[0:1, 0:1], total[0:1, :], float(AHEAD - 1), None, ALU.add))
                    chain.step(v.tensor_scalar(plan[0:1, row + 1, 0:1], counts_i[0:1, 0:1], 2, None,
                                               ALU.logical_shift_right))
                v.memset(sum0, 0.0)

        with ExitStack() as own:
            block = own.enter_context(nc.Block())

            @block.vector
            def _(dve):
                v = nc.vector
                v.tensor_scalar(self_row[:, 0:EMB], self_row[:, 0:EMB], 0.0, None, ALU.max)
                v.memset(self_row[:, EMB:], 1.0)
                v.tensor_scalar(eps2[:, :], eps2[:, :], 2.0, None, ALU.add)
                v.tensor_copy(ident_bf[:, :], ident[:, :])

        with ExitStack() as own:
            at = [0]
            xg = take(arena, at, [AHEAD * UNIT, D])
            hid = take(arena, at, [2, UNIT, (EMB + 2)])
            ea = take(arena, at, [AHEAD, UNIT * P])
            hits = take(arena, at, [AHEAD, UNIT, P])
            rel = take(arena, at, [AHEAD, UNIT])
            idx = [own.enter_context(nc.sbuf_tensor(f"idx{u}", [P, UNIT], I32)) for u in range(AHEAD)]
            ps_hid = [own.enter_context(nc.psum_tensor(f"ps_hid{i}", [P, UNIT, EMB], F32)) for i in range(2)]
            ps_sum = [own.enter_context(nc.psum_tensor(f"ps_sum{i}", [P, 2, 512], F32)) for i in range(2)]

            def many(name, n=AHEAD):
                return [phase_sem(f"{name}{i}") for i in range(n)]

            ea_in, xg_in = many("ea_in"), many("xg_in", AHEAD * UNIT)
            rel_set, hits_set = many("rel_set"), many("hits_set")
            hid_mm, hid_set, sum_mm, sum_out = many("hid_mm"), many("hid_set"), many("sum_mm"), many("sum_out")
            ones_set = phase_sem("ones_set")
            idx_set = many("idx_set")
            block = own.enter_context(nc.Block())

            @block.sync
            def _(sp):
                rounds, walk = Rounds(sp, plan, "ea"), Walk(sp, plan, "ea")

                def load(p):
                    tile, _ = walk.place()
                    rounds.seen(hid_mm, p - AHEAD)
                    sp.dma_start(ea[0:EDIM, p % AHEAD, :], eaT[:, bass.ds(tile * P, UNIT * P)]).then_inc(
                        ea_in[p % AHEAD], 16)
                    walk.advance()

                load(0)
                with sp.Fori(0, rounds.trips):
                    rounds.begin()
                    for u in range(AHEAD):
                        load(u + 1)
                    rounds.end()

            @block.gpsimd
            def _(pool):
                g = nc.gpsimd
                for s in rel_set + idx_set:
                    pool.sem_inc(s, 1)
                rounds, walk = Rounds(pool, plan, "xg"), Walk(pool, plan, "xg")

                def prepare(p):
                    u = p % AHEAD
                    rounds.seen(sum_mm, p - AHEAD)
                    tile, node = walk.place()
                    g.tensor_copy(idx[u][:, :], src_cols[:, bass.ds(tile, UNIT)]).then_inc(idx_set[u], 1)
                    g.tensor_tensor(rel[:, u, :], dst_cols[:, bass.ds(tile, UNIT)],
                                    node_base[:, bass.ds(node, 1), 0:UNIT].rearrange("p a b -> p (a b)"),
                                    ALU.subtract).then_inc(rel_set[u], 1)
                    rounds.seen(idx_set, p)
                    walk.advance()
                    for k in range(UNIT):
                        g.indirect_dma_start(xg[:, UNIT * u + k, :], None, x,
                                             bass.IndirectOffsetOnAxis(ap=idx[u][:, k:k + 1], axis=0)
                                             ).then_inc(xg_in[UNIT * u + k], 16)

                prepare(0)
                with pool.Fori(0, rounds.trips):
                    rounds.begin()
                    for u in range(AHEAD):
                        prepare(u + 1)
                    rounds.end()
                for k in range(UNIT):
                    pool.wait_ge(xg_in[k], pool.snap(rounds.trips * 16) + 16)

            @block.scalar
            def _(act):
                for s in hid_set:
                    act.sem_inc(s, 1)
                rounds = Rounds(act, plan, "hid")

                def relu(p):
                    rounds.seen(hid_mm, p)
                    rounds.seen(sum_mm, p - 2)
                    nc.scalar.activation(hid[:, p % 2, :, 0:EMB], ps_hid[p % 2][:, :, :],
                                         ACT.Relu).then_inc(hid_set[p % AHEAD], 1)

                relu(0)
                with act.Fori(0, rounds.trips):
                    rounds.begin()
                    for u in range(AHEAD):
                        relu(u + 1)
                    rounds.end()

            @block.tensor
            def _(pe):
                for s in hid_mm + sum_mm:
                    pe.sem_inc(s, 1)
                rounds = Rounds(pe, plan, "mm")

                def hidden(p):
                    rounds.landed(ea_in, p)
                    rounds.seen(hid_set, p - 2)
                    for k in range(UNIT):
                        mm = nc.tensor.matmul(ps_hid[p % 2][:, k, :], ea[0:EDIM + 1, p % AHEAD, k * P:(k + 1) * P],
                                              ee_w1b[:, :], start=True, stop=True)
                    mm.then_inc(hid_mm[p % AHEAD], 1)

                pe.wait_ge(ones_set, 1)
                hidden(0)
                with pe.Fori(0, rounds.trips):
                    rounds.begin()
                    for u in range(AHEAD):
                        hidden(u + 1)
                        rounds.seen(hits_set, u)
                        rounds.seen(hid_set, u)
                        rounds.seen(sum_out, u - 2)
                        for k in range(UNIT):
                            rounds.landed(xg_in, u, k)
                            nc.tensor.matmul(ps_sum[u % 2][:, 0, 0:D], hits[:, u, k, :], xg[:, UNIT * u + k, :],
                                             start=(k == 0), stop=(k == UNIT - 1))
                            mm = nc.tensor.matmul(ps_sum[u % 2][:, 1, 0:EMB + 2], hits[:, u, k, :],
                                                  hid[:, u % 2, k, :], start=(k == 0), stop=(k == UNIT - 1))
                        mm.then_inc(sum_mm[u], 1)
                    rounds.end()

            @block.vector
            def _(dve):
                v = nc.vector
                for s in hits_set + sum_out:
                    dve.sem_inc(s, 1)
                v.memset(hid[:, :, :, EMB:EMB + 1], 1.0)
                v.memset(hid[:, :, :, EMB + 1:EMB + 2], 0.0)
                v.memset(ea[EDIM:EDIM + 1, :, :], 1.0).then_inc(ones_set, 1)
                rounds, walk = Rounds(dve, plan, "sum"), Walk(dve, plan, "sum")

                def compare(p):
                    rounds.seen(rel_set, p)
                    rounds.seen(sum_mm, p - AHEAD)
                    for k in range(UNIT):
                        ins = v.tensor_scalar(hits[:, p % AHEAD, k, :], iota_row[:, :], rel[:, p % AHEAD, k:k + 1],
                                              None, ALU.is_equal)
                    ins.then_inc(hits_set[p % AHEAD], 1)

                compare(0)
                with dve.Fori(0, rounds.trips):
                    rounds.begin()
                    for u in range(AHEAD):
                        compare(u + 1)
                        _, node = walk.place()
                        rounds.seen(sum_mm, u)
                        rounds.seen(sum_out, u - 1)
                        to = sum0[:, bass.ds(node, 1), :].rearrange("p a f -> p (a f)")
                        v.tensor_tensor(to[:, 0:D + EMB].rearrange("p (a f) -> p a f", a=2),
                                        to[:, 0:D + EMB].rearrange("p (a f) -> p a f", a=2),
                                        ps_sum[u % 2][:, :, 0:EMB], ALU.add)
                        v.tensor_tensor(to[:, D + EMB:], to[:, D + EMB:], ps_sum[u % 2][:, 1, EMB:EMB + 1],
                                        ALU.add).then_inc(sum_out[u], 1)
                        walk.advance()
                    rounds.end()

        end_phase()
        node_mlp(nc, locals())
        end_phase()
        attention(nc, locals())
        end_phase()
        output_norm(nc, locals())


def total_zero(v, chain, total):
    chain.step(v.memset(total[0:1, :], 0.0))
    return total[0:1, :]


def norm_factors(g, chain, mv, powers):
    chain.step(g.tensor_tensor(mv[:, 2:3], mv[:, 1:2], powers[:, 0:1], ALU.add))
    g.tensor_tensor(mv[:, 3:4], mv[:, 0:1], powers[:, 2:3], ALU.mult)
    chain.step(g.tensor_tensor(mv[:, 2:3], mv[:, 2:3], powers[:, 1:2], ALU.pow))
    return g.tensor_tensor(mv[:, 3:4], mv[:, 3:4], mv[:, 2:3], ALU.mult)


def node_mlp(nc, env):
    e, phase_sem = env, env["phase_sem"]
    arena, take, sum0 = e["arena"], e["take"], e["sum0"]
    KH, KD = H // P, D // P
    STEPS = 4
    with ExitStack() as own:
        def sem(name):
            return phase_sem(name)

        def ps(name, shape):
            return own.enter_context(nc.psum_tensor(name, shape, F32))

        at = [0]
        edge_sum = take(arena, at, [EMB + 1])
        edge_sumT = take(arena, at, [KD, P])
        xa, xc = take(arena, at, [D]), take(arena, at, [D])
        h0, hT = take(arena, at, [D]), take(arena, at, [KD, P])
        a1, a2 = take(arena, at, [H]), take(arena, at, [H])
        a1T, a2T = take(arena, at, [KH, P]), take(arena, at, [KH, P])
        y, x1, x1T = take(arena, at, [D]), take(arena, at, [D]), take(arena, at, [KD, P])
        wh_row = take(arena, at, [TABLE])
        wh = wh_row[:, 0:HEADS * GROW].rearrange("p (h c) -> p h c", h=HEADS)
        wh_scores = wh[:, :, C:GROW].rearrange("p h c -> p (h c)")
        wh_parts = wh_row[:, HEADS * GROW:].bitcast(BF16)
        rest = take(arena, at, [HEADS])
        prod = take(arena, at, [D])
        st1, st2 = take(arena, at, [2, 6]), take(arena, at, [2, 6])
        mv1, mv2, mvx = take(arena, at, [4]), take(arena, at, [4]), take(arena, at, [4])
        ps_e = ps("ps_e", [P, 2, D])
        ps_y = ps("ps_y", [P, D])
        ps_x = ps("ps_x", [P, 2, D])
        ps_w = ps("ps_w", [P, 2, 512])
        ps_n = ps("ps_n", [P, KH, P])

        (xa_in, xc_in, edge_set, edge_t, edge_c, e_mm, h_set, h_t, h_c, a1_mm, a1_out, a1_set, a1_n,
         a1_t, a1_c, a2_mm, a2_out, a2_set, a2_n, a2_t, a2_c, y_mm, x1_set, x1_t, x1_c, wh_mm, wh_set,
         x1_stored, wh_stored, xc_used, h0_used, steps, a1_var, a2_var, y_var, y_set, x1_var, x1_fac,
         parts_set, pool_steps) = [sem(f"s_{n}") for n in (
            "xa_in xc_in edge_set edge_t edge_c e_mm h_set h_t h_c a1_mm a1_out a1_set a1_n a1_t a1_c "
            "a2_mm a2_out a2_set a2_n a2_t a2_c y_mm x1_set x1_t x1_c wh_mm wh_set x1_stored "
            "wh_stored xc_used h0_used dve_steps a1_var a2_var y_var y_set x1_var x1_fac parts_set pool_steps").split()]

        def pipeline(eng, body, chain=None, last=NODE_TILES):
            for i in range(STEPS - 1):
                body(i)
            if chain:
                chain.enter()
            with eng.Fori(STEPS - 1, last) as i:
                i = eng.snap(i, min_val=STEPS - 1, max_val=last - 1)
                if chain:
                    chain.begin()
                body(i)
                if chain:
                    chain.end()
            if chain:
                chain.leave(last - STEPS + 1)
            for i in range(last, NODE_TILES + STEPS - 1):
                body(i)

        def runs(i, lag):
            return not isinstance(i, int) or 0 <= i - lag < NODE_TILES

        def past(i, n=0):
            return not isinstance(i, int) or i - n > 0

        def rows(dram, i):
            return dram[bass.ds(i * P, P), :]

        block = own.enter_context(nc.Block())

        @block.sync
        def _(sp):
            def body(i):
                if runs(i, 0):
                    if past(i):
                        sp.wait_ge(h0_used, i)
                    sp.dma_start(xa, rows(e["x"], i)).then_inc(xa_in, 16)
                if runs(i, 2):
                    if past(i, 2):
                        sp.wait_ge(xc_used, i - 2)
                    sp.dma_start(xc, rows(e["x"], i - 2)).then_inc(xc_in, 16)
                    sp.wait_ge(x1_set, i - 1)
                    sp.dma_start(rows(e["x1_dram"], i - 2), x1).then_inc(x1_stored, 16)
                if runs(i, 3):
                    sp.wait_ge(parts_set, i - 2)
                    sp.dma_start(rows(e["table"], i - 3), wh_row).then_inc(wh_stored, 16)

            pipeline(sp, body)
            sp.wait_ge(x1_stored, 16 * NODE_TILES)
            sp.wait_ge(wh_stored, 16 * NODE_TILES)

        @block.gpsimd
        def _(pool):
            g, chain = nc.gpsimd, Chain(pool, pool_steps)

            def edges(i):
                if past(i):
                    pool.wait_ge(edge_t, i)
                    pool.wait_ge(h0_used, i)
                g.tensor_tensor(edge_sum, sum0[:, bass.ds(i, 1), D:].rearrange("p a f -> p (a f)"),
                                e["self_row"][:, :], ALU.add).then_inc(edge_set, 1)

            def factors(i, aggregated, mv, done):
                pool.wait_ge(aggregated, i)
                norm_factors(g, chain, mv, e["powers"]).then_inc(done, 1)

            def parts(i):
                no_change = e["powers"][:, 3:4].to_broadcast([P, HEADS])
                pool.wait_ge(wh_set, i - 2)
                chain.step(g.tensor_tensor(wh_parts[:, 0:HEADS], wh_scores, no_change, ALU.add))
                chain.step(g.tensor_tensor(rest, wh_scores, wh_parts[:, 0:HEADS], ALU.subtract))
                chain.step(g.tensor_tensor(wh_parts[:, HEADS:2 * HEADS], rest, no_change, ALU.add))
                g.tensor_tensor(wh_parts[:, 2 * HEADS:], rest, wh_parts[:, HEADS:2 * HEADS],
                                ALU.subtract).then_inc(parts_set, 1)

            def body(i):
                if runs(i, 1):
                    factors(i, a2_var, mv2, a2_set)
                if runs(i, 0):
                    factors(i + 1, a1_var, mv1, a1_set)
                if runs(i, 2):
                    factors(i - 1, y_var, mvx, y_set)
                    factors(i - 1, x1_var, mvx, x1_fac)
                if runs(i, -1):
                    edges(i + 1)
                if runs(i, 3):
                    parts(i)

            edges(0)
            pipeline(pool, body, chain, last=NODE_TILES - 1)

        @block.tensor
        def _(pe):
            t = nc.tensor
            ident = e["ident"]

            def body(i):
                if runs(i, 1):
                    pe.wait_ge(a1_n, i)
                    if past(i, 2):
                        pe.wait_ge(a2_c, i - 2)
                    for k in range(KH):
                        mm = t.transpose(ps_n[:, k, :], a1[:, k * P:(k + 1) * P], ident[:, :])
                    mm.then_inc(a1_t, 1)
                if runs(i, 0):
                    pe.wait_ge(edge_set, i + 1)
                    if past(i):
                        pe.wait_ge(h_c, i)
                    for k in range(KD):
                        mm = t.transpose(ps_e[:, 0, k * P:(k + 1) * P], edge_sum[:, k * P:(k + 1) * P], ident[:, :])
                    mm.then_inc(edge_t, 1)
                    pe.wait_ge(edge_c, i + 1)
                    for k in range(KD):
                        mm = t.matmul(ps_e[:, 1, :], edge_sumT[:, k, :], e["ee_w2s"][:, k, :],
                                      start=(k == 0), stop=(k == KD - 1))
                    mm.then_inc(e_mm, 1)
                if runs(i, 1):
                    pe.wait_ge(a1_c, i)
                    if past(i, 1):
                        pe.wait_ge(a1_out, i)
                    for n in range(2):
                        for k in range(KH):
                            mm = t.matmul(ps_w[:, n, :], a1T[:, k, :], e["w2s"][:, k, n * 512:(n + 1) * 512],
                                          start=(k == 0), stop=(k == KH - 1))
                    mm.then_inc(a2_mm, 1)
                if runs(i, 2):
                    pe.wait_ge(a2_n, i - 1)
                    pe.wait_ge(a1_c, min(i, NODE_TILES) if isinstance(i, int) else i)
                    for k in range(KH):
                        mm = t.transpose(ps_n[:, k, :], a2[:, k * P:(k + 1) * P], ident[:, :])
                    mm.then_inc(a2_t, 1)
                if runs(i, 0):
                    pe.wait_ge(h_set, i + 1)
                    for k in range(KD):
                        mm = t.transpose(ps_e[:, 0, k * P:(k + 1) * P], h0[:, k * P:(k + 1) * P], ident[:, :])
                    mm.then_inc(h_t, 1)
                if runs(i, 3):
                    pe.wait_ge(x1_set, i - 2)
                    if past(i, 3):
                        pe.wait_ge(wh_set, i - 3)
                    for k in range(KD):
                        mm = t.transpose(ps_x[:, 0, k * P:(k + 1) * P], x1[:, k * P:(k + 1) * P], ident[:, :])
                    mm.then_inc(x1_t, 1)
                if runs(i, 0):
                    pe.wait_ge(h_c, i + 1)
                    if past(i):
                        pe.wait_ge(a2_out, i)
                    for n in range(2):
                        for k in range(KD):
                            mm = t.matmul(ps_w[:, n, :], hT[:, k, :], e["w1s"][:, k, n * 512:(n + 1) * 512],
                                          start=(k == 0), stop=(k == KD - 1))
                    mm.then_inc(a1_mm, 1)
                if runs(i, 2):
                    pe.wait_ge(a2_c, i - 1)
                    if past(i, 2):
                        pe.wait_ge(x1_set, i - 2)
                    for k in range(KH):
                        mm = t.matmul(ps_y[:, :], a2T[:, k, :], e["w3s"][:, k, :],
                                      start=(k == 0), stop=(k == KH - 1))
                    mm.then_inc(y_mm, 1)
                if runs(i, 3):
                    pe.wait_ge(x1_c, i - 2)
                    for k in range(KD):
                        mm = t.matmul(ps_x[:, 1, :], x1T[:, k, :], e["gat_w"][:, k, :],
                                      start=(k == 0), stop=(k == KD - 1))
                    mm.then_inc(wh_mm, 1)

            pipeline(pe, body)

        @block.scalar
        def _(act):
            a = nc.scalar

            def body(i):
                if runs(i, 1):
                    act.wait_ge(a1_t, i)
                    if past(i, 1):
                        act.wait_ge(a2_mm, i - 1)
                    for k in range(KH):
                        ins = a.activation(a1T[:, k, :], ps_n[:, k, :], ACT.Relu, bias=e["be1s"][:, k:k + 1],
                                           scale=e["g1s"][:, k:k + 1])
                    ins.then_inc(a1_c, 1)
                if runs(i, 0):
                    act.wait_ge(edge_t, i + 1)
                    if past(i):
                        act.wait_ge(e_mm, i)
                    a.activation(edge_sumT.rearrange("p k n -> p (k n)"), ps_e[:, 0, :], ACT.Copy).then_inc(edge_c, 1)
                if runs(i, 2):
                    act.wait_ge(a2_t, i - 1)
                    if past(i, 2):
                        act.wait_ge(y_mm, i - 2)
                    for k in range(KH):
                        ins = a.activation(a2T[:, k, :], ps_n[:, k, :], ACT.Relu, bias=e["be2s"][:, k:k + 1],
                                           scale=e["g2s"][:, k:k + 1])
                    ins.then_inc(a2_c, 1)
                if runs(i, 0):
                    act.wait_ge(h_t, i + 1)
                    if past(i):
                        act.wait_ge(a1_mm, i)
                    a.activation(hT.rearrange("p k n -> p (k n)"), ps_e[:, 0, :], ACT.Copy).then_inc(h_c, 1)
                if runs(i, 3):
                    act.wait_ge(x1_t, i - 2)
                    if past(i, 3):
                        act.wait_ge(wh_mm, i - 3)
                    a.activation(x1T.rearrange("p k n -> p (k n)"), ps_x[:, 0, :], ACT.Copy).then_inc(x1_c, 1)
                if runs(i, 1):
                    act.wait_ge(a2_set, i)
                    a.activation(a2, a2, ACT.Identity, bias=mv2[:, 3:4], scale=mv2[:, 2:3]).then_inc(a2_n, 1)
                if runs(i, 0):
                    act.wait_ge(a1_set, i + 1)
                    a.activation(a1, a1, ACT.Identity, bias=mv1[:, 3:4], scale=mv1[:, 2:3]).then_inc(a1_n, 1)

            pipeline(act, body)

        @block.vector
        def _(dve):
            v, chain = nc.vector, Chain(dve, steps)

            def wide(i, mm, bias, a, st, mv, turned, read, aggregated):
                dve.wait_ge(mm, i)
                if past(i, 1):
                    dve.wait_ge(turned, i - 1)
                ins = v.tensor_tensor(a.rearrange("p (n f) -> p n f", n=2), ps_w[:, :, :],
                                      bias.rearrange("p (n f) -> p n f", n=2), ALU.add)
                ins.then_inc(read, 1)
                dve.wait_ge(read, i)
                for n in range(2):
                    ins = v.bn_stats(st[:, n, :], a[:, n * 512:(n + 1) * 512])
                chain.step(ins)
                v.memset(idle, 0.0)
                v.bn_aggr(mv[:, 0:2], st.rearrange("p a b -> p (a b)")).then_inc(aggregated, 1)

            def narrow(i, out, in_, aggregated, factors):
                chain.step(v.bn_stats(st1x, in_))
                v.memset(idle, 0.0)
                v.bn_aggr(mvx[:, 0:2], st1x).then_inc(aggregated, 1)
                dve.wait_ge(factors, i)
                return v.tensor_scalar(out, in_, mvx[:, 2:3], mvx[:, 3:4], ALU.mult, ALU.add)

            st1x, idle = take(arena, at, [6]), take(arena, at, [1])

            def body(i):
                if runs(i, 0):
                    dve.wait_ge(edge_set, i + 1)
                    dve.wait_ge(xa_in, (i + 1) * 16)
                    if past(i):
                        dve.wait_ge(h_t, i)
                    chain.step(v.scalar_tensor_tensor(h0, xa, e["eps2"][:, 0:1],
                                                      sum0[:, bass.ds(i, 1), 0:D].rearrange("p a f -> p (a f)"),
                                                      ALU.mult, ALU.add))
                    ins = v.scalar_tensor_tensor(h0, e["ee_b2_all"][:, :], edge_sum[:, EMB:EMB + 1], h0,
                                                 ALU.mult, ALU.add)
                    ins.then_inc(h0_used, 1)
                    dve.wait_ge(h0_used, i + 1)
                    dve.wait_ge(e_mm, i + 1)
                    v.tensor_tensor(h0, ps_e[:, 1, :], h0, ALU.add).then_inc(h_set, 1)
                if runs(i, 1):
                    wide(i, a2_mm, e["b2_all"][:, :], a2, st2, mv2, a2_t, a2_out, a2_var)
                if runs(i, 0):
                    wide(i + 1, a1_mm, e["b1_all"][:, :], a1, st1, mv1, a1_t, a1_out, a1_var)
                if runs(i, 2):
                    dve.wait_ge(y_mm, i - 1)
                    chain.step(v.tensor_tensor(y, ps_y[:, :], e["b3_all"][:, :], ALU.add))
                    dve.wait_ge(xc_in, (i - 1) * 16)
                    chain.step(v.tensor_tensor(y, y, xc, ALU.add))
                    chain.step(narrow(i - 1, y, y, y_var, y_set))
                    chain.step(v.tensor_tensor(y, y, e["bn_g_all"][:, :], ALU.mult))
                    chain.step(v.tensor_tensor(y, y, e["bn_b_all"][:, :], ALU.add))
                    ins = v.scalar_tensor_tensor(y, y, 0.0, xc, ALU.max, ALU.add)
                    ins.then_inc(xc_used, 1)
                    dve.wait_ge(xc_used, i - 1)
                    if past(i, 2):
                        dve.wait_ge(x1_t, i - 2)
                        dve.wait_ge(x1_stored, (i - 2) * 16)
                    narrow(i - 1, x1, y, x1_var, x1_fac).then_inc(x1_set, 1)
                if runs(i, 3):
                    dve.wait_ge(wh_mm, i - 2)
                    if past(i, 3):
                        dve.wait_ge(wh_stored, (i - 3) * 16)
                    v.tensor_copy(wh[:, :, 0:C], ps_x[:, 1, :].rearrange("p (h c) -> p h c", h=HEADS))
                    chain.step(v.tensor_tensor(prod, ps_x[:, 1, :], e["att_d"][:, :], ALU.mult))
                    chain.step(v.tensor_reduce(e["score_dst"][:, bass.ds(i - 3, 1), :],
                                               prod.rearrange("p (o h c) -> p o h c", o=1, h=HEADS), AX.X, ALU.add))
                    chain.step(v.tensor_tensor(prod, ps_x[:, 1, :], e["att_s"][:, :], ALU.mult))
                    v.tensor_reduce(wh[:, :, C:GROW], prod.rearrange("p (h c) -> p h c", h=HEADS), AX.X,
                                    ALU.add).then_inc(wh_set, 1)

            pipeline(dve, body, chain)


def attention(nc, env):
    e, phase_sem = env, env["phase_sem"]
    take, sums, sum1, plan = e["take"], e["sums"], e["sum1"], e["plan"]
    src_cols, dst_cols, ident = e["src_cols"], e["dst_cols"], e["ident"]
    with ExitStack() as own:
        def many(name, n=AHEAD):
            return [phase_sem(f"{name}{i}") for i in range(n)]

        def ps(name, shape, dt=F32):
            return own.enter_context(nc.psum_tensor(name, shape, dt))

        at = [e["SPARE"]]
        rows = take(sums, at, [AHEAD * GROUP * TABLE])
        rows_by_slot = rows.rearrange("p (t c) -> p t c", c=TABLE)
        whg = rows_by_slot[:, :, 0:HEADS * GROW].rearrange("p t (h c) -> p t h c", h=HEADS)
        parts = rows.bitcast(BF16).rearrange("p (t c) -> p t c", c=2 * TABLE)[:, :, 2 * HEADS * GROW:]
        hits = take(sums, at, [AHEAD * GROUP, P])
        hitsT = take(sums, at, [2 * GROUP, P])
        assert at[0] <= sums.shape[1]
        at = [0]
        miss = take(e["arena"], at, [GROUP * P]).bitcast(BF16).rearrange("p (g n) -> p g n", n=P)
        rel = take(e["arena"], at, [AHEAD, GROUP])
        ones = take(e["arena"], at, [GROUP * HEADS * P // 2]).bitcast(BF16).rearrange("p (g n) -> p g n", n=P)
        minus_big = take(e["arena"], at, [P // 2]).bitcast(BF16)
        flat = take(e["arena"], at, [P]).bitcast(BF16).rearrange("p (g n) -> p g n", n=P)
        partsT = take(e["arena"], at, [P]).bitcast(BF16).rearrange("p (g n) -> p g n", n=P)
        where = take(e["arena"], at, [GROUP, HEADS])
        idle = take(e["arena"], at, [1])
        tile_top = take(e["arena"], at, [GROUP, HEADS])
        top, zt = take(e["arena"], at, [HEADS]), take(e["arena"], at, [HEADS])
        node_z = take(e["arena"], at, [2, 2 * HEADS])
        fall, shrink = take(e["arena"], at, [2, HEADS]), take(e["arena"], at, [2, HEADS])
        ze, zp = take(e["arena"], at, [GROUP, HEADS]), take(e["arena"], at, [2 * GROUP, HEADS])
        idx = [own.enter_context(nc.sbuf_tensor(f"gidx{u}", [P, GROUP], I32)) for u in range(AHEAD)]
        ps_top = [ps(f"ps_top{i}", [P, HEADS, P]) for i in range(BANKS)]
        ps_parts = ps("ps_parts", [P, P], BF16)
        ps_miss = ps("ps_miss", [P, GROUP, P], BF16)
        ps_node = ps("ps_node", [P, GROUP, 2 * HEADS])
        ps_sum = [ps(f"ps_att{i}", [P, HEADS, GROW]) for i in range(2)]
        whg_in = many("whg_in", AHEAD * GROUP)
        top_mm, top_read = many("g_topmm", AHEAD * GROUP), many("g_topread", AHEAD * GROUP)
        (rel_set, idx_set, miss_set, hits_set, turned, parts_turned, flat_set, partsT_set, hitsT_set, node_set,
         fall_set, shrink_set, node_mm, zp_set, p_set, half_weighed, weighed, half_mm, att_mm, att_out) = [many(n) for n in (
            "g_rel g_idx g_miss g_hits g_turned g_pturned g_flat g_partsT g_hitsT g_node g_fall g_shrink "
            "g_nodemm g_zp g_p g_hweighed g_weighed g_halfmm g_attmm g_attout").split()]
        ident_bf = e["ident_bf"]
        ones_set = phase_sem("g_ones")
        HALF = GROUP // 2
        PART_ROWS = GROUP * PARTS * HEADS
        steps = phase_sem("g_steps")
        block = own.enter_context(nc.Block())

        def slot(p, n=AHEAD):
            return slice(GROUP * (p % n), GROUP * (p % n) + GROUP)

        @block.gpsimd
        def _(pool):
            g = nc.gpsimd
            for s in rel_set + idx_set:
                pool.sem_inc(s, 1)
            rounds, walk = Rounds(pool, plan, "whg", GROUP), Walk(pool, plan, "whg", GROUP)

            def prepare(p):
                u = p % AHEAD
                rounds.seen(miss_set, p - AHEAD)
                rounds.seen(half_mm, p - AHEAD)
                tile, node = walk.place()
                g.tensor_copy(idx[u][:, :], src_cols[:, bass.ds(tile, GROUP)]).then_inc(idx_set[u], 1)
                g.tensor_tensor(rel[:, u, :], dst_cols[:, bass.ds(tile, GROUP)],
                                e["node_base"][:, bass.ds(node, 1), :].rearrange("p a b -> p (a b)"),
                                ALU.subtract).then_inc(rel_set[u], 1)
                rounds.seen(idx_set, p)
                walk.advance()
                for k in range(GROUP):
                    if k == HALF:
                        rounds.seen(att_mm, p - AHEAD)
                        g.tensor_tensor(idle, idle, idle, ALU.subtract)
                    g.indirect_dma_start(rows_by_slot[:, GROUP * u + k, :], None,
                                         e["table"], bass.IndirectOffsetOnAxis(ap=idx[u][:, k:k + 1], axis=0)
                                         ).then_inc(whg_in[GROUP * u + k], 16)

            for p in range(AHEAD):
                prepare(p)
            with pool.Fori(0, rounds.trips):
                rounds.begin()
                for u in range(AHEAD):
                    prepare(u + AHEAD)
                rounds.end()
            for n in range(AHEAD * GROUP):
                pool.wait_ge(whg_in[n], pool.snap(rounds.trips * 16) + 16)

        @block.scalar
        def _(act):
            a = nc.scalar
            for s in hits_set + hitsT_set + shrink_set + p_set + half_weighed + weighed + flat_set + partsT_set:
                act.sem_inc(s, 1)
            rounds = Rounds(act, plan, "weigh", GROUP)

            def hit(p):
                s = p % AHEAD
                rounds.seen(miss_set, p)
                rounds.seen(att_mm, p - AHEAD)
                a.activation(hits[:, slot(p), :], miss[:, slot(p, 2), :], ACT.Copy, bias=1.0,
                             scale=-1.0).then_inc(hits_set[s], 1)
                rounds.seen(turned, p)
                rounds.seen(node_mm, p - 2)
                a.activation(hitsT[:, slot(p, 2), :], ps_miss[:, :, :], ACT.Copy, bias=1.0,
                             scale=-1.0).then_inc(hitsT_set[s], 1)

            def flatten(p):
                for k in range(GROUP):
                    rounds.landed(whg_in, p, k)
                rounds.seen(parts_turned, p - 2)
                a.activation(flat[:, p % 2, 0:PART_ROWS].rearrange("p (k c) -> p k c", k=GROUP),
                             parts[:, slot(p), :], ACT.Copy).then_inc(flat_set[p % AHEAD], 1)

            def turned_parts(p):
                rounds.seen(parts_turned, p)
                rounds.seen(top_mm, p - 2, GROUP - 1)
                a.activation(partsT[0:PART_ROWS, p % 2, :], ps_parts[0:PART_ROWS, :], ACT.Copy).then_inc(
                    partsT_set[p % AHEAD], 1)

            def shrinks(p):
                rounds.seen(fall_set, p)
                rounds.seen(att_out, p - 2)
                a.activation(shrink[:, p % 2, :], fall[:, p % 2, :], ACT.Exp).then_inc(shrink_set[p % AHEAD], 1)

            def weights(p):
                rounds.seen(zp_set, p)
                a.activation(whg[:, slot(p), :, C:GROW].rearrange("p k h c -> p k (h c)"),
                             zp[:, slot(p, 2), :], ACT.Exp).then_inc(p_set[p % AHEAD], 1)

            def weigh(p, first, behind):
                if p < 0:
                    return
                if first == 0:
                    rounds.seen(p_set, p)
                for k in range(first, behind):
                    for h in range(HEADS):
                        row = whg[:, GROUP * (p % AHEAD) + k, h, :]
                        ins = a.activation(row[:, 0:C], row[:, 0:C], ACT.Copy, scale=row[:, C:GROW])
                    if k == HALF - 1:
                        ins.then_inc(half_weighed[p % AHEAD], 1)
                    if k == GROUP - 1:
                        ins.then_inc(weighed[p % AHEAD], 1)

            def part(p):
                if p >= 1:
                    weights(p - 1)
                    shrinks(p - 1)
                weigh(p - 1, 0, HALF)
                flatten(p + 1)
                weigh(p - 1, HALF, GROUP - 1)
                turned_parts(p + 1)
                weigh(p - 1, GROUP - 1, GROUP)
                hit(p + 1)

            flatten(0)
            hit(0)
            turned_parts(0)
            part(0)
            part(1)
            with act.Fori(0, rounds.trips):
                rounds.begin()
                for u in range(AHEAD):
                    part(u + 2)
                rounds.end()

        @block.tensor
        def _(pe):
            t = nc.tensor
            for s in turned + parts_turned + top_mm + node_mm + half_mm + att_mm:
                pe.sem_inc(s, 1)
            rounds = Rounds(pe, plan, "att", GROUP)

            def nodes(p):
                rounds.seen(node_set, p)
                rounds.seen(hitsT_set, p)
                rounds.seen(zp_set, p - 1)
                for k in range(GROUP):
                    mm = t.matmul(ps_node[:, k, :], hitsT[:, GROUP * (p % 2) + k, :], node_z[:, p % 2, :],
                                  start=True, stop=True)
                mm.then_inc(node_mm[p % AHEAD], 1)

            def turn_misses(p):
                rounds.seen(miss_set, p)
                rounds.seen(hitsT_set, p - 1)
                for k in range(GROUP):
                    mm = t.transpose(ps_miss[:, k, :], miss[:, GROUP * (p % 2) + k, :], ident_bf[:, :])
                mm.then_inc(turned[p % AHEAD], 1)

            def turn_parts(p):
                rounds.seen(flat_set, p)
                rounds.seen(partsT_set, p - 1)
                t.transpose(ps_parts[0:PART_ROWS, :], flat[:, p % 2, 0:PART_ROWS], ident_bf[:, :]).then_inc(
                    parts_turned[p % AHEAD], 1)

            def spread(p, k):
                if k == 0:
                    rounds.seen(partsT_set, p)
                    rounds.seen(miss_set, p)
                rounds.seen(top_read, p if k >= BANKS else p - 1, (k - BANKS) % GROUP)
                to = ps_top[k % BANKS]
                t.matmul(to[:, :, :], miss[:, GROUP * (p % 2) + k, :], minus_big.rearrange(
                    "p (o n) -> p o n", o=1).to_broadcast([P, HEADS, P]), start=True, stop=False)
                for h in range(HEADS):
                    mm = t.matmul(to[:, h, :], ones[0:PART_ROWS, HEADS * k + h, :], partsT[0:PART_ROWS, p % 2, :],
                                  start=False, stop=(h == HEADS - 1))
                mm.then_inc(top_mm[GROUP * (p % AHEAD) + k], 1)

            def add_up(p, k):
                if k == HALF:
                    rounds.seen(weighed, p)
                if k == 0:
                    rounds.seen(half_weighed, p)
                    rounds.seen(hits_set, p)
                    rounds.seen(att_out, p - 2)
                at = GROUP * (p % AHEAD) + k
                mm = t.matmul(ps_sum[p % 2][:, :, :], hits[:, at, :], whg[:, at, :, :],
                              start=(k == 0), stop=(k == GROUP - 1))
                if k == HALF - 1:
                    mm.then_inc(half_mm[p % AHEAD], 1)
                if k == GROUP - 1:
                    mm.then_inc(att_mm[p % AHEAD], 1)

            def part(p):
                if p >= 1:
                    nodes(p - 1)
                for k in range(GROUP):
                    spread(p, k)
                    if p >= 2 and BANKS - 1 <= k < GROUP - 1:
                        add_up(p - 2, HALF + k - BANKS + 1)
                turn_misses(p + 1)
                turn_parts(p + 1)
                if p >= 1:
                    for k in range(HALF):
                        add_up(p - 1, k)

            turn_misses(0)
            turn_parts(0)
            pe.wait_ge(ones_set, 1)
            part(0)
            part(1)
            with pe.Fori(0, rounds.trips):
                rounds.begin()
                for u in range(AHEAD):
                    part(u + 2)
                rounds.end()

        @block.vector
        def _(dve):
            v, chain = nc.vector, Chain(dve, steps)
            for s in miss_set + top_read + node_set + fall_set + zp_set + att_out:
                dve.sem_inc(s, 1)
            v.memset(sum1, 0.0)
            v.tensor_scalar(minus_big, ident_bf[:, :], -BIG, None, ALU.mult)
            chain.step(v.tensor_reduce(where, ident[:, 0:PART_ROWS].rearrange(
                "p (k r h) -> p k h r", r=PARTS, h=HEADS), AX.X, ALU.add))
            v.tensor_copy(ones, where.rearrange("p k h -> p (k h)").rearrange("p (n o) -> p n o", o=1).to_broadcast(
                [P, GROUP * HEADS, P])).then_inc(ones_set, 1)
            dve.wait_ge(ones_set, 1)
            rounds = Rounds(dve, plan, "top", GROUP)
            walk = Walk(dve, plan, "top", GROUP)
            nodes = [dve.alloc_register(f"node_{n}") for n in range(3)]
            for n in range(3):
                dve.reg_mov(nodes[n], 0)
            iota_row = e["iota_row"]

            def state(tensor, node):
                return tensor[:, bass.ds(node, 1), :].rearrange("p a h -> p (a h)")

            def misses(p):
                rounds.seen(rel_set, p)
                rounds.seen(turned, p - 2)
                rounds.seen(hits_set, p - 2)
                rounds.seen(top_mm, p - 2, GROUP - 1)
                v.tensor_tensor(miss[:, slot(p, 2), :],
                                iota_row[:, :].rearrange("p (o n) -> p o n", o=1).to_broadcast([P, GROUP, P]),
                                rel[:, p % AHEAD, :].rearrange("p (g o) -> p g o", o=1).to_broadcast([P, GROUP, P]),
                                ALU.not_equal).then_inc(miss_set[p % AHEAD], 1)

            def tops(p):
                q, s = p % 2, p % AHEAD
                for k in range(GROUP):
                    rounds.seen(top_mm, p, k)
                    v.tensor_reduce(tile_top[:, k, :], ps_top[k % BANKS][:, :, :], AX.X, ALU.max).then_inc(
                        top_read[GROUP * s + k], 1)
                _, node = walk.place()
                dve.reg_mov(nodes[2], nodes[1])
                dve.reg_mov(nodes[1], nodes[0])
                dve.reg_mov(nodes[0], walk.node)
                to_sum = dve.snap(nodes[2], min_val=0, max_val=NODE_TILES)
                walk.advance()
                score, z = state(e["score_dst"], node), state(e["z_max"], node)
                rounds.seen(node_mm, p - 2)
                v.tensor_tensor(node_z[:, q, HEADS:], score, score, ALU.max)
                rounds.seen(top_read, p, GROUP - 1)
                chain.step(v.tensor_reduce(top, tile_top.rearrange("p k h -> p h k"), AX.X, ALU.max))
                chain.step(v.tensor_tensor(top, top, score, ALU.add))
                chain.step(v.scalar_tensor_tensor(zt, top, SLOPE, top, ALU.mult, ALU.max))
                v.tensor_tensor(node_z[:, q, 0:HEADS], z, zt, ALU.max).then_inc(node_set[s], 1)
                rounds.seen(node_set, p)
                rounds.seen(shrink_set, p - 2)
                v.tensor_tensor(fall[:, q, :], z, node_z[:, q, 0:HEADS], ALU.subtract).then_inc(fall_set[s], 1)
                rounds.seen(fall_set, p)
                chain.step(v.tensor_tensor(z, z, node_z[:, q, 0:HEADS], ALU.max))
                return to_sum

            def exponents(p):
                rounds.seen(node_mm, p)
                chain.step(v.tensor_tensor(ze, whg[:, slot(p), :, C:GROW].rearrange("p k h c -> p k (h c)"),
                                           ps_node[:, :, HEADS:], ALU.add))
                chain.step(v.scalar_tensor_tensor(ze, ze, SLOPE, ze, ALU.mult, ALU.max))
                chain.step(v.tensor_tensor(ze, ze, ps_node[:, :, 0:HEADS], ALU.subtract))
                rounds.seen(p_set, p - 2)
                v.tensor_scalar(zp[:, slot(p, 2), :], ze, 0.0, None, ALU.min).then_inc(zp_set[p % AHEAD], 1)

            def accumulate(p, node):
                rounds.seen(att_mm, p)
                rounds.seen(shrink_set, p)
                rounds.seen(att_out, p - 1)
                to = sum1[:, bass.ds(node, 1), :].rearrange("p a (h c) -> p (a h) c", h=HEADS)
                for h in range(HEADS):
                    ins = v.scalar_tensor_tensor(to[:, h, :], to[:, h, :], shrink[:, p % 2, h:h + 1],
                                                 ps_sum[p % 2][:, h, :], ALU.mult, ALU.add)
                ins.then_inc(att_out[p % AHEAD], 1)

            def part(p):
                if p >= 1:
                    exponents(p - 1)
                node = tops(p)
                misses(p + 2)
                if p >= 2:
                    accumulate(p - 2, node)

            misses(0)
            misses(1)
            part(0)
            part(1)
            chain.enter()
            with dve.Fori(0, rounds.trips):
                rounds.begin()
                chain.begin()
                for u in range(AHEAD):
                    part(u + 2)
                chain.end()
                rounds.end()


def output_norm(nc, env):
    e, phase_sem, take, sum1 = env, env["phase_sem"], env["take"], env["sum1"]
    with ExitStack() as own:
        def sem(name):
            return phase_sem(name)

        at = [0]
        arena = e["arena"]
        x1 = take(arena, at, [2, D])
        den = take(arena, at, [HEADS])
        low, high = take(arena, at, [2, D]), take(arena, at, [2, D])
        res, st, mv = take(arena, at, [2, D]), take(arena, at, [6]), take(arena, at, [2, 4])
        idle = take(arena, at, [1])
        x1_in = [sem("x1_in0"), sem("x1_in1")]
        stored = [sem("stored0"), sem("stored1")]
        low_set, exp_set, var_set, res_set, normed, steps, pool_steps = [
            sem(f"f_{n}") for n in "low exp var res normed steps pool_steps".split()]
        out, x1_dram = e["out"], e["x1_dram"]
        PAIRS = -(-NODE_TILES // 2)
        block = own.enter_context(nc.Block())

        @block.sync
        def _(sp):
            def load(i, q):
                sp.dma_start(x1[:, q, :], x1_dram[bass.ds(i * P, P), :]).then_inc(x1_in[q], 16)

            def store(i, q):
                sp.wait_ge(normed, i + 1)
                sp.dma_start(out[bass.ds(i * P, P), :], res[:, q, :]).then_inc(stored[q], 16)

            load(0, 0)
            load(1, 1)
            with sp.Fori(0, NODE_TILES // 2 - 1) as j:
                j = sp.snap(j, min_val=0, max_val=NODE_TILES // 2 - 2)
                for q in range(2):
                    store(2 * j + q, q)
                    load(2 * j + 2 + q, q)
            store(NODE_TILES - 3, 0)
            load(NODE_TILES - 1, 0)
            store(NODE_TILES - 2, 1)
            store(NODE_TILES - 1, 0)
            sp.wait_ge(stored[0], 16 * PAIRS)
            sp.wait_ge(stored[1], 16 * (NODE_TILES - PAIRS))

        def halves(eng, body, chain=None):
            for q in range(2):
                body(q, q, 0)
            if chain:
                chain.enter()
            with eng.Fori(1, NODE_TILES // 2) as j:
                j = eng.snap(j, min_val=1, max_val=NODE_TILES // 2 - 1)
                if chain:
                    chain.begin()
                for q in range(2):
                    body(2 * j + q, q, j)
                if chain:
                    chain.end()
            if chain:
                chain.leave(NODE_TILES // 2 - 1)
            body(NODE_TILES - 1, 0, NODE_TILES // 2)

        @block.gpsimd
        def _(pool):
            g, chain = nc.gpsimd, Chain(pool, pool_steps)

            def body(i, q, j):
                pool.wait_ge(var_set, i + 1)
                norm_factors(g, chain, mv[:, q, :], e["powers"]).then_inc(res_set, 1)

            halves(pool, body, chain)

        @block.scalar
        def _(act):
            def body(i, q, j):
                act.wait_ge(low_set, i + 1)
                nc.scalar.activation(low[:, q, :], low[:, q, :], ACT.Exp).then_inc(exp_set, 1)
                act.wait_ge(res_set, i + 1)
                nc.scalar.activation(res[:, q, :], res[:, q, :], ACT.Identity, bias=mv[:, q, 3:4],
                                     scale=mv[:, q, 2:3]).then_inc(normed, 1)

            halves(act, body)

        @block.vector
        def _(dve):
            v, chain = nc.vector, Chain(dve, steps)

            def body(i, q, j):
                s = sum1[:, bass.ds(i, 1), :].rearrange("p a (h c) -> p (a h) c", h=HEADS)
                chain.step(v.tensor_scalar(den, s[:, :, C:GROW].rearrange("p h c -> p (h c)"), DEN_EPS, None,
                                           ALU.add))
                chain.step(v.reciprocal(den, den))
                hq = high[:, q, :].rearrange("p (h c) -> p h c", h=HEADS)
                chain.step(v.tensor_tensor(hq, s[:, :, 0:C], den.rearrange("p (h c) -> p h c", c=1).to_broadcast(
                    [P, HEADS, C]), ALU.mult))
                v.tensor_scalar(low[:, q, :], high[:, q, :], 0.0, None, ALU.min).then_inc(low_set, 1)
                dve.wait_ge(x1_in[q], (j + 1) * 16)
                if not isinstance(i, int) or i >= 2:
                    dve.wait_ge(stored[q], j * 16)
                chain.step(v.scalar_tensor_tensor(res[:, q, :], high[:, q, :], 0.0, x1[:, q, :], ALU.max, ALU.add))
                dve.wait_ge(exp_set, i + 1)
                chain.step(v.scalar_tensor_tensor(res[:, q, :], low[:, q, :], -1.0, res[:, q, :], ALU.add, ALU.add))
                chain.step(v.bn_stats(st, res[:, q, :]))
                v.memset(idle, 0.0)
                v.bn_aggr(mv[:, q, 0:2], st).then_inc(var_set, 1)

            halves(dve, body, chain)


def kernel(**inputs):
    import numpy as np
    import concourse.bacc as bacc
    from concourse.bass_utils import run_bass_kernel_spmd

    a = {k: np.asarray(v) for k, v in inputs.items()}
    L0 = {k[len("L0_gnn_"):]: v for k, v in a.items() if k.startswith("L0_gnn_")}

    def padded(v, n, fill):
        out = np.full((n, *v.shape[1:]), fill, v.dtype)
        out[:len(v)] = v
        return out

    dst = padded(a["dst"], ALL_TILES * P, -1)
    arrays = {
        "x": padded(a["x"], NODE_TILES * P, 0),
        "srcT": padded(a["src"], ALL_TILES * P, 0).reshape(ALL_TILES, P).T,
        "dstT": dst.reshape(ALL_TILES, P).T,
        "dst_rows": padded(a["dst"], TILE_ROWS * P * P, -1).reshape(TILE_ROWS, P, P).transpose(1, 0, 2),
        "eaT": padded(a["edge_attr_64"], ALL_TILES * P, 0).T,
        "eps": L0["eps"].reshape(1),
        "ee_w1": L0["ee_w1"], "ee_b1": L0["ee_b1"], "ee_w2": L0["ee_w2"], "ee_b2": L0["ee_b2"],
        "w1": L0["w1"], "b1": L0["b1"],
        "g1T": L0["g1"].reshape(-1, P).T, "be1T": L0["be1"].reshape(-1, P).T,
        "w2": L0["w2"], "b2": L0["b2"],
        "g2T": L0["g2"].reshape(-1, P).T, "be2T": L0["be2"].reshape(-1, P).T,
        "w3": L0["w3"], "b3": L0["b3"], "bn_g": L0["bn_g"], "bn_b": L0["bn_b"],
        "gat_wT": a["L1_gnn_W"].T,
        "att_src": a["L1_gnn_att"][:, :C].reshape(-1), "att_dst": a["L1_gnn_att"][:, C:].reshape(-1),
    }
    nc = bacc.Bacc("TRN2", target_bir_lowering=False, num_devices=1)
    args, fed = [], {}
    for name, v in arrays.items():
        v = np.ascontiguousarray(v)
        fed[f"in_{name}"] = v
        args.append(nc.dram_tensor(f"in_{name}", v.shape, mybir.dt.from_np(v.dtype), kind="ExternalInput").ap())
    out = nc.dram_tensor("out_rows", (NODE_TILES * P, D), F32, kind="ExternalOutput").ap()
    bass_gnn_resnorm(nc, *args, out)
    r = run_bass_kernel_spmd(nc, [fed], core_ids=[0])
    return r.results[0]["out_rows"][:N_NODES]
```

```python
from contextlib import ExitStack

import concourse.bass as bass
from concourse import mybir

ALU = mybir.AluOpType
ACT = mybir.ActivationFunctionType
AX = mybir.AxisListType
F32 = mybir.dt.float32
I32 = mybir.dt.int32
BF16 = mybir.dt.bfloat16
F32R = mybir.dt.float32r

P = 128
N_NODES, N_EDGES = 6250, 100000
D, EDIM, EMB, H = 256, 64, 256, 1024
HEADS, C = 4, 64
NODE_TILES = -(-N_NODES // P)
EDGE_TILES = -(-N_EDGES // P)
BATCH = 7
UNIT = 2
AHEAD = 4
GROUP = 6
PAD_TILES = 2 * AHEAD * GROUP
ALL_TILES = EDGE_TILES + PAD_TILES
B_HIGH, B_LOW = 64, 96
TILE_ROWS = -(-EDGE_TILES // P)
GROW = C + 1
PARTS = 3
TABLE = HEADS * GROW + HEADS * PARTS // 2
BIG = 2.0 ** 100
BANKS = 3
DIV_GROUP = float(65536 // GROUP + 1)
FAR = 1000.0
LN_EPS = 1e-5
SLOPE = 0.2
DEN_EPS = 1e-16
MANY = 1 << 20
COUNT_ROW = {UNIT: 1, GROUP: 3}


class Chain:

    def __init__(self, eng, sem):
        self.eng, self.sem, self.base, self.count = eng, sem, None, 0

    def note(self, ins):
        self.count += 1
        ins.then_inc(self.sem, 1)
        return self.count

    def reach(self, count):
        self.eng.wait_ge(self.sem, count if self.base is None else self.base + count)

    def step(self, ins):
        self.reach(self.note(ins))

    def enter(self):
        self.reg = self.eng.alloc_register(f"{self.sem.name}_count")
        self.eng.reg_mov(self.reg, self.count)
        self.before = self.count

    def begin(self):
        self.base, self.count = self.eng.snap(self.reg, min_val=0, max_val=MANY * 64), 0

    def end(self):
        self.eng.reg_add(self.reg, self.reg, self.count)

    def leave(self, trips):
        self.count, self.base = self.before + trips * self.count, None


class Walk:

    def __init__(self, eng, plan, name, size=UNIT):
        self.eng, self.plan, self.size = eng, plan, size
        self.row = COUNT_ROW[size]
        self.tile = eng.alloc_register(f"{name}_tile")
        self.node = eng.alloc_register(f"{name}_node")
        self.left = eng.alloc_register(f"{name}_left")
        eng.reg_mov(self.node, 0)
        eng.reg_load(self.tile, plan[0:1, 0, 0:1])
        eng.reg_load(self.left, plan[0:1, self.row, 0:1])

    def place(self):
        return (self.eng.snap(self.tile, min_val=0, max_val=ALL_TILES - self.size),
                self.eng.snap(self.node, min_val=0, max_val=NODE_TILES))

    def advance(self):
        eng = self.eng
        eng.reg_add(self.tile, self.tile, self.size)
        eng.reg_add(self.left, self.left, -1)
        with eng.If_eq(self.left, 0):
            eng.reg_add(self.node, self.node, 1)
            node = eng.snap(self.node, min_val=0, max_val=NODE_TILES)
            eng.reg_load(self.tile, self.plan[0:1, 0, bass.ds(node, 1)])
            eng.reg_load(self.left, self.plan[0:1, self.row, bass.ds(node, 1)])


class Rounds:

    def __init__(self, eng, plan, name, size=UNIT):
        self.eng, self.name, self.size = eng, name, size
        self.reg = eng.alloc_register(f"{name}_round")
        eng.reg_mov(self.reg, 1)
        self.trips = eng.value_load(plan[0:1, COUNT_ROW[size] + 1, 0:1], min_val=1, max_val=MANY)
        self.now = [1, 2, 3]

    def begin(self):
        n = self.eng.snap(self.reg, min_val=1, max_val=MANY)
        self.now = [n, self.eng.snap(n + 1), self.eng.snap(n + 2)]

    def end(self):
        self.eng.reg_add(self.reg, self.reg, 1)

    def seen(self, sems, at, k=None):
        sem = sems[at % AHEAD] if k is None else sems[self.size * (at % AHEAD) + k]
        self.eng.wait_ge(sem, self.now[1 + at // AHEAD])

    def landed(self, sems, at, k=None):
        sem = sems[at % AHEAD] if k is None else sems[self.size * (at % AHEAD) + k]
        self.eng.wait_ge(sem, self.now[at // AHEAD] * 16)


def bass_gnn_resnorm(nc, x, srcT, dstT, dst_rows, eaT, eps, ee_w1, ee_b1, ee_w2, ee_b2, w1, b1, g1T,
                     be1T, w2, b2, g2T, be2T, w3, b3, bn_g, bn_b, gat_wT, att_src, att_dst, out):
    with ExitStack() as ctx:
        def sb(name, shape, dt=F32):
            return ctx.enter_context(nc.sbuf_tensor(name, shape, dt))

        in_phase = []

        def phase_sem(name):
            in_phase.append(nc.alloc_semaphore(name))
            return in_phase[-1]

        def end_phase():
            nc.clear_and_free_semaphores(in_phase)
            nc.all_engine_barrier()
            in_phase.clear()

        table = nc.dram_tensor("wh_table", (NODE_TILES * P, TABLE), F32, kind="Internal").ap()
        x1_dram = nc.dram_tensor("x1_rows", (NODE_TILES * P, D), F32, kind="Internal").ap()

        plan = sb("plan", [1, 5, NODE_TILES + 1], I32)
        src_cols = sb("src_cols", [P, ALL_TILES], I32)
        dst_cols = sb("dst_cols", [P, ALL_TILES])
        node_base = sb("node_base", [P, NODE_TILES + 1])
        iota_row = sb("iota_row", [P, P])
        ident = sb("ident", [P, P])
        ident_bf = sb("ident_bf", [P, P], BF16)
        ee_whl = sb("ee_whl", [P, EMB], F32R)
        ee_whb = sb("ee_whb", [P, EMB], F32R)
        ee_w2s = sb("ee_w2s", [P, 2, D])
        w1s = sb("w1s", [P, D // P, H])
        w2s = sb("w2s", [P, H // P, H])
        w3s = sb("w3s", [P, H // P, D])
        gat_w = sb("gat_w", [P, D // P, D])
        g1s, be1s = sb("g1s", [P, H // P]), sb("be1s", [P, H // P])
        g2s, be2s = sb("g2s", [P, H // P]), sb("be2s", [P, H // P])
        b1_all, b2_all = sb("b1_all", [P, H]), sb("b2_all", [P, H])
        self_row = sb("self_row", [P, EMB + 1])
        ee_b2_all = sb("ee_b2_all", [P, D])
        b3_all = sb("b3_all", [P, D])
        bn_g_all, bn_b_all = sb("bn_g_all", [P, D]), sb("bn_b_all", [P, D])
        att_s, att_d = sb("att_s", [P, D]), sb("att_d", [P, D])
        eps2 = sb("eps2", [P, 1])
        powers = sb("powers", [P, 4])
        score_dst = sb("score_dst", [P, NODE_TILES + 1, HEADS])
        z_max = sb("z_max", [P, NODE_TILES + 1, HEADS])
        SUM0 = D + EMB + 1
        sums = sb("sums", [P, (NODE_TILES + 1) * SUM0])
        sum0 = sums[:, :].rearrange("p (b f) -> p b f", f=SUM0)
        SUM1 = HEADS * GROW
        sum1 = sums[:, 0:(NODE_TILES + 1) * SUM1].rearrange("p (b f) -> p b f", f=SUM1)
        SPARE = (NODE_TILES + 1) * SUM1
        ARENA = 7000

        def phase_arena(own, columns=ARENA):
            arenas.append(f"arena{len(arenas)}")
            return own.enter_context(nc.sbuf_tensor(arenas[-1], [P, columns], F32))

        arenas = []

        def take(tensor, at, shape):
            n = 1
            for s in shape:
                n *= s
            v = tensor[:, at[0]:at[0] + n]
            at[0] += n
            if len(shape) == 2:
                return v.rearrange("p (a b) -> p a b", b=shape[1])
            if len(shape) == 3:
                return v.rearrange("p (a b c) -> p a b c", b=shape[1], c=shape[2])
            return v

        planning = ExitStack()
        arena = phase_arena(planning)
        at_raw = [ARENA - 2 * EMB]
        ee_w1_raw, ee_b1_raw = take(arena, at_raw, [EMB]), take(arena, at_raw, [EMB])
        with ExitStack() as own:
            at = [0]
            dst_f = take(arena, at, [TILE_ROWS, P])
            dst_neg = take(arena, at, [TILE_ROWS, P])
            hi, lo = take(arena, at, [TILE_ROWS]), take(arena, at, [TILE_ROWS])
            tile_no, tile_back = take(arena, at, [TILE_ROWS]), take(arena, at, [TILE_ROWS])
            base_lo, base_hi = take(arena, at, [NODE_TILES]), take(arena, at, [NODE_TILES])
            above, meets = take(arena, at, [NODE_TILES]), take(arena, at, [NODE_TILES])
            ranges, ranges_all = take(arena, at, [2, NODE_TILES]), take(arena, at, [2, NODE_TILES])
            firsts, counts = take(arena, at, [NODE_TILES]), take(arena, at, [NODE_TILES])
            total, wanted = take(arena, at, [1]), take(arena, at, [NODE_TILES])
            counts_i = own.enter_context(nc.sbuf_tensor("counts_i", [1, NODE_TILES + 1], I32))
            rows_i = sums[:, ALL_TILES:ALL_TILES + TILE_ROWS * P].bitcast(I32).rearrange("p (c e) -> p c e", e=P)
            cols_i = sums[:, 0:ALL_TILES].bitcast(I32)
            plan_in, loaded, weights_in = phase_sem("plan_in"), phase_sem("loaded"), phase_sem("weights_in")
            made = phase_sem("made")
            ranged = phase_sem("ranged")
            reduced = phase_sem("reduced")
            own_steps, pool_steps = phase_sem("plan_steps"), phase_sem("const_steps")
            iota_made = phase_sem("iota_made")
            POOL_ZEROS = ALL_TILES + TILE_ROWS * P
            ACT_ZEROS = sums.shape[1] - (sums.shape[1] - POOL_ZEROS) // 2 // P * P
            block = own.enter_context(nc.Block())

            @block.scalar
            def _(act):
                act.wait_ge(iota_made, 1)
                to = sums[:, ACT_ZEROS:].rearrange("p (n e) -> p n e", e=P)
                nc.scalar.activation(to, iota_row[:, :].rearrange("p (o e) -> p o e", o=1).to_broadcast(
                    [P, to.shape[1], P]), ACT.Copy, scale=0.0)

            def every_partition(row, n):
                return row.rearrange("(o n) -> o n", o=1).to_broadcast([P, n])

            @block.sync
            def _(sp):
                sp.dma_start(rows_i[:, :, :], dst_rows).then_inc(plan_in, 16)
                sp.dma_start(cols_i, dstT).then_inc(plan_in, 16)
                sp.dma_start(src_cols[:, :], srcT).then_inc(loaded, 16)
                for q in range(2):
                    sp.dma_start(ee_w1_raw[q * EDIM:(q + 1) * EDIM, :], ee_w1).then_inc(loaded, 16)
                for row in (B_HIGH, B_LOW):
                    sp.dma_start(ee_b1_raw[row:row + 1, :], ee_b1.rearrange("(o n) -> o n", o=1)).then_inc(loaded, 16)
                sp.dma_start(self_row[:, 0:EMB], every_partition(ee_b1, EMB)).then_inc(loaded, 16)
                sp.dma_start(eps2[:, :], every_partition(eps, 1)).then_inc(loaded, 16)
                sp.wait_ge(loaded, 16 * 7)
                for to, of in [(ee_w2s, ee_w2), (w1s, w1), (w2s, w2), (w3s, w3), (gat_w, gat_wT)]:
                    sp.dma_start(to[:, :, :], of.rearrange("(k p) n -> p k n", p=P)).then_inc(weights_in, 16)
                for to, of in [(g1s, g1T), (be1s, be1T), (g2s, g2T), (be2s, be2T)]:
                    sp.dma_start(to[:, :], of).then_inc(weights_in, 16)
                for to, of in [(b1_all, b1), (b2_all, b2), (ee_b2_all, ee_b2), (b3_all, b3),
                               (bn_g_all, bn_g), (bn_b_all, bn_b), (att_s, att_src), (att_d, att_dst)]:
                    sp.dma_start(to[:, :], every_partition(of, to.shape[1])).then_inc(weights_in, 16)

            @block.gpsimd
            def _(pool):
                g = nc.gpsimd
                g.iota(tile_no, [[P, TILE_ROWS]], base=0, channel_multiplier=1,
                       allow_small_or_imprecise_dtypes=True).then_inc(made, 1)
                g.iota(base_lo, [[P, NODE_TILES]], base=0, channel_multiplier=0,
                       allow_small_or_imprecise_dtypes=True).then_inc(made, 1)
                g.iota(base_hi, [[P, NODE_TILES]], base=P - 1, channel_multiplier=0,
                       allow_small_or_imprecise_dtypes=True).then_inc(made, 1)
                g.iota(iota_row[:, :], [[1, P]], base=0, channel_multiplier=0,
                       allow_small_or_imprecise_dtypes=True).then_inc(iota_made, 1)
                g.iota(node_base[:, :], [[P, NODE_TILES + 1]], base=0, channel_multiplier=0,
                       allow_small_or_imprecise_dtypes=True)
                for n, c in enumerate((LN_EPS, -0.5, -1.0, 0.0)):
                    g.memset(powers[:, n:n + 1], c)
                g.memset(ident[:, :], 0.0).then_inc(pool_steps, 1)
                pool.wait_ge(pool_steps, 1)
                g.affine_select(out=ident[:, :], in_=ident[:, :], compare_op=ALU.not_equal, fill=1.0, base=0,
                                pattern=[[-1, P]], channel_multiplier=1)
                g.memset(sums[:, POOL_ZEROS:ACT_ZEROS], 0.0)
                pool.wait_ge(ranged, 1)
                g.partition_all_reduce(ranges_all, ranges, P, bass.bass_isa.ReduceOp.max).then_inc(reduced, 1)

            @block.vector
            def _(dve):
                v, chain = nc.vector, Chain(dve, own_steps)
                dve.wait_ge(plan_in, 32)
                v.tensor_copy(dst_cols[:, :], cols_i)
                v.memset(score_dst[:, :, :], 0.0)
                v.memset(z_max[:, :, :], -BIG)
                chain.step(v.tensor_copy(dst_f, rows_i[:, :, :]))
                v.tensor_reduce(hi, dst_f, AX.X, ALU.max)
                chain.step(v.tensor_scalar(dst_neg, dst_f, 0.0, 1.0e6, ALU.is_lt, ALU.mult))
                chain.step(v.tensor_tensor(dst_neg, dst_neg, dst_f, ALU.add))
                chain.step(v.tensor_reduce(lo, dst_neg, AX.X, ALU.min))
                dve.wait_ge(made, 3)
                v.memset(ranges, 0.0)
                v.tensor_scalar(tile_back, tile_no, -1.0, FAR, ALU.mult, ALU.add)
                chain.step(v.tensor_scalar(tile_no, tile_no, 1.0, None, ALU.add))
                for c in range(TILE_ROWS):
                    chain.step(v.tensor_scalar(above, base_hi, lo[:, c:c + 1], None, ALU.is_ge))
                    chain.step(v.scalar_tensor_tensor(meets, base_lo, hi[:, c:c + 1], above, ALU.is_le, ALU.mult))
                    v.scalar_tensor_tensor(ranges[:, 0, :], meets, tile_back[:, c:c + 1], ranges[:, 0, :],
                                           ALU.mult, ALU.max)
                    chain.step(v.scalar_tensor_tensor(ranges[:, 1, :], meets, tile_no[:, c:c + 1],
                                                      ranges[:, 1, :], ALU.mult, ALU.max))
                v.tensor_copy(total[0:1, :], total_zero(v, chain, total)).then_inc(ranged, 1)
                dve.wait_ge(reduced, 1)
                r = ranges_all[0:1, :, :]
                chain.step(v.tensor_scalar(firsts[0:1, :], r[:, 0, :], -1.0, FAR, ALU.mult, ALU.add))
                v.tensor_scalar(plan[0:1, 0, 0:NODE_TILES], firsts[0:1, :], float(EDGE_TILES), None, ALU.min)
                chain.step(v.scalar_tensor_tensor(counts[0:1, :], r[:, 0, :], -FAR, r[:, 1, :], ALU.add, ALU.add))
                v.memset(plan[0:1, 0, NODE_TILES:], EDGE_TILES)
                for size, times, shift in ((UNIT, 1.0, 1), (GROUP, DIV_GROUP, 16)):
                    row = COUNT_ROW[size]
                    chain.step(v.tensor_scalar(wanted[0:1, :], counts[0:1, :], 1.0, float(size - 1), ALU.max,
                                               ALU.add))
                    chain.step(v.tensor_scalar(counts_i[0:1, 0:NODE_TILES], wanted[0:1, :], times, None, ALU.mult))
                    chain.step(v.tensor_scalar(plan[0:1, row, 0:NODE_TILES], counts_i[0:1, 0:NODE_TILES], shift,
                                               None, ALU.logical_shift_right))
                    v.memset(plan[0:1, row, NODE_TILES:], MANY)
                    chain.step(v.tensor_reduce(total[0:1, :], plan[0:1, row, 0:NODE_TILES], AX.X, ALU.add))
                    chain.step(v.tensor_scalar(counts_i[0:1, 0:1], total[0:1, :], float(AHEAD - 1), None, ALU.add))
                    chain.step(v.tensor_scalar(plan[0:1, row + 1, 0:1], counts_i[0:1, 0:1], 2, None,
                                               ALU.logical_shift_right))
                v.memset(sums[:, 0:POOL_ZEROS], 0.0)

        with ExitStack() as own:
            split_steps = phase_sem("split_steps")
            block = own.enter_context(nc.Block())

            @block.vector
            def _(dve):
                v, chain = nc.vector, Chain(dve, split_steps)
                v.memset(ee_whb[EDIM:, :].bitcast(F32), 0.0)
                v.tensor_copy(ee_whb[0:EDIM, :], ee_w1_raw[0:EDIM, :])
                chain.step(v.tensor_copy(ee_whl[:, :], ee_w1_raw))
                v.tensor_tensor(ee_whl[EDIM:, :], ee_w1_raw[EDIM:, :], ee_whl[EDIM:, :].bitcast(F32), ALU.subtract)
                high, low = slice(B_HIGH, B_HIGH + 1), slice(B_LOW, B_LOW + 1)
                v.tensor_copy(ee_whb[high, :], ee_b1_raw[high, :])
                chain.step(v.tensor_copy(ee_whb[low, :], ee_b1_raw[low, :]))
                v.tensor_tensor(ee_whb[low, :], ee_b1_raw[low, :], ee_whb[low, :].bitcast(F32), ALU.subtract)
                v.tensor_scalar(self_row[:, 0:EMB], self_row[:, 0:EMB], 0.0, None, ALU.max)
                v.memset(self_row[:, EMB:], 1.0)
                v.tensor_scalar(eps2[:, :], eps2[:, :], 2.0, None, ALU.add)
                v.tensor_copy(ident_bf[:, :], ident[:, :])

        planning.close()
        with ExitStack() as own:
            arena, at = phase_arena(own, ARENA - 2 * 2 * UNIT * P), [0]
            xg = take(arena, at, [AHEAD * UNIT, D])
            hid = take(arena, at, [2, UNIT, (EMB + 2)])
            ea = take(arena, at, [AHEAD, UNIT * P])
            ea_high, ea_low = [own.enter_context(nc.sbuf_tensor(name, [P, 2, UNIT * P], F32R))
                               for name in ("ea_high", "ea_low")]
            hits = take(arena, at, [AHEAD, UNIT, P])
            rel = take(arena, at, [2, UNIT])
            idx = [own.enter_context(nc.sbuf_tensor(f"idx{u}", [P, UNIT], I32)) for u in range(AHEAD)]
            ps_hid = [own.enter_context(nc.psum_tensor(f"ps_hid{i}", [P, UNIT, EMB], F32)) for i in range(2)]
            ps_sum = [own.enter_context(nc.psum_tensor(f"ps_sum{i}", [P, 2, 512], F32)) for i in range(2)]

            def many(name, n=AHEAD):
                return [phase_sem(f"{name}{i}") for i in range(n)]

            ea_in, xg_in = [many("ea_in"), many("ea_in_again")], many("xg_in", AHEAD * UNIT)
            high_set, low_set = many("high_set"), many("low_set")
            rel_set, hits_set = many("rel_set"), many("hits_set")
            hid_mm, hid_set, sum_mm, sum_out = many("hid_mm"), many("hid_set"), many("sum_mm"), many("sum_out")
            ones_set = phase_sem("ones_set")
            idx_set = many("idx_set")
            block = own.enter_context(nc.Block())

            @block.sync
            def _(sp):
                rounds, walk = Rounds(sp, plan, "ea"), Walk(sp, plan, "ea")

                def load(p):
                    tile, _ = walk.place()
                    rounds.seen(low_set, p - AHEAD)
                    for q in range(2):
                        sp.dma_start(ea[q * EDIM:(q + 1) * EDIM, p % AHEAD, :],
                                     eaT[:, bass.ds(tile * P, UNIT * P)]).then_inc(ea_in[q][p % AHEAD], 16)
                    walk.advance()

                load(0)
                load(1)
                with sp.Fori(0, rounds.trips):
                    rounds.begin()
                    for u in range(AHEAD):
                        load(u + 2)
                    rounds.end()
                sp.wait_ge(weights_in, 16 * 17)

            @block.gpsimd
            def _(pool):
                g = nc.gpsimd
                for s in idx_set:
                    pool.sem_inc(s, 1)
                rounds, walk = Rounds(pool, plan, "xg"), Walk(pool, plan, "xg")

                def index(p):
                    tile, _ = walk.place()
                    rounds.seen(sum_mm, p - AHEAD)
                    g.tensor_copy(idx[p % AHEAD][:, :], src_cols[:, bass.ds(tile, UNIT)]).then_inc(
                        idx_set[p % AHEAD], 1)

                def gather(p):
                    rounds.seen(idx_set, p)
                    walk.advance()
                    for k in range(UNIT):
                        g.indirect_dma_start(xg[:, UNIT * (p % AHEAD) + k, :], None, x,
                                             bass.IndirectOffsetOnAxis(ap=idx[p % AHEAD][:, k:k + 1], axis=0)
                                             ).then_inc(xg_in[UNIT * (p % AHEAD) + k], 16)

                index(0)
                walk.advance()
                index(1)
                gather(0)
                with pool.Fori(0, rounds.trips):
                    rounds.begin()
                    for u in range(AHEAD):
                        index(u + 2)
                        gather(u + 1)
                    rounds.end()
                for k in range(UNIT):
                    pool.wait_ge(xg_in[k], pool.snap(rounds.trips * 16) + 16)

            @block.scalar
            def _(act):
                for s in hid_set + high_set:
                    act.sem_inc(s, 1)
                rounds = Rounds(act, plan, "hid")

                def high(p):
                    for q in range(2):
                        rounds.landed(ea_in[q], p)
                    rounds.seen(hid_mm, p - 2)
                    rounds.seen(low_set, p - 2)
                    nc.scalar.activation(ea_high[:, p % 2, :], ea[:, p % AHEAD, :], ACT.Copy).then_inc(
                        high_set[p % AHEAD], 1)

                def relu(p):
                    rounds.seen(hid_mm, p)
                    rounds.seen(sum_mm, p - 2)
                    nc.scalar.activation(hid[:, p % 2, :, 0:EMB], ps_hid[p % 2][:, :, :],
                                         ACT.Relu).then_inc(hid_set[p % AHEAD], 1)

                high(0)
                high(1)
                relu(0)
                with act.Fori(0, rounds.trips):
                    rounds.begin()
                    for u in range(AHEAD):
                        high(u + 2)
                        relu(u + 1)
                    rounds.end()

            @block.tensor
            def _(pe):
                for s in hid_mm + sum_mm:
                    pe.sem_inc(s, 1)
                rounds = Rounds(pe, plan, "mm")

                def hidden(p):
                    rounds.seen(high_set, p)
                    rounds.seen(low_set, p)
                    rounds.seen(hid_set, p - 2)
                    for k in range(UNIT):
                        tile = slice(k * P, (k + 1) * P)
                        nc.tensor.matmul(ps_hid[p % 2][:, k, :], ea_high[:, p % 2, tile], ee_whl[:, :],
                                         start=True, stop=False)
                        mm = nc.tensor.matmul(ps_hid[p % 2][:, k, :], ea_low[:, p % 2, tile], ee_whb[:, :],
                                              start=False, stop=True)
                    mm.then_inc(hid_mm[p % AHEAD], 1)

                pe.wait_ge(ones_set, 1)
                hidden(0)
                with pe.Fori(0, rounds.trips):
                    rounds.begin()
                    for u in range(AHEAD):
                        hidden(u + 1)
                        rounds.seen(hits_set, u)
                        rounds.seen(hid_set, u)
                        rounds.seen(sum_out, u - 2)
                        for k in range(UNIT):
                            rounds.landed(xg_in, u, k)
                            nc.tensor.matmul(ps_sum[u % 2][:, 0, 0:D], hits[:, u, k, :], xg[:, UNIT * u + k, :],
                                             start=(k == 0), stop=(k == UNIT - 1))
                            mm = nc.tensor.matmul(ps_sum[u % 2][:, 1, 0:EMB + 2], hits[:, u, k, :],
                                                  hid[:, u % 2, k, :], start=(k == 0), stop=(k == UNIT - 1))
                        mm.then_inc(sum_mm[u], 1)
                    rounds.end()

            @block.vector
            def _(dve):
                v = nc.vector
                for s in hits_set + sum_out + low_set + rel_set:
                    dve.sem_inc(s, 1)
                v.memset(hid[:, :, :, EMB:EMB + 1], 1.0)
                v.memset(hid[:, :, :, EMB + 1:EMB + 2], 0.0)
                v.memset(ea_low[EDIM:, :, :].bitcast(F32), 1.0).then_inc(ones_set, 1)
                rounds, walk = Rounds(dve, plan, "sum"), Walk(dve, plan, "sum")

                before = dve.alloc_register("node_before")

                def low(p):
                    rounds.seen(high_set, p)
                    rounds.seen(hid_mm, p - 2)
                    v.tensor_tensor(ea_low[0:EDIM, p % 2, :], ea[0:EDIM, p % AHEAD, :],
                                    ea_high[0:EDIM, p % 2, :].bitcast(F32), ALU.subtract).then_inc(
                                        low_set[p % AHEAD], 1)

                def compare(p):
                    rounds.seen(hits_set, p - 2)
                    tile, node = walk.place()
                    v.tensor_tensor(rel[:, p % 2, :], dst_cols[:, bass.ds(tile, UNIT)],
                                    node_base[:, bass.ds(node, 1)].to_broadcast([P, UNIT]),
                                    ALU.subtract).then_inc(rel_set[p % AHEAD], 1)
                    node_before = dve.snap(before, min_val=0, max_val=NODE_TILES)
                    dve.reg_mov(before, walk.node)
                    rounds.seen(rel_set, p)
                    rounds.seen(sum_mm, p - AHEAD)
                    for k in range(UNIT):
                        ins = v.tensor_scalar(hits[:, p % AHEAD, k, :], iota_row[:, :], rel[:, p % 2, k:k + 1],
                                              None, ALU.is_equal)
                    ins.then_inc(hits_set[p % AHEAD], 1)
                    walk.advance()
                    return node_before

                dve.reg_mov(before, 0)
                low(0)
                low(1)
                compare(0)
                with dve.Fori(0, rounds.trips):
                    rounds.begin()
                    for u in range(AHEAD):
                        node = compare(u + 1)
                        low(u + 2)
                        rounds.seen(sum_mm, u)
                        rounds.seen(sum_out, u - 1)
                        to = sum0[:, bass.ds(node, 1), :].rearrange("p a f -> p (a f)")
                        v.tensor_tensor(to[:, 0:D + EMB].rearrange("p (a f) -> p a f", a=2),
                                        to[:, 0:D + EMB].rearrange("p (a f) -> p a f", a=2),
                                        ps_sum[u % 2][:, :, 0:EMB], ALU.add)
                        v.tensor_tensor(to[:, D + EMB:], to[:, D + EMB:], ps_sum[u % 2][:, 1, EMB:EMB + 1],
                                        ALU.add).then_inc(sum_out[u], 1)
                    rounds.end()

        end_phase()
        node_mlp(nc, locals())
        end_phase()
        attention(nc, locals())
        end_phase()
        output_norm(nc, locals())


def total_zero(v, chain, total):
    chain.step(v.memset(total[0:1, :], 0.0))
    return total[0:1, :]


def norm_factors(g, chain, mv, powers):
    mean, var, scale, shift = [mv[:, :, c:c + 1].rearrange("p n o -> p (n o)") for c in range(4)]
    eps, root, minus = [powers[:, c:c + 1].to_broadcast([P, mv.shape[1]]) for c in range(3)]
    chain.step(g.tensor_tensor(scale, var, eps, ALU.add))
    g.tensor_tensor(shift, mean, minus, ALU.mult)
    chain.step(g.tensor_tensor(scale, scale, root, ALU.pow))
    return g.tensor_tensor(shift, shift, scale, ALU.mult)


def node_mlp(nc, env):
    e, phase_sem = env, env["phase_sem"]
    take, sum0 = e["take"], e["sum0"]
    KH, KD = H // P, D // P
    STEPS = 5
    with ExitStack() as own:
        def ps(name, shape):
            return own.enter_context(nc.psum_tensor(name, shape, F32))

        arena, at = e["phase_arena"](own), [0]
        edge_sum = take(arena, at, [EMB + 1])
        edge_sumT = take(arena, at, [KD, P])
        xa, xc = take(arena, at, [D]), take(arena, at, [D])
        h0, hT = take(arena, at, [D]), take(arena, at, [KD, P])
        a1, a2 = take(arena, at, [H]), take(arena, at, [H])
        a1T, a2T = take(arena, at, [KH, P]), take(arena, at, [KH, P])
        y, x1, x1T = take(arena, at, [D]), take(arena, at, [D]), take(arena, at, [KD, P])
        wh_row = take(arena, at, [TABLE])
        wh = wh_row[:, 0:HEADS * GROW].rearrange("p (h c) -> p h c", h=HEADS)
        wh_scores = wh[:, :, C:GROW].rearrange("p h c -> p (h c)")
        wh_parts = wh_row[:, HEADS * GROW:].bitcast(BF16)
        rest = take(arena, at, [HEADS])
        prod = take(arena, at, [D])
        st1, st2 = take(arena, at, [2, 6]), take(arena, at, [2, 6])
        mv1, mv2, mvx = take(arena, at, [4]), take(arena, at, [4]), take(arena, at, [4])
        ps_e = ps("ps_e", [P, 2, D])
        ps_x = ps("ps_x", [P, 2, D])
        ps_1 = ps("ps_1", [P, 2, 512])
        ps_2 = ps("ps_2", [P, 2, 512])
        ps_n = ps("ps_n", [P, KH, P])

        (xa_in, xc_in, edge_set, edge_t, edge_c, e_mm, h_set, h_t, h_c, a1_mm, a1_out, a1_set, a1_n,
         a1_t, a1_c, a2_mm, a2_out, a2_set, a2_n, a2_t, a2_c, y_mm, x1_set, x1_t, x1_c, wh_mm, wh_set,
         x1_stored, wh_stored, xc_used, h0_used, steps, a1_var, a2_var, y_var, y_set, x1_var, x1_fac,
         parts_set, pool_steps) = [phase_sem(f"s_{n}") for n in (
            "xa_in xc_in edge_set edge_t edge_c e_mm h_set h_t h_c a1_mm a1_out a1_set a1_n a1_t a1_c "
            "a2_mm a2_out a2_set a2_n a2_t a2_c y_mm x1_set x1_t x1_c wh_mm wh_set x1_stored "
            "wh_stored xc_used h0_used dve_steps a1_var a2_var y_var y_set x1_var x1_fac parts_set pool_steps").split()]

        def pipeline(eng, body, chain=None, last=NODE_TILES):
            for i in range(STEPS - 1):
                body(i)
            if chain:
                chain.enter()
            with eng.Fori(STEPS - 1, last) as i:
                i = eng.snap(i, min_val=STEPS - 1, max_val=last - 1)
                if chain:
                    chain.begin()
                body(i)
                if chain:
                    chain.end()
            if chain:
                chain.leave(last - STEPS + 1)
            for i in range(last, NODE_TILES + STEPS - 1):
                body(i)

        def runs(i, lag):
            return not isinstance(i, int) or 0 <= i - lag < NODE_TILES

        def past(i, n=0):
            return not isinstance(i, int) or i - n > 0

        def rows(dram, i):
            return dram[bass.ds(i * P, P), :]

        block = own.enter_context(nc.Block())

        @block.sync
        def _(sp):
            def body(i):
                if runs(i, 0):
                    if past(i):
                        sp.wait_ge(h0_used, i)
                    sp.dma_start(xa, rows(e["x"], i)).then_inc(xa_in, 16)
                if runs(i, 4):
                    t = i - 4
                    sp.wait_ge(x1_set, t + 1)
                    sp.dma_start(rows(e["x1_dram"], t), x1).then_inc(x1_stored, 16)
                if runs(i, 3):
                    t = i - 3
                    if past(i, 3):
                        sp.wait_ge(xc_used, t)
                    sp.dma_start(xc, rows(e["x"], t)).then_inc(xc_in, 16)
                if runs(i, 4):
                    t = i - 4
                    sp.wait_ge(parts_set, t + 1)
                    sp.dma_start(rows(e["table"], t), wh_row).then_inc(wh_stored, 16)

            pipeline(sp, body)
            sp.wait_ge(x1_stored, 16 * NODE_TILES)
            sp.wait_ge(wh_stored, 16 * NODE_TILES)

        @block.gpsimd
        def _(pool):
            g, chain = nc.gpsimd, Chain(pool, pool_steps)

            def edges(i):
                if past(i):
                    pool.wait_ge(edge_t, i)
                    pool.wait_ge(h0_used, i)
                g.tensor_tensor(edge_sum, sum0[:, bass.ds(i, 1), D:].rearrange("p a f -> p (a f)"),
                                e["self_row"][:, :], ALU.add).then_inc(edge_set, 1)

            def factors(t, aggregated, mv, done):
                pool.wait_ge(aggregated, t + 1)
                norm_factors(g, chain, mv.rearrange("p (n c) -> p n c", n=1), e["powers"]).then_inc(done, 1)

            def parts(t):
                no_change = e["powers"][:, 3:4].to_broadcast([P, HEADS])
                pool.wait_ge(wh_set, t + 1)
                chain.step(g.tensor_tensor(wh_parts[:, 0:HEADS], wh_scores, no_change, ALU.add))
                chain.step(g.tensor_tensor(rest, wh_scores, wh_parts[:, 0:HEADS], ALU.subtract))
                chain.step(g.tensor_tensor(wh_parts[:, HEADS:2 * HEADS], rest, no_change, ALU.add))
                g.tensor_tensor(wh_parts[:, 2 * HEADS:], rest, wh_parts[:, HEADS:2 * HEADS],
                                ALU.subtract).then_inc(parts_set, 1)

            def body(i):
                if runs(i, 3):
                    factors(i - 3, a2_var, mv2, a2_set)
                if runs(i, 4):
                    factors(i - 4, y_var, mvx, y_set)
                if runs(i, 1):
                    factors(i - 1, a1_var, mv1, a1_set)
                if runs(i, 4):
                    factors(i - 4, x1_var, mvx, x1_fac)
                if runs(i, -1):
                    edges(i + 1)
                if runs(i, 4):
                    parts(i - 4)

            edges(0)
            pipeline(pool, body, chain, last=NODE_TILES - 1)

        @block.tensor
        def _(pe):
            t_ = nc.tensor
            ident = e["ident"]

            def turn(to, of, n):
                for k in range(n):
                    mm = t_.transpose(to[:, k * P:(k + 1) * P], of[:, k * P:(k + 1) * P], ident[:, :])
                return mm

            def product(to, rowsT, weights, n):
                for k in range(n):
                    mm = t_.matmul(to, rowsT[:, k, :], weights[:, k, :], start=(k == 0), stop=(k == n - 1))
                return mm

            def half(n):
                return slice(n * 512, (n + 1) * 512)

            turned_rows = ps_n[:, :, :].rearrange("p k n -> p (k n)")

            def body(i):
                if runs(i, 2):
                    t = i - 2
                    pe.wait_ge(a1_n, t + 1)
                    if past(i, 3):
                        pe.wait_ge(a2_c, t - 1)
                    turn(turned_rows, a1, KH).then_inc(a1_t, 1)
                if runs(i, 1):
                    t = i - 1
                    pe.wait_ge(h_c, t + 1)
                    if past(i, 1):
                        pe.wait_ge(a1_out, t)
                    for n in range(2):
                        mm = product(ps_1[:, n, :], hT, e["w1s"][:, :, half(n)], KD)
                    mm.then_inc(a1_mm, 1)
                if runs(i, 0):
                    pe.wait_ge(edge_set, i + 1)
                    if past(i):
                        pe.wait_ge(h_c, i)
                    turn(ps_e[:, 0, :], edge_sum, KD).then_inc(edge_t, 1)
                if runs(i, 2):
                    t = i - 2
                    pe.wait_ge(a1_c, t + 1)
                    if past(i, 2):
                        pe.wait_ge(a2_out, t)
                    product(ps_2[:, 0, :], a1T, e["w2s"][:, :, half(0)], KH)
                if runs(i, 0):
                    pe.wait_ge(edge_c, i + 1)
                    product(ps_e[:, 1, :], edge_sumT, e["ee_w2s"], KD).then_inc(e_mm, 1)
                if runs(i, 4):
                    t = i - 4
                    pe.wait_ge(x1_set, t + 1)
                    turn(ps_x[:, 1, :], x1, KD).then_inc(x1_t, 1)
                if runs(i, 3):
                    t = i - 3
                    pe.wait_ge(a2_n, t + 1)
                    pe.wait_ge(a1_c, min(t + 2, NODE_TILES) if isinstance(i, int) else t + 2)
                    turn(turned_rows, a2, KH).then_inc(a2_t, 1)
                if runs(i, 4):
                    t = i - 4
                    pe.wait_ge(x1_c, t + 1)
                    product(ps_x[:, 0, :], x1T, e["gat_w"], KD).then_inc(wh_mm, 1)
                if runs(i, 2):
                    product(ps_2[:, 1, :], a1T, e["w2s"][:, :, half(1)], KH).then_inc(a2_mm, 1)
                if runs(i, 0):
                    pe.wait_ge(h_set, i + 1)
                    turn(ps_e[:, 0, :], h0, KD).then_inc(h_t, 1)
                if runs(i, 3):
                    t = i - 3
                    pe.wait_ge(a2_c, t + 1)
                    if past(i, 3):
                        pe.wait_ge(wh_set, t)
                    product(ps_x[:, 0, :], a2T, e["w3s"], KH).then_inc(y_mm, 1)

            pipeline(pe, body)

        @block.scalar
        def _(act):
            a = nc.scalar

            def scaled(to, scale, shift):
                for k in range(KH):
                    ins = a.activation(to[:, k, :], ps_n[:, k, :], ACT.Relu, bias=shift[:, k:k + 1],
                                       scale=scale[:, k:k + 1])
                return ins

            def copied(to, of):
                return a.activation(to.rearrange("p k n -> p (k n)"), of, ACT.Copy)

            def normed(x, mv):
                return a.activation(x, x, ACT.Identity, bias=mv[:, 3:4], scale=mv[:, 2:3])

            def body(i):
                if runs(i, 2):
                    t = i - 2
                    act.wait_ge(a1_t, t + 1)
                    if past(i, 2):
                        act.wait_ge(a2_mm, t)
                    scaled(a1T, e["g1s"], e["be1s"]).then_inc(a1_c, 1)
                if runs(i, 0):
                    act.wait_ge(edge_t, i + 1)
                    if past(i):
                        act.wait_ge(e_mm, i)
                    copied(edge_sumT, ps_e[:, 0, :]).then_inc(edge_c, 1)
                if runs(i, 3):
                    act.wait_ge(a2_set, i - 2)
                    normed(a2, mv2).then_inc(a2_n, 1)
                if runs(i, 4):
                    t = i - 4
                    act.wait_ge(x1_t, t + 1)
                    if past(i, 4):
                        act.wait_ge(wh_mm, t)
                    copied(x1T, ps_x[:, 1, :]).then_inc(x1_c, 1)
                if runs(i, 3):
                    t = i - 3
                    act.wait_ge(a2_t, t + 1)
                    if past(i, 3):
                        act.wait_ge(y_mm, t)
                    scaled(a2T, e["g2s"], e["be2s"]).then_inc(a2_c, 1)
                if runs(i, 1):
                    act.wait_ge(a1_set, i)
                    normed(a1, mv1).then_inc(a1_n, 1)
                if runs(i, 0):
                    act.wait_ge(h_t, i + 1)
                    if past(i):
                        act.wait_ge(a1_mm, i)
                    copied(hT, ps_e[:, 0, :]).then_inc(h_c, 1)

            pipeline(act, body)

        @block.vector
        def _(dve):
            v, chain = nc.vector, Chain(dve, steps)

            def wide(t, first, mm, of, bias, a, st, mv, turned, read, aggregated):
                dve.wait_ge(mm, t + 1)
                if not first:
                    dve.wait_ge(turned, t)
                ins = v.tensor_tensor(a.rearrange("p (n f) -> p n f", n=2), of[:, :, :],
                                      bias.rearrange("p (n f) -> p n f", n=2), ALU.add)
                ins.then_inc(read, 1)
                dve.wait_ge(read, t + 1)
                for n in range(2):
                    ins = v.bn_stats(st[:, n, :], a[:, n * 512:(n + 1) * 512])
                chain.step(ins)
                v.memset(idle, 0.0)
                v.bn_aggr(mv[:, 0:2], st.rearrange("p a b -> p (a b)")).then_inc(aggregated, 1)

            def narrow(x, aggregated):
                chain.step(v.bn_stats(st1x, x))
                v.memset(idle, 0.0)
                v.bn_aggr(mvx[:, 0:2], st1x).then_inc(aggregated, 1)

            st1x, idle = take(arena, at, [6]), take(arena, at, [1])

            def body(i):
                if runs(i, 3):
                    wide(i - 3, not past(i, 3), a2_mm, ps_2, e["b2_all"][:, :], a2, st2, mv2, a2_t, a2_out, a2_var)
                if runs(i, 4):
                    t = i - 4
                    dve.wait_ge(y_mm, t + 1)
                    chain.step(v.tensor_tensor(y, ps_x[:, 0, :], e["b3_all"][:, :], ALU.add))
                    dve.wait_ge(xc_in, (t + 1) * 16)
                    chain.step(v.tensor_tensor(y, y, xc, ALU.add))
                    narrow(y, y_var)
                if runs(i, 1):
                    wide(i - 1, not past(i, 1), a1_mm, ps_1, e["b1_all"][:, :], a1, st1, mv1, a1_t, a1_out, a1_var)
                if runs(i, 4):
                    t = i - 4
                    dve.wait_ge(y_set, t + 1)
                    chain.step(v.tensor_scalar(y, y, mvx[:, 2:3], mvx[:, 3:4], ALU.mult, ALU.add))
                    chain.step(v.tensor_tensor(y, y, e["bn_g_all"][:, :], ALU.mult))
                    chain.step(v.tensor_tensor(y, y, e["bn_b_all"][:, :], ALU.add))
                    v.scalar_tensor_tensor(y, y, 0.0, xc, ALU.max, ALU.add).then_inc(xc_used, 1)
                    dve.wait_ge(xc_used, t + 1)
                    narrow(y, x1_var)
                if runs(i, 0):
                    dve.wait_ge(edge_set, i + 1)
                    dve.wait_ge(xa_in, (i + 1) * 16)
                    if past(i):
                        dve.wait_ge(h_t, i)
                    chain.step(v.scalar_tensor_tensor(h0, xa, e["eps2"][:, 0:1],
                                                      sum0[:, bass.ds(i, 1), 0:D].rearrange("p a f -> p (a f)"),
                                                      ALU.mult, ALU.add))
                    v.scalar_tensor_tensor(h0, e["ee_b2_all"][:, :], edge_sum[:, EMB:EMB + 1], h0,
                                           ALU.mult, ALU.add).then_inc(h0_used, 1)
                if runs(i, 4):
                    t = i - 4
                    dve.wait_ge(x1_fac, t + 1)
                    if past(i, 4):
                        dve.wait_ge(x1_t, t)
                        dve.wait_ge(x1_stored, t * 16)
                    v.tensor_scalar(x1, y, mvx[:, 2:3], mvx[:, 3:4], ALU.mult, ALU.add).then_inc(x1_set, 1)
                if runs(i, 0):
                    dve.wait_ge(h0_used, i + 1)
                    dve.wait_ge(e_mm, i + 1)
                    v.tensor_tensor(h0, ps_e[:, 1, :], h0, ALU.add).then_inc(h_set, 1)
                if runs(i, 4):
                    t = i - 4
                    dve.wait_ge(wh_mm, t + 1)
                    if past(i, 4):
                        dve.wait_ge(wh_stored, t * 16)
                    v.tensor_copy(wh[:, :, 0:C], ps_x[:, 0, :].rearrange("p (h c) -> p h c", h=HEADS))
                    chain.step(v.tensor_tensor(prod, ps_x[:, 0, :], e["att_d"][:, :], ALU.mult))
                    chain.step(v.tensor_reduce(e["score_dst"][:, bass.ds(t, 1), :],
                                               prod.rearrange("p (o h c) -> p o h c", o=1, h=HEADS), AX.X, ALU.add))
                    chain.step(v.tensor_tensor(prod, ps_x[:, 0, :], e["att_s"][:, :], ALU.mult))
                    v.tensor_reduce(wh_scores.rearrange("p (h o) -> p h o", o=1),
                                    prod.rearrange("p (h c) -> p h c", h=HEADS), AX.X, ALU.add).then_inc(wh_set, 1)

            pipeline(dve, body, chain)


def attention(nc, env):
    e, phase_sem = env, env["phase_sem"]
    take, sums, sum1, plan = e["take"], e["sums"], e["sum1"], e["plan"]
    src_cols, dst_cols, ident = e["src_cols"], e["dst_cols"], e["ident"]
    with ExitStack() as own:
        def many(name, n=AHEAD):
            return [phase_sem(f"{name}{i}") for i in range(n)]

        def ps(name, shape, dt=F32):
            return own.enter_context(nc.psum_tensor(name, shape, dt))

        at = [e["SPARE"]]
        rows = take(sums, at, [AHEAD * GROUP * TABLE])
        rows_by_slot = rows.rearrange("p (t c) -> p t c", c=TABLE)
        whg = rows_by_slot[:, :, 0:HEADS * GROW].rearrange("p t (h c) -> p t h c", h=HEADS)
        parts = rows.bitcast(BF16).rearrange("p (t c) -> p t c", c=2 * TABLE)[:, :, 2 * HEADS * GROW:]
        hits = take(sums, at, [AHEAD * GROUP, P])
        hitsT = take(sums, at, [2 * GROUP, P])
        assert at[0] <= sums.shape[1]
        arena, at = e["phase_arena"](own), [0]
        miss = take(arena, at, [GROUP * P]).bitcast(BF16).rearrange("p (g n) -> p g n", n=P)
        rel = take(arena, at, [AHEAD, GROUP])
        ones = take(arena, at, [GROUP * HEADS * P // 2]).bitcast(BF16).rearrange("p (g n) -> p g n", n=P)
        minus_big = take(arena, at, [P // 2]).bitcast(BF16)
        flat = take(arena, at, [P]).bitcast(BF16).rearrange("p (g n) -> p g n", n=P)
        partsT = take(arena, at, [P]).bitcast(BF16).rearrange("p (g n) -> p g n", n=P)
        where = take(arena, at, [GROUP, HEADS])
        idle = take(arena, at, [1])
        tile_top = take(arena, at, [GROUP, HEADS])
        top, zt = take(arena, at, [HEADS]), take(arena, at, [HEADS])
        node_z = take(arena, at, [2, 2 * HEADS])
        fall, shrink = take(arena, at, [2, HEADS]), take(arena, at, [2, HEADS])
        ze, zp = take(arena, at, [GROUP, HEADS]), take(arena, at, [2 * GROUP, HEADS])
        idx = [own.enter_context(nc.sbuf_tensor(f"gidx{u}", [P, GROUP], I32)) for u in range(AHEAD)]
        ps_top = [ps(f"ps_top{i}", [P, HEADS, P]) for i in range(BANKS)]
        ps_parts = ps("ps_parts", [P, P], BF16)
        ps_miss = ps("ps_miss", [P, GROUP, P], BF16)
        ps_node = ps("ps_node", [P, GROUP, 2 * HEADS])
        ps_sum = [ps(f"ps_att{i}", [P, HEADS, GROW]) for i in range(2)]
        whg_in = many("whg_in", AHEAD * GROUP)
        top_mm, top_read = many("g_topmm", AHEAD * GROUP), many("g_topread", AHEAD * GROUP)
        (rel_set, idx_set, miss_set, hits_set, turned, parts_turned, flat_set, partsT_set, hitsT_set, node_set,
         fall_set, shrink_set, node_mm, zp_set, p_set, half_weighed, weighed, half_mm, att_mm, att_out) = [many(n) for n in (
            "g_rel g_idx g_miss g_hits g_turned g_pturned g_flat g_partsT g_hitsT g_node g_fall g_shrink "
            "g_nodemm g_zp g_p g_hweighed g_weighed g_halfmm g_attmm g_attout").split()]
        ident_bf = e["ident_bf"]
        ones_set = phase_sem("g_ones")
        HALF = GROUP // 2
        assert GROUP % BANKS == 0 and GROUP * PARTS * HEADS <= P
        PART_ROWS = GROUP * PARTS * HEADS
        steps = phase_sem("g_steps")
        block = own.enter_context(nc.Block())

        def slot(p, n=AHEAD):
            return slice(GROUP * (p % n), GROUP * (p % n) + GROUP)

        @block.gpsimd
        def _(pool):
            g = nc.gpsimd
            for s in rel_set + idx_set:
                pool.sem_inc(s, 1)
            rounds, walk = Rounds(pool, plan, "whg", GROUP), Walk(pool, plan, "whg", GROUP)

            def prepare(p):
                u = p % AHEAD
                rounds.seen(miss_set, p - AHEAD)
                rounds.seen(half_mm, p - AHEAD)
                tile, node = walk.place()
                g.tensor_copy(idx[u][:, :], src_cols[:, bass.ds(tile, GROUP)]).then_inc(idx_set[u], 1)
                g.tensor_tensor(rel[:, u, :], dst_cols[:, bass.ds(tile, GROUP)],
                                e["node_base"][:, bass.ds(node, 1)].to_broadcast([P, GROUP]),
                                ALU.subtract).then_inc(rel_set[u], 1)
                rounds.seen(idx_set, p)
                walk.advance()
                for k in range(GROUP):
                    if k == HALF:
                        rounds.seen(att_mm, p - AHEAD)
                        g.tensor_tensor(idle, e["powers"][:, 0:1], e["powers"][:, 0:1], ALU.add)
                    g.indirect_dma_start(rows_by_slot[:, GROUP * u + k, :], None,
                                         e["table"], bass.IndirectOffsetOnAxis(ap=idx[u][:, k:k + 1], axis=0)
                                         ).then_inc(whg_in[GROUP * u + k], 16)

            for p in range(AHEAD):
                prepare(p)
            with pool.Fori(0, rounds.trips):
                rounds.begin()
                for u in range(AHEAD):
                    prepare(u + AHEAD)
                rounds.end()
            for n in range(AHEAD * GROUP):
                pool.wait_ge(whg_in[n], pool.snap(rounds.trips * 16) + 16)

        @block.scalar
        def _(act):
            a = nc.scalar
            for s in hits_set + hitsT_set + shrink_set + p_set + half_weighed + weighed + flat_set + partsT_set:
                act.sem_inc(s, 1)
            rounds = Rounds(act, plan, "weigh", GROUP)

            def hit(p):
                s = p % AHEAD
                rounds.seen(miss_set, p)
                rounds.seen(att_mm, p - AHEAD)
                a.activation(hits[:, slot(p), :], miss[:, slot(p, 2), :], ACT.Copy, bias=1.0,
                             scale=-1.0).then_inc(hits_set[s], 1)
                rounds.seen(turned, p)
                rounds.seen(node_mm, p - 2)
                a.activation(hitsT[:, slot(p, 2), :], ps_miss[:, :, :], ACT.Copy, bias=1.0,
                             scale=-1.0).then_inc(hitsT_set[s], 1)

            def flatten(p):
                for k in range(GROUP):
                    rounds.landed(whg_in, p, k)
                rounds.seen(parts_turned, p - 2)
                a.activation(flat[:, p % 2, 0:PART_ROWS].rearrange("p (k c) -> p k c", k=GROUP),
                             parts[:, slot(p), :], ACT.Copy).then_inc(flat_set[p % AHEAD], 1)

            def turned_parts(p):
                rounds.seen(parts_turned, p)
                rounds.seen(top_mm, p - 2, GROUP - 1)
                a.activation(partsT[0:PART_ROWS, p % 2, :], ps_parts[0:PART_ROWS, :], ACT.Copy).then_inc(
                    partsT_set[p % AHEAD], 1)

            def shrinks(p):
                rounds.seen(fall_set, p)
                rounds.seen(att_out, p - 2)
                a.activation(shrink[:, p % 2, :], fall[:, p % 2, :], ACT.Exp).then_inc(shrink_set[p % AHEAD], 1)

            def weights(p):
                rounds.seen(zp_set, p)
                a.activation(whg[:, slot(p), :, C:GROW].rearrange("p k h c -> p k (h c)"),
                             zp[:, slot(p, 2), :], ACT.Exp).then_inc(p_set[p % AHEAD], 1)

            def weigh(p, first, behind):
                if p < 0:
                    return
                if first == 0:
                    rounds.seen(p_set, p)
                for k in range(first, behind):
                    for h in range(HEADS):
                        row = whg[:, GROUP * (p % AHEAD) + k, h, :]
                        ins = a.activation(row[:, 0:C], row[:, 0:C], ACT.Copy, scale=row[:, C:GROW])
                    if k == HALF - 1:
                        ins.then_inc(half_weighed[p % AHEAD], 1)
                    if k == GROUP - 1:
                        ins.then_inc(weighed[p % AHEAD], 1)

            def part(p):
                if p >= 1:
                    weights(p - 1)
                    shrinks(p - 1)
                weigh(p - 1, 0, HALF)
                flatten(p + 1)
                weigh(p - 1, HALF, GROUP - 1)
                turned_parts(p + 1)
                weigh(p - 1, GROUP - 1, GROUP)
                hit(p + 1)

            flatten(0)
            hit(0)
            turned_parts(0)
            part(0)
            part(1)
            with act.Fori(0, rounds.trips):
                rounds.begin()
                for u in range(AHEAD):
                    part(u + 2)
                rounds.end()

        @block.tensor
        def _(pe):
            t = nc.tensor
            for s in turned + parts_turned + top_mm + node_mm + half_mm + att_mm:
                pe.sem_inc(s, 1)
            rounds = Rounds(pe, plan, "att", GROUP)

            def nodes(p):
                rounds.seen(node_set, p)
                rounds.seen(hitsT_set, p)
                rounds.seen(zp_set, p - 1)
                for k in range(GROUP):
                    mm = t.matmul(ps_node[:, k, :], hitsT[:, GROUP * (p % 2) + k, :], node_z[:, p % 2, :],
                                  start=True, stop=True)
                mm.then_inc(node_mm[p % AHEAD], 1)

            def turn_misses(p):
                rounds.seen(miss_set, p)
                rounds.seen(hitsT_set, p - 1)
                for k in range(GROUP):
                    mm = t.transpose(ps_miss[:, k, :], miss[:, GROUP * (p % 2) + k, :], ident_bf[:, :])
                mm.then_inc(turned[p % AHEAD], 1)

            def turn_parts(p):
                rounds.seen(flat_set, p)
                rounds.seen(partsT_set, p - 1)
                t.transpose(ps_parts[0:PART_ROWS, :], flat[:, p % 2, 0:PART_ROWS], ident_bf[:, :]).then_inc(
                    parts_turned[p % AHEAD], 1)

            def spread(p, k):
                if k == 0:
                    rounds.seen(partsT_set, p)
                    rounds.seen(miss_set, p)
                rounds.seen(top_read, p if k >= BANKS else p - 1, (k - BANKS) % GROUP)
                to = ps_top[k % BANKS]
                t.matmul(to[:, :, :], miss[:, GROUP * (p % 2) + k, :], minus_big.rearrange(
                    "p (o n) -> p o n", o=1).to_broadcast([P, HEADS, P]), start=True, stop=False)
                for h in range(HEADS):
                    mm = t.matmul(to[:, h, :], ones[0:PART_ROWS, HEADS * k + h, :], partsT[0:PART_ROWS, p % 2, :],
                                  start=False, stop=(h == HEADS - 1))
                mm.then_inc(top_mm[GROUP * (p % AHEAD) + k], 1)

            def add_up(p, k):
                if k == HALF:
                    rounds.seen(weighed, p)
                if k == 0:
                    rounds.seen(half_weighed, p)
                    rounds.seen(hits_set, p)
                    rounds.seen(att_out, p - 2)
                at = GROUP * (p % AHEAD) + k
                mm = t.matmul(ps_sum[p % 2][:, :, :], hits[:, at, :], whg[:, at, :, :],
                              start=(k == 0), stop=(k == GROUP - 1))
                if k == HALF - 1:
                    mm.then_inc(half_mm[p % AHEAD], 1)
                if k == GROUP - 1:
                    mm.then_inc(att_mm[p % AHEAD], 1)

            def part(p):
                if p >= 1:
                    nodes(p - 1)
                for k in range(GROUP):
                    spread(p, k)
                    if p >= 2 and BANKS - 1 <= k < GROUP - 1:
                        add_up(p - 2, HALF + k - BANKS + 1)
                turn_misses(p + 1)
                turn_parts(p + 1)
                if p >= 1:
                    for k in range(HALF):
                        add_up(p - 1, k)

            turn_misses(0)
            turn_parts(0)
            pe.wait_ge(ones_set, 1)
            part(0)
            part(1)
            with pe.Fori(0, rounds.trips):
                rounds.begin()
                for u in range(AHEAD):
                    part(u + 2)
                rounds.end()

        @block.vector
        def _(dve):
            v, chain = nc.vector, Chain(dve, steps)
            for s in miss_set + top_read + node_set + fall_set + zp_set + att_out:
                dve.sem_inc(s, 1)
            v.memset(sum1, 0.0)
            v.tensor_scalar(minus_big, ident_bf[:, :], -BIG, None, ALU.mult)
            chain.step(v.tensor_reduce(where, ident[:, 0:PART_ROWS].rearrange(
                "p (k r h) -> p k h r", r=PARTS, h=HEADS), AX.X, ALU.add))
            v.tensor_copy(ones, where.rearrange("p k h -> p (k h)").rearrange("p (n o) -> p n o", o=1).to_broadcast(
                [P, GROUP * HEADS, P])).then_inc(ones_set, 1)
            dve.wait_ge(ones_set, 1)
            rounds = Rounds(dve, plan, "top", GROUP)
            walk = Walk(dve, plan, "top", GROUP)
            nodes = [dve.alloc_register(f"node_{n}") for n in range(3)]
            for n in range(3):
                dve.reg_mov(nodes[n], 0)
            iota_row = e["iota_row"]

            def state(tensor, node):
                return tensor[:, bass.ds(node, 1), :].rearrange("p a h -> p (a h)")

            def misses(p):
                rounds.seen(rel_set, p)
                rounds.seen(turned, p - 2)
                rounds.seen(hits_set, p - 2)
                rounds.seen(top_mm, p - 2, GROUP - 1)
                v.tensor_tensor(miss[:, slot(p, 2), :],
                                iota_row[:, :].rearrange("p (o n) -> p o n", o=1).to_broadcast([P, GROUP, P]),
                                rel[:, p % AHEAD, :].rearrange("p (g o) -> p g o", o=1).to_broadcast([P, GROUP, P]),
                                ALU.not_equal).then_inc(miss_set[p % AHEAD], 1)

            def tops(p):
                q, s = p % 2, p % AHEAD
                for k in range(GROUP):
                    rounds.seen(top_mm, p, k)
                    v.tensor_reduce(tile_top[:, k, :], ps_top[k % BANKS][:, :, :], AX.X, ALU.max).then_inc(
                        top_read[GROUP * s + k], 1)
                _, node = walk.place()
                dve.reg_mov(nodes[2], nodes[1])
                dve.reg_mov(nodes[1], nodes[0])
                dve.reg_mov(nodes[0], walk.node)
                to_sum = dve.snap(nodes[2], min_val=0, max_val=NODE_TILES)
                walk.advance()
                score, z = state(e["score_dst"], node), state(e["z_max"], node)
                rounds.seen(node_mm, p - 2)
                v.tensor_tensor(node_z[:, q, HEADS:], score, score, ALU.max)
                rounds.seen(top_read, p, GROUP - 1)
                chain.step(v.tensor_reduce(top, tile_top.rearrange("p k h -> p h k"), AX.X, ALU.max))
                chain.step(v.tensor_tensor(top, top, score, ALU.add))
                chain.step(v.scalar_tensor_tensor(zt, top, SLOPE, top, ALU.mult, ALU.max))
                v.tensor_tensor(node_z[:, q, 0:HEADS], z, zt, ALU.max).then_inc(node_set[s], 1)
                rounds.seen(node_set, p)
                rounds.seen(shrink_set, p - 2)
                v.tensor_tensor(fall[:, q, :], z, node_z[:, q, 0:HEADS], ALU.subtract).then_inc(fall_set[s], 1)
                rounds.seen(fall_set, p)
                chain.step(v.tensor_tensor(z, z, node_z[:, q, 0:HEADS], ALU.max))
                return to_sum

            def exponents(p):
                rounds.seen(node_mm, p)
                chain.step(v.tensor_tensor(ze, whg[:, slot(p), :, C:GROW].rearrange("p k h c -> p k (h c)"),
                                           ps_node[:, :, HEADS:], ALU.add))
                chain.step(v.scalar_tensor_tensor(ze, ze, SLOPE, ze, ALU.mult, ALU.max))
                chain.step(v.tensor_tensor(ze, ze, ps_node[:, :, 0:HEADS], ALU.subtract))
                rounds.seen(p_set, p - 2)
                v.tensor_scalar(zp[:, slot(p, 2), :], ze, 0.0, None, ALU.min).then_inc(zp_set[p % AHEAD], 1)

            def accumulate(p, node):
                rounds.seen(att_mm, p)
                rounds.seen(shrink_set, p)
                rounds.seen(att_out, p - 1)
                to = sum1[:, bass.ds(node, 1), :].rearrange("p a (h c) -> p (a h) c", h=HEADS)
                for h in range(HEADS):
                    ins = v.scalar_tensor_tensor(to[:, h, :], to[:, h, :], shrink[:, p % 2, h:h + 1],
                                                 ps_sum[p % 2][:, h, :], ALU.mult, ALU.add)
                ins.then_inc(att_out[p % AHEAD], 1)

            def part(p):
                if p >= 1:
                    exponents(p - 1)
                node = tops(p)
                misses(p + 2)
                if p >= 2:
                    accumulate(p - 2, node)

            misses(0)
            misses(1)
            part(0)
            part(1)
            chain.enter()
            with dve.Fori(0, rounds.trips):
                rounds.begin()
                chain.begin()
                for u in range(AHEAD):
                    part(u + 2)
                chain.end()
                rounds.end()


def output_norm(nc, env):
    e, phase_sem, take, sum1 = env, env["phase_sem"], env["take"], env["sum1"]
    with ExitStack() as own:
        arena, at = e["phase_arena"](own), [0]
        den, st = take(arena, at, [BATCH * HEADS]), take(arena, at, [BATCH, 6])
        mv = take(arena, at, [2, BATCH, 4])
        wide = [e["SPARE"]]
        x1, res = take(e["sums"], wide, [2, BATCH, D]), take(e["sums"], wide, [2, BATCH, D])
        low, high = take(e["sums"], wide, [BATCH * D]), take(e["sums"], wide, [BATCH * D])
        idle = take(arena, at, [1])
        x1_in = [phase_sem("x1_in0"), phase_sem("x1_in1")]
        stored = [phase_sem("stored0"), phase_sem("stored1")]
        low_set, exp_set, var_set, res_set, normed, steps, pool_steps = [
            phase_sem(f"f_{n}") for n in "low exp var res normed steps pool_steps".split()]
        out, x1_dram = e["out"], e["x1_dram"]
        BATCHES = NODE_TILES // BATCH
        PAIRS = -(-BATCHES // 2)
        block = own.enter_context(nc.Block())

        def batch(dram, i):
            return dram[bass.ds(i * BATCH * P, BATCH * P), :].rearrange("(t p) d -> p t d", p=P)

        @block.sync
        def _(sp):
            def load(i, q):
                sp.dma_start(x1[:, q, :, :], batch(x1_dram, i)).then_inc(x1_in[q], 16)

            def store(i, q):
                sp.wait_ge(normed, i + 1)
                sp.dma_start(batch(out, i), res[:, q, :, :]).then_inc(stored[q], 16)

            load(0, 0)
            load(1, 1)
            with sp.Fori(0, BATCHES // 2 - 1) as j:
                j = sp.snap(j, min_val=0, max_val=BATCHES // 2 - 2)
                for q in range(2):
                    store(2 * j + q, q)
                    load(2 * j + 2 + q, q)
            store(BATCHES - 3, 0)
            load(BATCHES - 1, 0)
            store(BATCHES - 2, 1)
            store(BATCHES - 1, 0)
            sp.wait_ge(stored[0], 16 * PAIRS)
            sp.wait_ge(stored[1], 16 * (BATCHES - PAIRS))

        def halves(eng, body, chain=None):
            for q in range(2):
                body(q, q, 0)
            if chain:
                chain.enter()
            with eng.Fori(1, BATCHES // 2) as j:
                j = eng.snap(j, min_val=1, max_val=BATCHES // 2 - 1)
                if chain:
                    chain.begin()
                for q in range(2):
                    body(2 * j + q, q, j)
                if chain:
                    chain.end()
            if chain:
                chain.leave(BATCHES // 2 - 1)
            body(BATCHES - 1, 0, BATCHES // 2)

        @block.gpsimd
        def _(pool):
            g, chain = nc.gpsimd, Chain(pool, pool_steps)

            def body(i, q, j):
                pool.wait_ge(var_set, i + 1)
                norm_factors(g, chain, mv[:, q, :, :], e["powers"]).then_inc(res_set, 1)

            halves(pool, body, chain)

        @block.scalar
        def _(act):
            def body(i, q, j):
                act.wait_ge(low_set, i + 1)
                nc.scalar.activation(low, low, ACT.Exp).then_inc(exp_set, 1)
                act.wait_ge(res_set, i + 1)
                for n in range(BATCH):
                    ins = nc.scalar.activation(res[:, q, n, :], res[:, q, n, :], ACT.Identity,
                                               bias=mv[:, q, n, 3:4], scale=mv[:, q, n, 2:3])
                ins.then_inc(normed, 1)

            halves(act, body)

        @block.vector
        def _(dve):
            v, chain = nc.vector, Chain(dve, steps)

            def body(i, q, j):
                s = sum1[:, bass.ds(i * BATCH, BATCH), :].rearrange("p a (h c) -> p (a h) c", h=HEADS)
                chain.step(v.tensor_scalar(den, s[:, :, C:GROW].rearrange("p h c -> p (h c)"), DEN_EPS, None,
                                           ALU.add))
                chain.step(v.reciprocal(den, den))
                chain.step(v.tensor_tensor(high.rearrange("p (h c) -> p h c", c=C), s[:, :, 0:C],
                                           den.rearrange("p (h c) -> p h c", c=1).to_broadcast(
                                               [P, BATCH * HEADS, C]), ALU.mult))
                v.tensor_scalar(low, high, 0.0, None, ALU.min).then_inc(low_set, 1)
                dve.wait_ge(x1_in[q], (j + 1) * 16)
                if not isinstance(i, int) or i >= 2:
                    dve.wait_ge(stored[q], j * 16)
                row = res[:, q, :, :].rearrange("p t d -> p (t d)")
                chain.step(v.scalar_tensor_tensor(row, high, 0.0, x1[:, q, :, :].rearrange("p t d -> p (t d)"),
                                                  ALU.max, ALU.add))
                dve.wait_ge(exp_set, i + 1)
                chain.step(v.scalar_tensor_tensor(row, low, -1.0, row, ALU.add, ALU.add))
                for n in range(BATCH):
                    ins = v.bn_stats(st[:, n, :], res[:, q, n, :])
                chain.step(ins)
                v.memset(idle, 0.0)
                for n in range(BATCH):
                    ins = v.bn_aggr(mv[:, q, n, 0:2], st[:, n, :])
                ins.then_inc(var_set, 1)

            halves(dve, body, chain)


def kernel(**inputs):
    import numpy as np
    import concourse.bacc as bacc
    from concourse.bass_utils import run_bass_kernel_spmd

    a = {k: np.asarray(v) for k, v in inputs.items()}
    L0 = {k[len("L0_gnn_"):]: v for k, v in a.items() if k.startswith("L0_gnn_")}

    def padded(v, n, fill):
        out = np.full((n, *v.shape[1:]), fill, v.dtype)
        out[:len(v)] = v
        return out

    dst = padded(a["dst"], ALL_TILES * P, -1)
    arrays = {
        "x": padded(a["x"], NODE_TILES * P, 0),
        "srcT": padded(a["src"], ALL_TILES * P, 0).reshape(ALL_TILES, P).T,
        "dstT": dst.reshape(ALL_TILES, P).T,
        "dst_rows": padded(a["dst"], TILE_ROWS * P * P, -1).reshape(TILE_ROWS, P, P).transpose(1, 0, 2),
        "eaT": padded(a["edge_attr_64"], ALL_TILES * P, 0).T,
        "eps": L0["eps"].reshape(1),
        "ee_w1": L0["ee_w1"], "ee_b1": L0["ee_b1"], "ee_w2": L0["ee_w2"], "ee_b2": L0["ee_b2"],
        "w1": L0["w1"], "b1": L0["b1"],
        "g1T": L0["g1"].reshape(-1, P).T, "be1T": L0["be1"].reshape(-1, P).T,
        "w2": L0["w2"], "b2": L0["b2"],
        "g2T": L0["g2"].reshape(-1, P).T, "be2T": L0["be2"].reshape(-1, P).T,
        "w3": L0["w3"], "b3": L0["b3"], "bn_g": L0["bn_g"], "bn_b": L0["bn_b"],
        "gat_wT": a["L1_gnn_W"].T,
        "att_src": a["L1_gnn_att"][:, :C].reshape(-1), "att_dst": a["L1_gnn_att"][:, C:].reshape(-1),
    }
    nc = bacc.Bacc("TRN2", target_bir_lowering=False, num_devices=1)
    args, fed = [], {}
    for name, v in arrays.items():
        v = np.ascontiguousarray(v)
        fed[f"in_{name}"] = v
        args.append(nc.dram_tensor(f"in_{name}", v.shape, mybir.dt.from_np(v.dtype), kind="ExternalInput").ap())
    out = nc.dram_tensor("out_rows", (NODE_TILES * P, D), F32, kind="ExternalOutput").ap()
    bass_gnn_resnorm(nc, *args, out)
    r = run_bass_kernel_spmd(nc, [fed], core_ids=[0])
    return r.results[0]["out_rows"][:N_NODES]
```
